# Optimizing a Trainium2 kernel written in Bass

```python
import numpy as np
import jax
import jax.numpy as jnp

def _softmax(x, axis=-1):
    return jax.nn.softmax(x, axis=axis)

def _gelu(x):
    return jax.nn.gelu(x, approximate=True)

def _silu(x):
    return jax.nn.silu(x)

def _sigmoid(x):
    return jax.nn.sigmoid(x)

def _layernorm(x, axis=-1, eps=1e-05):
    m = jnp.mean(x, axis=axis, keepdims=True)
    v = jnp.var(x, axis=axis, keepdims=True)
    return (x - m) / jnp.sqrt(v + eps)

def _scatter_add(tgt, idx, src, axis=0):
    return tgt.at[idx].add(src)

def _segment_sum(src, seg, n):
    return jax.ops.segment_sum(src, seg, n)
kernel_name = 'mk_gps_d4_gnn_r16_eb100d'

def setup_inputs(seed: int=0):
    np.random.seed(seed)
    _w = jnp.asarray

    def _rec_inputs():
        import jax
        import jax.numpy as jnp
        _gk = jax.random.key(seed)
        x = -0.0002117 + 1 * jax.random.normal(jax.random.fold_in(_gk, 1), (625, 512), jnp.float32)
        src = jax.random.randint(jax.random.fold_in(_gk, 2), (20000,), 0, 625, jnp.int32)
        dst = jnp.minimum((625 * jax.random.uniform(jax.random.fold_in(_gk, 3), (20000,)) ** 2.0).astype(jnp.int32), 9999)
        _o = jnp.argsort(dst, stable=True)
        src = src[_o]
        dst = dst[_o]
        edge_weight = jax.random.uniform(jax.random.fold_in(_gk, 13), (20000,), jnp.float32, 0.0, 0.0999999)
        node_vec = jax.random.uniform(jax.random.fold_in(_gk, 14), (625,), jnp.float32, 0.0, 0.999988)
        return (x, src, dst, edge_weight, node_vec)
    x, src, dst, edge_weight, node_vec = _rec_inputs()

    def _L0_gnn_setup():
        import jax, jax.numpy as jnp
        import numpy as np
        N_NODES = 3125
        N_EDGES = 25000
        DIM = 512

        def _graph_conv(x, W0, W1, b, diag, edge_vals, edge_src, edge_dst):
            n = x.shape[0]
            self_term = diag[:, None] * (x @ W0)
            msgs = edge_vals[:, None] * (x @ W1)[edge_src]
            neigh = jax.ops.segment_sum(msgs, edge_dst, num_segments=n)
            return jax.nn.relu(self_term + neigh + b)
        key = jax.random.key(seed)
        ks = jax.random.split(key, 10)
        scale = 1.0 / np.sqrt(DIM)
        return {'x': jax.random.normal(ks[0], (N_NODES, DIM), jnp.float32), 'W0_1': jax.random.normal(ks[1], (DIM, DIM), jnp.float32) * scale, 'W1_1': jax.random.normal(ks[2], (DIM, DIM), jnp.float32) * scale, 'b1': jnp.zeros((DIM,), jnp.float32), 'W0_2': jax.random.normal(ks[3], (DIM, DIM), jnp.float32) * scale, 'W1_2': jax.random.normal(ks[4], (DIM, DIM), jnp.float32) * scale, 'b2': jnp.zeros((DIM,), jnp.float32), 'diag': jax.random.uniform(ks[5], (N_NODES,), jnp.float32), 'edge_vals': jax.random.uniform(ks[6], (N_EDGES,), jnp.float32) * 0.1, 'edge_src': jax.random.randint(ks[7], (N_EDGES,), 0, N_NODES, jnp.int32), 'edge_dst': jax.random.randint(ks[8], (N_EDGES,), 0, N_NODES, jnp.int32)}
    _L0_gnn_all = _L0_gnn_setup()
    _L0_gnn_in = {k: v for k, v in _L0_gnn_all.items() if k in ('W0_1', 'W1_1', 'b1', 'W0_2', 'W1_2', 'b2')}
    del _L0_gnn_all

    def _L0_mix_setup():
        import jax, jax.numpy as jnp
        import numpy as np
        N, B, C, H = (256, 8, 512, 8)
        D = C // H
        EPS = 1e-06

        def _dot(a, b):
            return jnp.einsum('bhsd,bhd->bhs', a, b)
        key = jax.random.key(seed)
        ks = jax.random.split(key, 6)
        scale = 0.02
        return {'query': jax.random.normal(ks[0], (N, B, C), dtype=jnp.float32), 'Wq': jax.random.normal(ks[1], (C, C), dtype=jnp.float32) * scale, 'bq': jnp.zeros((C,), dtype=jnp.float32), 'Wk': jax.random.normal(ks[2], (C, C), dtype=jnp.float32) * scale, 'bk': jnp.zeros((C,), dtype=jnp.float32), 'Wv': jax.random.normal(ks[3], (C, C), dtype=jnp.float32) * scale, 'bv': jnp.zeros((C,), dtype=jnp.float32), 'Wo': jax.random.normal(ks[4], (C, C), dtype=jnp.float32) * scale, 'bo': jnp.zeros((C,), dtype=jnp.float32), 'temperature': jnp.ones((1,), dtype=jnp.float32)}
    _L0_mix_all = _L0_mix_setup()
    _L0_mix_in = {k: v for k, v in _L0_mix_all.items() if k in ('Wq', 'bq', 'Wk', 'bk', 'Wv', 'bv', 'Wo', 'bo', 'temperature')}
    del _L0_mix_all

    def _L0_ffn_setup():
        import jax, jax.numpy as jnp
        import numpy as np
        DIM = 512
        FFN_DIM = 1408
        GROUP = 128
        EPS = 1e-05

        def _quantize_weight(w, group_size):
            o, i = w.shape
            wg = w.reshape(o, i // group_size, group_size)
            scale = jnp.mean(jnp.abs(wg), axis=-1, keepdims=True) + EPS
            wq = jnp.clip(jnp.round(wg / scale), -1.0, 1.0) * scale
            return wq.reshape(o, i)

        def _bitlinear(x, w, group_size=GROUP):
            wq = w + jax.lax.stop_gradient(_quantize_weight(w, group_size) - w)
            return jnp.einsum('bsd,fd->bsf', x, wq)
        key = jax.random.key(seed)
        k_x, k_g, k_u, k_d = jax.random.split(key, 4)
        x = jax.random.normal(k_x, (8, 256, DIM), dtype=jnp.float32)
        sd_in = 1.0 / np.sqrt(DIM)
        sd_ffn = 1.0 / np.sqrt(FFN_DIM)
        w_gate = jax.random.normal(k_g, (FFN_DIM, DIM), dtype=jnp.float32) * sd_in
        w_up = jax.random.normal(k_u, (FFN_DIM, DIM), dtype=jnp.float32) * sd_in
        w_down = jax.random.normal(k_d, (DIM, FFN_DIM), dtype=jnp.float32) * sd_ffn
        return {'x': x, 'w_gate': w_gate, 'w_up': w_up, 'w_down': w_down}
    _L0_ffn_all = _L0_ffn_setup()
    _L0_ffn_in = {k: v for k, v in _L0_ffn_all.items() if k in ('w_gate', 'w_up', 'w_down')}
    del _L0_ffn_all

    def _L1_gnn_setup():
        import jax, jax.numpy as jnp
        import numpy as np
        N_NODES = 625
        N_EDGES = 10000
        D_IN = 512
        D_OUT = 512
        key = jax.random.key(seed)
        k1, k2, k3, k4, k5 = jax.random.split(key, 5)
        feature = jax.random.normal(k1, (N_NODES, D_IN), dtype=jnp.float32)
        src = jax.random.randint(k2, (N_EDGES,), 0, N_NODES, dtype=jnp.int64)
        dst = jax.random.randint(k3, (N_EDGES,), 0, N_NODES, dtype=jnp.int64)
        W = jax.random.normal(k4, (2 * D_IN, D_OUT), dtype=jnp.float32) * (1.0 / np.sqrt(2 * D_IN))
        b = jax.random.normal(k5, (D_OUT,), dtype=jnp.float32) * 0.01
        return {'feature': feature, 'src': src, 'dst': dst, 'W': W, 'b': b}
    _L1_gnn_all = _L1_gnn_setup()
    _L1_gnn_in = {k: v for k, v in _L1_gnn_all.items() if k in ('W', 'b')}
    del _L1_gnn_all

    def _L1_mix_setup():
        import jax, jax.numpy as jnp
        import numpy as np
        NUM_HEADS = 8
        EPS = 1e-06
        key = jax.random.key(seed)
        k1, k2, k3 = jax.random.split(key, 3)
        B, N, C = (8, 256, 512)
        x = jax.random.normal(k1, (B, N, C), dtype=jnp.float32)
        Wq = jax.random.normal(k2, (C, C), dtype=jnp.float32) * (1.0 / np.sqrt(C))
        Wkv = jax.random.normal(k3, (2 * C, C), dtype=jnp.float32) * (1.0 / np.sqrt(C))
        return {'x': x, 'Wq': Wq, 'Wkv': Wkv}
    _L1_mix_all = _L1_mix_setup()
    _L1_mix_in = {k: v for k, v in _L1_mix_all.items() if k in ('Wq', 'Wkv')}
    del _L1_mix_all

    def _L1_ffn_setup():
        import jax, jax.numpy as jnp
        import numpy as np
        B, L, H, E, F, C = (8, 512, 512, 8, 1024, 2)
        key = jax.random.key(seed)
        ks = jax.random.split(key, 4)
        x = jax.random.normal(ks[0], (B, L, H), jnp.float32)
        Wg = jax.random.normal(ks[1], (H, E), jnp.float32) * H ** (-0.5)
        W1 = jax.random.normal(ks[2], (E, H, F), jnp.float32) * H ** (-0.5)
        b1 = jnp.zeros((E, F), jnp.float32)
        W2 = jax.random.normal(ks[3], (E, F, H), jnp.float32) * F ** (-0.5)
        b2 = jnp.zeros((E, H), jnp.float32)
        return {'x': x, 'Wg': Wg, 'W1': W1, 'b1': b1, 'W2': W2, 'b2': b2}
    _L1_ffn_all = _L1_ffn_setup()
    _L1_ffn_in = {k: v for k, v in _L1_ffn_all.items() if k in ('Wg', 'W1', 'b1', 'W2', 'b2')}
    del _L1_ffn_all

    def _L2_gnn_setup():
        import jax, jax.numpy as jnp
        import numpy as np
        N_NODES = 625
        N_EDGES = 10000
        IN_DIM = 512
        HID = 256
        HEADS = 4
        OUT_DIM = 512
        NEG_SLOPE = 0.2

        def _glorot(key, shape):
            fan_in, fan_out = (shape[0], shape[-1])
            lim = jnp.sqrt(6.0 / (fan_in + fan_out))
            return jax.random.uniform(key, shape, jnp.float32, -lim, lim)

        def gat_conv(x, src, dst, W, att_src, att_dst, bias):
            N = x.shape[0]
            h = (x @ W).reshape(N, HEADS, HID)
            a_src = jnp.sum(h * att_src, axis=-1)
            a_dst = jnp.sum(h * att_dst, axis=-1)
            e = jax.nn.leaky_relu(a_src[src] + a_dst[dst], NEG_SLOPE)
            m = jax.ops.segment_max(e, dst, num_segments=N)
            e = jnp.exp(e - m[dst])
            s = jax.ops.segment_sum(e, dst, num_segments=N)
            alpha = e / (s[dst] + 1e-16)
            msg = alpha[:, :, None] * h[src]
            out = jax.ops.segment_sum(msg, dst, num_segments=N)
            return out.reshape(N, HEADS * HID) + bias
        key = jax.random.key(seed)
        ks = jax.random.split(key, 16)
        x = jax.random.normal(ks[0], (N_NODES, IN_DIM), jnp.float32)
        edge_index = jax.random.randint(ks[1], (2, N_EDGES), 0, N_NODES, jnp.int64)
        W1 = _glorot(ks[2], (IN_DIM, HEADS * HID))
        att_src1 = _glorot(ks[3], (HEADS, HID))
        att_dst1 = _glorot(ks[4], (HEADS, HID))
        b1 = jnp.zeros((HEADS * HID,), jnp.float32)
        W2 = _glorot(ks[5], (HEADS * HID, HEADS * HID))
        att_src2 = _glorot(ks[6], (HEADS, HID))
        att_dst2 = _glorot(ks[7], (HEADS, HID))
        b2 = jnp.zeros((HEADS * HID,), jnp.float32)
        fcW = _glorot(ks[8], (HEADS * HID, OUT_DIM))
        fcb = jnp.zeros((OUT_DIM,), jnp.float32)
        return dict(x=x, edge_index=edge_index, W1=W1, att_src1=att_src1, att_dst1=att_dst1, b1=b1, W2=W2, att_src2=att_src2, att_dst2=att_dst2, b2=b2, fcW=fcW, fcb=fcb)
    _L2_gnn_all = _L2_gnn_setup()
    _L2_gnn_in = {k: v for k, v in _L2_gnn_all.items() if k in ('W1', 'att_src1', 'att_dst1', 'b1', 'W2', 'att_src2', 'att_dst2', 'b2', 'fcW', 'fcb')}
    del _L2_gnn_all

    def _L2_mix_setup():
        import jax, jax.numpy as jnp
        import numpy as np
        import math
        E = 512
        H = 8
        D = E // H
        M = 64
        EPS = 1e-08
        CLAMP_MAX = 50.0

        def _make_omega(key):
            w = jax.random.normal(key, (D, M), dtype=jnp.float32) / np.sqrt(D)
            q, _ = jnp.linalg.qr(w)
            return q

        def _positive_random_feature_map(v, omega):
            f = jnp.minimum(v @ omega, CLAMP_MAX)
            l2 = jnp.maximum(jnp.linalg.norm(v, axis=-1, keepdims=True), EPS)
            norm_term = jnp.maximum(jnp.exp(-0.5 * l2 * l2), EPS)
            return norm_term * jnp.exp(f)
        key = jax.random.key(seed)
        ks = jax.random.split(key, 8)
        B, S = (2, 1024)
        x = jax.random.normal(ks[0], (B, S, E), dtype=jnp.float32)
        sc = 1.0 / np.sqrt(E)
        Wq = jax.random.normal(ks[1], (E, E), dtype=jnp.float32) * sc
        Wk = jax.random.normal(ks[2], (E, E), dtype=jnp.float32) * sc
        Wv = jax.random.normal(ks[3], (E, E), dtype=jnp.float32) * sc
        Wo = jax.random.normal(ks[4], (E, E), dtype=jnp.float32) * sc
        omega_q = _make_omega(ks[5])
        omega_k = _make_omega(ks[6])
        return {'x': x, 'Wq': Wq, 'Wk': Wk, 'Wv': Wv, 'Wo': Wo, 'omega_q': omega_q, 'omega_k': omega_k}
    _L2_mix_all = _L2_mix_setup()
    _L2_mix_in = {k: v for k, v in _L2_mix_all.items() if k in ('Wq', 'Wk', 'Wv', 'Wo', 'omega_q', 'omega_k')}
    del _L2_mix_all

    def _L2_ffn_setup():
        import jax, jax.numpy as jnp
        import numpy as np
        DIM = 512
        DEPTH = 4
        E = 2 ** DEPTH
        HID = 4 * DIM
        B, S = (8, 256)

        def _fff_forward(x, Wr, br, W1, b1, W2, b2):
            Bb, Ss, D = x.shape
            E_ = W1.shape[0]
            depth = int(np.log2(E_))
            xf = x.reshape(-1, D)
            N = xf.shape[0]
            leaf = jnp.zeros((N,), jnp.int32)
            for d in range(depth):
                off = 2 ** d - 1
                cnt = 2 ** d
                logits = xf @ Wr[off:off + cnt].T + br[off:off + cnt]
                sel = jnp.take_along_axis(logits, leaf[:, None], axis=1)[:, 0]
                leaf = leaf * 2 + (sel > 0).astype(jnp.int32)
            onehot = jax.nn.one_hot(leaf, E_, dtype=xf.dtype)

            def body(acc, params):
                w1, bb1, w2, bb2, m = params
                h = jax.nn.gelu(xf @ w1 + bb1, approximate=False)
                y = h @ w2 + bb2
                return (acc + m[:, None] * y, None)
            out, _ = jax.lax.scan(body, jnp.zeros_like(xf), (W1, b1, W2, b2, onehot.T))
            return out.reshape(Bb, Ss, D)
        key = jax.random.key(seed)
        ks = jax.random.split(key, 7)
        sc_in = 1.0 / np.sqrt(DIM)
        sc_hid = 1.0 / np.sqrt(HID)
        return {'x': jax.random.normal(ks[0], (B, S, DIM), jnp.float32), 'Wr': jax.random.normal(ks[1], (E - 1, DIM), jnp.float32) * sc_in, 'br': jax.random.normal(ks[2], (E - 1,), jnp.float32) * 0.01, 'W1': jax.random.normal(ks[3], (E, DIM, HID), jnp.float32) * sc_in, 'b1': jax.random.normal(ks[4], (E, HID), jnp.float32) * 0.01, 'W2': jax.random.normal(ks[5], (E, HID, DIM), jnp.float32) * sc_hid, 'b2': jax.random.normal(ks[6], (E, DIM), jnp.float32) * 0.01}
    _L2_ffn_all = _L2_ffn_setup()
    _L2_ffn_in = {k: v for k, v in _L2_ffn_all.items() if k in ('Wr', 'br', 'W1', 'b1', 'W2', 'b2')}
    del _L2_ffn_all

    def _L3_gnn_setup():
        import jax, jax.numpy as jnp
        import numpy as np
        N_NODES = 1250
        N_EDGES = 10000
        N_IN = 512
        N_OUT = 512
        key = jax.random.key(seed)
        k1, k2, k3, k4, k5 = jax.random.split(key, 5)
        x = jax.random.normal(k1, (N_NODES, N_IN), dtype=jnp.float32)
        vals = jax.random.uniform(k2, (N_EDGES,), dtype=jnp.float32)
        bound = 1.0 / np.sqrt(N_IN)
        weight = jax.random.uniform(k3, (N_OUT, N_IN), minval=-bound, maxval=bound, dtype=jnp.float32)
        row = jax.random.randint(k4, (N_EDGES,), 0, N_NODES, dtype=jnp.int32)
        col = jax.random.randint(k5, (N_EDGES,), 0, N_NODES, dtype=jnp.int32)
        return {'x': x, 'vals': vals, 'weight': weight, 'row': row, 'col': col}
    _L3_gnn_all = _L3_gnn_setup()
    _L3_gnn_in = {k: v for k, v in _L3_gnn_all.items() if k in ('weight',)}
    del _L3_gnn_all

    def _L3_mix_setup():
        import jax, jax.numpy as jnp
        import numpy as np
        EPS = 1e-06
        H = 8
        DH = 64
        LN_EPS = 1e-05

        def _layernorm(x, g, b):
            m = jnp.mean(x, axis=-1, keepdims=True)
            v = jnp.mean(jnp.square(x - m), axis=-1, keepdims=True)
            return (x - m) / jnp.sqrt(v + LN_EPS) * g + b

        def _flow_attention(x, Wq, bq, Wk, bk, Wv, bv, Wo, bo):
            B, L, D = x.shape
            S = L
            q = jax.nn.sigmoid((x @ Wq + bq).reshape(B, L, H, DH).transpose(0, 2, 1, 3))
            k = jax.nn.sigmoid((x @ Wk + bk).reshape(B, S, H, DH).transpose(0, 2, 1, 3))
            v = (x @ Wv + bv).reshape(B, S, H, DH).transpose(0, 2, 1, 3)
            sink_incoming = 1.0 / jnp.einsum('nhld,nhd->nhl', q + EPS, k.sum(axis=2) + EPS)
            source_outgoing = 1.0 / jnp.einsum('nhld,nhd->nhl', k + EPS, q.sum(axis=2) + EPS)
            conserved_sink = jnp.einsum('nhld,nhd->nhl', q + EPS, (k * source_outgoing[..., None]).sum(axis=2) + EPS)
            conserved_source = jnp.einsum('nhld,nhd->nhl', k + EPS, (q * sink_incoming[..., None]).sum(axis=2) + EPS)
            conserved_source = jnp.clip(conserved_source, -1.0, 1.0)
            sink_allocation = jax.nn.sigmoid(conserved_sink * (float(L) / float(S)))
            source_competition = jax.nn.softmax(conserved_source, axis=-1) * float(S)
            kv = jnp.einsum('nhld,nhlm->nhdm', k, v * source_competition[..., None])
            o = jnp.einsum('nhld,nhdm->nhlm', q * sink_incoming[..., None], kv)
            o = o * sink_allocation[..., None]
            o = o.transpose(0, 2, 1, 3).reshape(B, L, D)
            return o @ Wo + bo
        key = jax.random.key(seed)
        ks = jax.random.split(key, 16)
        B, L, D, F = (2, 1024, 512, 128)
        s = 0.02
        inp = {'x': jax.random.normal(ks[0], (B, L, D), dtype=jnp.float32), 'Wq': jax.random.normal(ks[1], (D, D), dtype=jnp.float32) * s, 'bq': jnp.zeros((D,), jnp.float32), 'Wk': jax.random.normal(ks[2], (D, D), dtype=jnp.float32) * s, 'bk': jnp.zeros((D,), jnp.float32), 'Wv': jax.random.normal(ks[3], (D, D), dtype=jnp.float32) * s, 'bv': jnp.zeros((D,), jnp.float32), 'Wo': jax.random.normal(ks[4], (D, D), dtype=jnp.float32) * s, 'bo': jnp.zeros((D,), jnp.float32), 'W1': jax.random.normal(ks[5], (D, F), dtype=jnp.float32) * s, 'b1': jnp.zeros((F,), jnp.float32), 'W2': jax.random.normal(ks[6], (F, D), dtype=jnp.float32) * s, 'b2': jnp.zeros((D,), jnp.float32), 'g1': jnp.ones((D,), jnp.float32), 'be1': jnp.zeros((D,), jnp.float32), 'g2': jnp.ones((D,), jnp.float32), 'be2': jnp.zeros((D,), jnp.float32)}
        return inp
    _L3_mix_all = _L3_mix_setup()
    _L3_mix_in = {k: v for k, v in _L3_mix_all.items() if k in ('Wq', 'bq', 'Wk', 'bk', 'Wv', 'bv', 'Wo', 'bo', 'W1', 'b1', 'W2', 'b2', 'g1', 'be1', 'g2', 'be2')}
    del _L3_mix_all

    def _L3_ffn_setup():
        import jax, jax.numpy as jnp
        import numpy as np
        EPS = 1e-05

        def _bitlinear(x, w):
            w_scale = jnp.clip(jnp.mean(jnp.abs(w)), EPS, None)
            w_q = jnp.clip(jnp.round(w / w_scale), -1.0, 1.0) * w_scale
            w_eff = w + jax.lax.stop_gradient(w_q - w)
            x_scale = 127.0 / jnp.clip(jnp.max(jnp.abs(x), axis=-1, keepdims=True), EPS, None)
            x_q = jnp.clip(jnp.round(x * x_scale), -128.0, 127.0) / x_scale
            x_eff = x + jax.lax.stop_gradient(x_q - x)
            return jnp.einsum('bsi,oi->bso', x_eff, w_eff)

        def _ste_round_clamp_int8(h):
            h_q = jnp.clip(jnp.round(h), -128.0, 127.0)
            return h + jax.lax.stop_gradient(h_q - h)
        key = jax.random.key(seed)
        k1, k2, k3 = jax.random.split(key, 3)
        B, S, D, F = (8, 512, 512, 128)
        x = jax.random.normal(k1, (B, S, D), dtype=jnp.float32)
        w_up = jax.random.normal(k2, (F, D), dtype=jnp.float32) * (1.0 / np.sqrt(D))
        w_down = jax.random.normal(k3, (D, F), dtype=jnp.float32) * (1.0 / np.sqrt(F))
        return {'x': x, 'w_up': w_up, 'w_down': w_down}
    _L3_ffn_all = _L3_ffn_setup()
    _L3_ffn_in = {k: v for k, v in _L3_ffn_all.items() if k in ('w_up', 'w_down')}
    del _L3_ffn_all
    return {'x': x, 'src': src, 'dst': dst, 'edge_weight': edge_weight, 'node_vec': node_vec, 'L0_gnn_W0_1': _L0_gnn_in['W0_1'], 'L0_gnn_W1_1': _L0_gnn_in['W1_1'], 'L0_gnn_b1': _L0_gnn_in['b1'], 'L0_gnn_W0_2': _L0_gnn_in['W0_2'], 'L0_gnn_W1_2': _L0_gnn_in['W1_2'], 'L0_gnn_b2': _L0_gnn_in['b2'], 'L0_mix_Wq': _L0_mix_in['Wq'], 'L0_mix_bq': _L0_mix_in['bq'], 'L0_mix_Wk': _L0_mix_in['Wk'], 'L0_mix_bk': _L0_mix_in['bk'], 'L0_mix_Wv': _L0_mix_in['Wv'], 'L0_mix_bv': _L0_mix_in['bv'], 'L0_mix_Wo': _L0_mix_in['Wo'], 'L0_mix_bo': _L0_mix_in['bo'], 'L0_mix_temperature': _L0_mix_in['temperature'], 'L0_ffn_w_gate': _L0_ffn_in['w_gate'], 'L0_ffn_w_up': _L0_ffn_in['w_up'], 'L0_ffn_w_down': _L0_ffn_in['w_down'], 'L1_gnn_W': _L1_gnn_in['W'], 'L1_gnn_b': _L1_gnn_in['b'], 'L1_mix_Wq': _L1_mix_in['Wq'], 'L1_mix_Wkv': _L1_mix_in['Wkv'], 'L1_ffn_Wg': _L1_ffn_in['Wg'], 'L1_ffn_W1': _L1_ffn_in['W1'], 'L1_ffn_b1': _L1_ffn_in['b1'], 'L1_ffn_W2': _L1_ffn_in['W2'], 'L1_ffn_b2': _L1_ffn_in['b2'], 'L2_gnn_W1': _L2_gnn_in['W1'], 'L2_gnn_att_src1': _L2_gnn_in['att_src1'], 'L2_gnn_att_dst1': _L2_gnn_in['att_dst1'], 'L2_gnn_b1': _L2_gnn_in['b1'], 'L2_gnn_W2': _L2_gnn_in['W2'], 'L2_gnn_att_src2': _L2_gnn_in['att_src2'], 'L2_gnn_att_dst2': _L2_gnn_in['att_dst2'], 'L2_gnn_b2': _L2_gnn_in['b2'], 'L2_gnn_fcW': _L2_gnn_in['fcW'], 'L2_gnn_fcb': _L2_gnn_in['fcb'], 'L2_mix_Wq': _L2_mix_in['Wq'], 'L2_mix_Wk': _L2_mix_in['Wk'], 'L2_mix_Wv': _L2_mix_in['Wv'], 'L2_mix_Wo': _L2_mix_in['Wo'], 'L2_mix_omega_q': _L2_mix_in['omega_q'], 'L2_mix_omega_k': _L2_mix_in['omega_k'], 'L2_ffn_Wr': _L2_ffn_in['Wr'], 'L2_ffn_br': _L2_ffn_in['br'], 'L2_ffn_W1': _L2_ffn_in['W1'], 'L2_ffn_b1': _L2_ffn_in['b1'], 'L2_ffn_W2': _L2_ffn_in['W2'], 'L2_ffn_b2': _L2_ffn_in['b2'], 'L3_gnn_weight': _L3_gnn_in['weight'], 'L3_mix_Wq': _L3_mix_in['Wq'], 'L3_mix_bq': _L3_mix_in['bq'], 'L3_mix_Wk': _L3_mix_in['Wk'], 'L3_mix_bk': _L3_mix_in['bk'], 'L3_mix_Wv': _L3_mix_in['Wv'], 'L3_mix_bv': _L3_mix_in['bv'], 'L3_mix_Wo': _L3_mix_in['Wo'], 'L3_mix_bo': _L3_mix_in['bo'], 'L3_mix_W1': _L3_mix_in['W1'], 'L3_mix_b1': _L3_mix_in['b1'], 'L3_mix_W2': _L3_mix_in['W2'], 'L3_mix_b2': _L3_mix_in['b2'], 'L3_mix_g1': _L3_mix_in['g1'], 'L3_mix_be1': _L3_mix_in['be1'], 'L3_mix_g2': _L3_mix_in['g2'], 'L3_mix_be2': _L3_mix_in['be2'], 'L3_ffn_w_up': _L3_ffn_in['w_up'], 'L3_ffn_w_down': _L3_ffn_in['w_down']}

def reference(x, src, dst, edge_weight, node_vec, L0_gnn_W0_1, L0_gnn_W1_1, L0_gnn_b1, L0_gnn_W0_2, L0_gnn_W1_2, L0_gnn_b2, L0_mix_Wq, L0_mix_bq, L0_mix_Wk, L0_mix_bk, L0_mix_Wv, L0_mix_bv, L0_mix_Wo, L0_mix_bo, L0_mix_temperature, L0_ffn_w_gate, L0_ffn_w_up, L0_ffn_w_down, L1_gnn_W, L1_gnn_b, L1_mix_Wq, L1_mix_Wkv, L1_ffn_Wg, L1_ffn_W1, L1_ffn_b1, L1_ffn_W2, L1_ffn_b2, L2_gnn_W1, L2_gnn_att_src1, L2_gnn_att_dst1, L2_gnn_b1, L2_gnn_W2, L2_gnn_att_src2, L2_gnn_att_dst2, L2_gnn_b2, L2_gnn_fcW, L2_gnn_fcb, L2_mix_Wq, L2_mix_Wk, L2_mix_Wv, L2_mix_Wo, L2_mix_omega_q, L2_mix_omega_k, L2_ffn_Wr, L2_ffn_br, L2_ffn_W1, L2_ffn_b1, L2_ffn_W2, L2_ffn_b2, L3_gnn_weight, L3_mix_Wq, L3_mix_bq, L3_mix_Wk, L3_mix_bk, L3_mix_Wv, L3_mix_bv, L3_mix_Wo, L3_mix_bo, L3_mix_W1, L3_mix_b1, L3_mix_W2, L3_mix_b2, L3_mix_g1, L3_mix_be1, L3_mix_g2, L3_mix_be2, L3_ffn_w_up, L3_ffn_w_down):
    import jax
    import jax.numpy as jnp

    def _L0_gnn_ref(x, W0_1, W1_1, b1, W0_2, W1_2, b2, diag, edge_vals, edge_src, edge_dst):
        import jax, jax.numpy as jnp
        import numpy as np
        N_NODES = 3125
        N_EDGES = 25000
        DIM = 512

        def _graph_conv(x, W0, W1, b, diag, edge_vals, edge_src, edge_dst):
            n = x.shape[0]
            self_term = diag[:, None] * (x @ W0)
            msgs = edge_vals[:, None] * (x @ W1)[edge_src]
            neigh = jax.ops.segment_sum(msgs, edge_dst, num_segments=n)
            return jax.nn.relu(self_term + neigh + b)
        h = _graph_conv(x, W0_1, W1_1, b1, diag, edge_vals, edge_src, edge_dst)
        h = _graph_conv(h, W0_2, W1_2, b2, diag, edge_vals, edge_src, edge_dst)
        return (h + x) * 0.5

    def _L0_mix_ref(query, Wq, bq, Wk, bk, Wv, bv, Wo, bo, temperature):
        import jax, jax.numpy as jnp
        import numpy as np
        N, B, C, H = (256, 8, 512, 8)
        D = C // H
        EPS = 1e-06

        def _dot(a, b):
            return jnp.einsum('bhsd,bhd->bhs', a, b)
        n, b, c = query.shape
        q = (query @ Wq + bq).reshape(n, b, H, D).transpose(1, 2, 0, 3)
        k = (query @ Wk + bk).reshape(n, b, H, D).transpose(1, 2, 0, 3)
        v = (query @ Wv + bv).reshape(n, b, H, D).transpose(1, 2, 0, 3)
        q = jax.nn.sigmoid(q)
        k = jax.nn.sigmoid(k)
        hw = k.shape[2]
        sink_incoming = 1.0 / (_dot(q + EPS, k.sum(axis=2) + EPS) + EPS)
        source_outgoing = 1.0 / (_dot(k + EPS, q.sum(axis=2) + EPS) + EPS)
        conserved_sink = _dot(q + EPS, (k * source_outgoing[..., None]).sum(axis=2) + EPS) + EPS
        conserved_source = _dot(k + EPS, (q * sink_incoming[..., None]).sum(axis=2) + EPS) + EPS
        conserved_source = jnp.clip(conserved_source, -1.0, 1.0)
        sink_allocation = jax.nn.sigmoid(conserved_sink * (float(n) / float(hw)))
        source_competition = jax.nn.softmax(conserved_source / temperature, axis=-1) * float(c)
        kv = jnp.einsum('bhsd,bhse->bhde', k, v * source_competition[..., None])
        out_update = jnp.einsum('bhnd,bhde->bhne', q, kv)
        out_update = out_update * sink_incoming[..., None] * sink_allocation[..., None]
        out = out_update.reshape(b, n, c)
        out = out @ Wo + bo
        out = out.transpose(1, 0, 2)
        return query + out

    def _L0_ffn_ref(x, w_gate, w_up, w_down):
        import jax, jax.numpy as jnp
        import numpy as np
        DIM = 512
        FFN_DIM = 1408
        GROUP = 128
        EPS = 1e-05

        def _quantize_weight(w, group_size):
            o, i = w.shape
            wg = w.reshape(o, i // group_size, group_size)
            scale = jnp.mean(jnp.abs(wg), axis=-1, keepdims=True) + EPS
            wq = jnp.clip(jnp.round(wg / scale), -1.0, 1.0) * scale
            return wq.reshape(o, i)

        def _bitlinear(x, w, group_size=GROUP):
            wq = w + jax.lax.stop_gradient(_quantize_weight(w, group_size) - w)
            return jnp.einsum('bsd,fd->bsf', x, wq)
        gate = _bitlinear(x, w_gate)
        up = _bitlinear(x, w_up)
        h = jax.nn.silu(gate) * up
        return _bitlinear(h, w_down)

    def _L1_gnn_ref(feature, src, dst, W, b):
        import jax, jax.numpy as jnp
        import numpy as np
        N_NODES = 625
        N_EDGES = 10000
        D_IN = 512
        D_OUT = 512
        n = feature.shape[0]
        neigh = jax.ops.segment_sum(feature[src], dst, num_segments=n)
        degs = jax.ops.segment_sum(jnp.ones_like(dst, dtype=feature.dtype), dst, num_segments=n)
        hk_neigh = neigh / jnp.maximum(degs, 1.0)[:, None]
        hk = jnp.concatenate([feature, hk_neigh], axis=-1) @ W + b
        return jax.nn.relu(hk)

    def _L1_mix_ref(x, Wq, Wkv):
        import jax, jax.numpy as jnp
        import numpy as np
        NUM_HEADS = 8
        EPS = 1e-06
        B, N, C = x.shape
        h = NUM_HEADS
        d = C // h
        q = (x @ Wq.T).reshape(B, N, h, d)
        kv = (x @ Wkv.T).reshape(B, N, 2, h, d)
        k = kv[:, :, 0]
        v = kv[:, :, 1]
        Q = jax.nn.elu(q) + 1.0
        K = jax.nn.elu(k) + 1.0
        v_length = v.shape[1]
        v = v / v_length
        KV = jnp.einsum('nshd,nshv->nhdv', K, v)
        Z = 1.0 / (jnp.einsum('nlhd,nhd->nlh', Q, K.sum(axis=1)) + EPS)
        out = jnp.einsum('nlhd,nhdv,nlh->nlhv', Q, KV, Z) * v_length
        return out.reshape(B, N, C)

    def _L1_ffn_ref(x, Wg, W1, b1, W2, b2):
        import jax, jax.numpy as jnp
        import numpy as np
        B, L, H, E, F, C = (8, 512, 512, 8, 1024, 2)
        b, l, h = x.shape
        e = Wg.shape[1]
        k = min(max(int(l * C / e), 1), l)
        S = jax.nn.softmax(x @ Wg, axis=-1)
        St = jnp.swapaxes(S, 1, 2)
        G, I = jax.lax.top_k(St, k)
        ex = jnp.take_along_axis(x[:, None], I[..., None], axis=2)
        hmid = jax.nn.gelu(jnp.einsum('bekh,ehf->bekf', ex, W1) + b1[None, :, None, :], approximate=False)
        out = jnp.einsum('bekf,efh->bekh', hmid, W2) + b2[None, :, None, :]
        vals = G[..., None] * out
        new_x = jnp.zeros_like(x).at[jnp.arange(b)[:, None, None], I].add(vals)
        return new_x

    def _L2_gnn_ref(x, edge_index, W1, att_src1, att_dst1, b1, W2, att_src2, att_dst2, b2, fcW, fcb):
        import jax, jax.numpy as jnp
        import numpy as np
        N_NODES = 625
        N_EDGES = 10000
        IN_DIM = 512
        HID = 256
        HEADS = 4
        OUT_DIM = 512
        NEG_SLOPE = 0.2

        def _glorot(key, shape):
            fan_in, fan_out = (shape[0], shape[-1])
            lim = jnp.sqrt(6.0 / (fan_in + fan_out))
            return jax.random.uniform(key, shape, jnp.float32, -lim, lim)

        def gat_conv(x, src, dst, W, att_src, att_dst, bias):
            N = x.shape[0]
            h = (x @ W).reshape(N, HEADS, HID)
            a_src = jnp.sum(h * att_src, axis=-1)
            a_dst = jnp.sum(h * att_dst, axis=-1)
            e = jax.nn.leaky_relu(a_src[src] + a_dst[dst], NEG_SLOPE)
            m = jax.ops.segment_max(e, dst, num_segments=N)
            e = jnp.exp(e - m[dst])
            s = jax.ops.segment_sum(e, dst, num_segments=N)
            alpha = e / (s[dst] + 1e-16)
            msg = alpha[:, :, None] * h[src]
            out = jax.ops.segment_sum(msg, dst, num_segments=N)
            return out.reshape(N, HEADS * HID) + bias
        N = x.shape[0]
        loops = jnp.arange(N, dtype=edge_index.dtype)
        src = jnp.concatenate([edge_index[0], loops])
        dst = jnp.concatenate([edge_index[1], loops])
        h = gat_conv(x, src, dst, W1, att_src1, att_dst1, b1)
        h = jax.nn.relu(h)
        h = gat_conv(h, src, dst, W2, att_src2, att_dst2, b2)
        h = jax.nn.relu(h)
        return h @ fcW + fcb

    def _L2_mix_ref(x, Wq, Wk, Wv, Wo, omega_q, omega_k):
        import jax, jax.numpy as jnp
        import numpy as np
        import math
        E = 512
        H = 8
        D = E // H
        M = 64
        EPS = 1e-08
        CLAMP_MAX = 50.0

        def _make_omega(key):
            w = jax.random.normal(key, (D, M), dtype=jnp.float32) / np.sqrt(D)
            q, _ = jnp.linalg.qr(w)
            return q

        def _positive_random_feature_map(v, omega):
            f = jnp.minimum(v @ omega, CLAMP_MAX)
            l2 = jnp.maximum(jnp.linalg.norm(v, axis=-1, keepdims=True), EPS)
            norm_term = jnp.maximum(jnp.exp(-0.5 * l2 * l2), EPS)
            return norm_term * jnp.exp(f)
        B, S, _ = x.shape
        scale = 1.0 / np.sqrt(D)

        def heads(y):
            return y.reshape(B, S, H, D).transpose(0, 2, 1, 3)
        Q = heads(x @ Wq) * scale
        K = heads(x @ Wk) * scale
        V = heads(x @ Wv)
        Q_phi = _positive_random_feature_map(Q, omega_q)
        K_phi = _positive_random_feature_map(K, omega_k)
        KV = jnp.einsum('bhsm,bhsd->bhmd', K_phi, V)
        QKV = jnp.einsum('bhsm,bhmd->bhsd', Q_phi, KV)
        K_ones = K_phi.sum(axis=2)
        QK_ones = jnp.einsum('bhsm,bhm->bhs', Q_phi, K_ones)
        attn = QKV / QK_ones[..., None]
        out = attn.transpose(0, 2, 1, 3).reshape(B, S, E)
        return out @ Wo

    def _L2_ffn_ref(x, Wr, br, W1, b1, W2, b2):
        import jax, jax.numpy as jnp
        import numpy as np
        DIM = 512
        DEPTH = 4
        E = 2 ** DEPTH
        HID = 4 * DIM
        B, S = (8, 256)

        def _fff_forward(x, Wr, br, W1, b1, W2, b2):
            Bb, Ss, D = x.shape
            E_ = W1.shape[0]
            depth = int(np.log2(E_))
            xf = x.reshape(-1, D)
            N = xf.shape[0]
            leaf = jnp.zeros((N,), jnp.int32)
            for d in range(depth):
                off = 2 ** d - 1
                cnt = 2 ** d
                logits = xf @ Wr[off:off + cnt].T + br[off:off + cnt]
                sel = jnp.take_along_axis(logits, leaf[:, None], axis=1)[:, 0]
                leaf = leaf * 2 + (sel > 0).astype(jnp.int32)
            onehot = jax.nn.one_hot(leaf, E_, dtype=xf.dtype)

            def body(acc, params):
                w1, bb1, w2, bb2, m = params
                h = jax.nn.gelu(xf @ w1 + bb1, approximate=False)
                y = h @ w2 + bb2
                return (acc + m[:, None] * y, None)
            out, _ = jax.lax.scan(body, jnp.zeros_like(xf), (W1, b1, W2, b2, onehot.T))
            return out.reshape(Bb, Ss, D)
        return _fff_forward(x, Wr, br, W1, b1, W2, b2)

    def _L3_gnn_ref(x, vals, weight, row, col):
        import jax, jax.numpy as jnp
        import numpy as np
        N_NODES = 1250
        N_EDGES = 10000
        N_IN = 512
        N_OUT = 512
        n = x.shape[0]
        msgs = x[col] * vals[:, None]
        agg = jax.ops.segment_sum(msgs, row, num_segments=n)
        return jnp.einsum('nd,od->no', agg, weight)

    def _L3_mix_ref(x, Wq, bq, Wk, bk, Wv, bv, Wo, bo, W1, b1, W2, b2, g1, be1, g2, be2):
        import jax, jax.numpy as jnp
        import numpy as np
        EPS = 1e-06
        H = 8
        DH = 64
        LN_EPS = 1e-05

        def _layernorm(x, g, b):
            m = jnp.mean(x, axis=-1, keepdims=True)
            v = jnp.mean(jnp.square(x - m), axis=-1, keepdims=True)
            return (x - m) / jnp.sqrt(v + LN_EPS) * g + b

        def _flow_attention(x, Wq, bq, Wk, bk, Wv, bv, Wo, bo):
            B, L, D = x.shape
            S = L
            q = jax.nn.sigmoid((x @ Wq + bq).reshape(B, L, H, DH).transpose(0, 2, 1, 3))
            k = jax.nn.sigmoid((x @ Wk + bk).reshape(B, S, H, DH).transpose(0, 2, 1, 3))
            v = (x @ Wv + bv).reshape(B, S, H, DH).transpose(0, 2, 1, 3)
            sink_incoming = 1.0 / jnp.einsum('nhld,nhd->nhl', q + EPS, k.sum(axis=2) + EPS)
            source_outgoing = 1.0 / jnp.einsum('nhld,nhd->nhl', k + EPS, q.sum(axis=2) + EPS)
            conserved_sink = jnp.einsum('nhld,nhd->nhl', q + EPS, (k * source_outgoing[..., None]).sum(axis=2) + EPS)
            conserved_source = jnp.einsum('nhld,nhd->nhl', k + EPS, (q * sink_incoming[..., None]).sum(axis=2) + EPS)
            conserved_source = jnp.clip(conserved_source, -1.0, 1.0)
            sink_allocation = jax.nn.sigmoid(conserved_sink * (float(L) / float(S)))
            source_competition = jax.nn.softmax(conserved_source, axis=-1) * float(S)
            kv = jnp.einsum('nhld,nhlm->nhdm', k, v * source_competition[..., None])
            o = jnp.einsum('nhld,nhdm->nhlm', q * sink_incoming[..., None], kv)
            o = o * sink_allocation[..., None]
            o = o.transpose(0, 2, 1, 3).reshape(B, L, D)
            return o @ Wo + bo
        sa = _flow_attention(_layernorm(x, g1, be1), Wq, bq, Wk, bk, Wv, bv, Wo, bo)[0]
        x = x + sa
        h = _layernorm(x, g2, be2)
        h = jax.nn.gelu(h @ W1 + b1, approximate=False) @ W2 + b2
        return x + h

    def _L3_ffn_ref(x, w_up, w_down):
        import jax, jax.numpy as jnp
        import numpy as np
        EPS = 1e-05

        def _bitlinear(x, w):
            w_scale = jnp.clip(jnp.mean(jnp.abs(w)), EPS, None)
            w_q = jnp.clip(jnp.round(w / w_scale), -1.0, 1.0) * w_scale
            w_eff = w + jax.lax.stop_gradient(w_q - w)
            x_scale = 127.0 / jnp.clip(jnp.max(jnp.abs(x), axis=-1, keepdims=True), EPS, None)
            x_q = jnp.clip(jnp.round(x * x_scale), -128.0, 127.0) / x_scale
            x_eff = x + jax.lax.stop_gradient(x_q - x)
            return jnp.einsum('bsi,oi->bso', x_eff, w_eff)

        def _ste_round_clamp_int8(h):
            h_q = jnp.clip(jnp.round(h), -128.0, 127.0)
            return h + jax.lax.stop_gradient(h_q - h)
        h = _bitlinear(x, w_up)
        h = jax.nn.relu(h)
        h = _ste_round_clamp_int8(h)
        return _bitlinear(h, w_down)
    edge_index = jnp.stack([src, dst])
    xn = _layernorm(x, axis=-1)
    x = x + _L0_gnn_ref(xn, L0_gnn_W0_1, L0_gnn_W1_1, L0_gnn_b1, L0_gnn_W0_2, L0_gnn_W1_2, L0_gnn_b2, node_vec, edge_weight, src, dst) + _L0_mix_ref(xn[None], L0_mix_Wq, L0_mix_bq, L0_mix_Wk, L0_mix_bk, L0_mix_Wv, L0_mix_bv, L0_mix_Wo, L0_mix_bo, L0_mix_temperature)[0]
    x = x + _L0_ffn_ref(_layernorm(x, axis=-1)[None], L0_ffn_w_gate, L0_ffn_w_up, L0_ffn_w_down)[0]
    xn = _layernorm(x, axis=-1)
    x = x + _L1_gnn_ref(xn, src, dst, L1_gnn_W, L1_gnn_b) + _L1_mix_ref(xn[None], L1_mix_Wq, L1_mix_Wkv)[0]
    x = x + _L1_ffn_ref(_layernorm(x, axis=-1)[None], L1_ffn_Wg, L1_ffn_W1, L1_ffn_b1, L1_ffn_W2, L1_ffn_b2)[0]
    xn = _layernorm(x, axis=-1)
    x = x + _L2_gnn_ref(xn, edge_index, L2_gnn_W1, L2_gnn_att_src1, L2_gnn_att_dst1, L2_gnn_b1, L2_gnn_W2, L2_gnn_att_src2, L2_gnn_att_dst2, L2_gnn_b2, L2_gnn_fcW, L2_gnn_fcb) + _L2_mix_ref(xn[None], L2_mix_Wq, L2_mix_Wk, L2_mix_Wv, L2_mix_Wo, L2_mix_omega_q, L2_mix_omega_k)[0]
    x = x + _L2_ffn_ref(_layernorm(x, axis=-1)[None], L2_ffn_Wr, L2_ffn_br, L2_ffn_W1, L2_ffn_b1, L2_ffn_W2, L2_ffn_b2)[0]
    xn = _layernorm(x, axis=-1)
    x = x + _L3_gnn_ref(xn, edge_weight, L3_gnn_weight, src, dst) + _L3_mix_ref(xn[None], L3_mix_Wq, L3_mix_bq, L3_mix_Wk, L3_mix_bk, L3_mix_Wv, L3_mix_bv, L3_mix_Wo, L3_mix_bo, L3_mix_W1, L3_mix_b1, L3_mix_W2, L3_mix_b2, L3_mix_g1, L3_mix_be1, L3_mix_g2, L3_mix_be2)[0]
    x = x + _L3_ffn_ref(_layernorm(x, axis=-1)[None], L3_ffn_w_up, L3_ffn_w_down)[0]
    return x

_drawn_inputs = setup_inputs


def setup_inputs(seed=0):
    import zlib

    import numpy as np

    out = dict(_drawn_inputs(seed))
    spreads = {'L0_gnn_b1': (0.0, 0.8),
     'L0_gnn_b2': (0.0, 2.0),
     'L0_mix_bq': (0.0, 2.0),
     'L0_mix_bk': (0.0, 2.0),
     'L0_mix_bv': (0.0, 0.1),
     'L0_mix_bo': (0.0, 2.0),
     'L1_ffn_b1': (0.0, 2.0),
     'L1_ffn_b2': (0.0, 2.0),
     'L2_gnn_b1': (0.0, 0.8),
     'L2_gnn_b2': (0.0, 2.0),
     'L2_gnn_fcb': (0.0, 2.0),
     'L3_mix_bq': (0.0, 2.0),
     'L3_mix_bk': (0.0, 2.0),
     'L3_mix_bv': (0.0, 2.0),
     'L3_mix_bo': (0.0, 2.0),
     'L3_mix_b1': (0.0, 2.0),
     'L3_mix_b2': (0.0, 2.0),
     'L3_mix_g1': (1.0, 0.6),
     'L3_mix_be1': (0.0, 2.0),
     'L3_mix_g2': (1.0, 0.6),
     'L3_mix_be2': (0.0, 2.0)}
    factors = {'edge_weight': 8.0,
     'node_vec': 8.0,
     'L0_gnn_W0_1': 8.0,
     'L0_gnn_W1_1': 8.0,
     'L0_gnn_W0_2': 8.0,
     'L0_gnn_W1_2': 8.0,
     'L0_mix_Wq': 200.0,
     'L0_mix_Wk': 200.0,
     'L0_ffn_w_gate': 8.0,
     'L0_ffn_w_up': 8.0,
     'L0_ffn_w_down': 8.0,
     'L1_gnn_W': 8.0,
     'L1_gnn_b': 200.0,
     'L1_mix_Wq': 200.0,
     'L1_mix_Wkv': 21.919,
     'L1_ffn_Wg': 8.0,
     'L1_ffn_W1': 8.0,
     'L1_ffn_W2': 8.0,
     'L2_gnn_W1': 8.0,
     'L2_gnn_att_src1': 8.0,
     'L2_gnn_att_dst1': 8.0,
     'L2_gnn_W2': 8.0,
     'L2_gnn_att_src2': 8.0,
     'L2_gnn_att_dst2': 200.0,
     'L2_gnn_fcW': 8.0,
     'L2_mix_Wq': 8.0,
     'L2_mix_Wk': 8.0,
     'L2_mix_Wv': 8.0,
     'L2_mix_Wo': 8.0,
     'L2_mix_omega_q': 8.0,
     'L2_mix_omega_k': 8.0,
     'L2_ffn_Wr': 7.036,
     'L2_ffn_br': 200.0,
     'L2_ffn_W1': 7.533,
     'L2_ffn_b1': 200.0,
     'L2_ffn_W2': 6.802,
     'L2_ffn_b2': 200.0,
     'L3_gnn_weight': 8.0,
     'L3_mix_Wq': 200.0,
     'L3_mix_Wk': 200.0,
     'L3_mix_Wv': 40.103,
     'L3_mix_Wo': 41.265,
     'L3_mix_W1': 64.0,
     'L3_mix_W2': 64.0,
     'L3_ffn_w_up': 33.247,
     'L3_ffn_w_down': 26.324}
    for name, (base, spread) in spreads.items():
        noise = np.random.default_rng([zlib.crc32(name.encode()), seed]).standard_normal(out[name].shape)
        drawn = base * np.exp(spread * noise) if base else spread * noise
        out[name] = jnp.asarray(drawn.astype(out[name].dtype))
    for name, factor in factors.items():
        out[name] = (out[name] * factor).astype(out[name].dtype)
    return out
```

```python
from contextlib import ExitStack

import numpy as np
import concourse.bass as bass
from concourse import mybir

ALU = mybir.AluOpType
ACT = mybir.ActivationFunctionType
AX = mybir.AxisListType
F32 = mybir.dt.float32
F16 = mybir.dt.float16
BF16 = mybir.dt.bfloat16
I32 = mybir.dt.int32
U32 = mybir.dt.uint32

NODES = 625
ROWS = 125
TILES = NODES // ROWS
DIM = 512
CH = DIM // 128
HALVES = [(0, 313), (313, NODES)]
EDGES = 20000
EDGE_TILES = EDGES // ROWS
BANKS = 8
BANK = 512
HEADS, HDIM = 8, 64
PAIRS = HEADS // 2

FFN0 = 1408
EXP1, FF1 = 8, 1024
TOP1 = max(NODES * 2 // EXP1, 1)
TOPC = TOP1 // 2
GAT_HEADS, GAT_HID = 4, 256
GAT_DIM = GAT_HEADS * GAT_HID
EXP2, FF2 = 16, 2048
SLOT = 128
SLOTS = EXP2 + NODES // SLOT
FF3 = 128
ROUND = 1.5 * 2 ** 23


class Signal:

    def __init__(self, sem):
        self.sem, self.count = sem, 0

    def up(self, by=1):
        self.count += by
        return self.count

    def span(self, raises):
        self.count += raises
        return self.count - raises


class Core:

    def __init__(self, nc, ctx):
        def signal(name):
            return Signal(ctx.enter_context(nc.semaphore(name)))

        self.nc = nc
        self.psum = ctx.enter_context(nc.psum_tensor("psum", [128, BANKS, BANK], F32))
        self.bank_filled = signal("bank_filled")
        self.vector_freed = signal("vector_freed_bank")
        self.scalar_freed = signal("scalar_freed_bank")
        self.vector_done = signal("vector_done")
        self.scalar_done = signal("scalar_done")
        self.pool_done = signal("pool_done")
        self.landed = signal("loads_landed")
        self.made = signal("one_hots_made")
        self.used = signal("one_hots_used")
        self.summed = signal("all_edges_summed")
        self.spread = signal("probabilities_spread")
        self.ranked = signal("expert_ranked")

    def bank(self, j):
        return self.psum[:, j % BANKS, :]


def product(rows, terms, cols=None, at=0):
    return ("sum", rows, at, cols, terms)


def turned(rows, cols, source, ident, at=0):
    return ("turn", rows, at, cols, (source, ident))


def fill(nc, bank, products):
    for kind, rows, at, cols, terms in products:
        if kind == "turn":
            last = nc.tensor.transpose(bank[0:rows, at:at + cols], terms[0], terms[1])
            continue
        for n, (lhs, rhs) in enumerate(terms):
            last = nc.tensor.matmul(bank[0:rows, at:at + cols], lhs, rhs,
                                    start=(n == 0), stop=(n == len(terms) - 1))
    return last


def halves(m_rows, terms_of):
    return [[product(m_rows, terms_of(a, b), b - a)] for a, b in HALVES]


def rows_of(t):
    return slice(t * ROWS, (t + 1) * ROWS)


def chunk(c):
    return slice(c * 128, (c + 1) * 128)


class Scope:

    made = 0

    def __init__(self, nc, ctx, tag):
        Scope.made += 1
        self.nc, self.ctx, self.tag = nc, ctx, f"{tag}{Scope.made}_"

    def __call__(self, name, shape, dt=F32):
        return self.ctx.enter_context(self.nc.sbuf_tensor(self.tag + name, shape, dt))


def norm_phases(core, c, src, xn, xnT, loads=(), eps=1e-5, gain=None, shift=None):
    nc = core.nc
    with ExitStack() as ctx:
        sb = Scope(nc, ctx, "norm_")
        stats = sb("stats", [ROWS, TILES, 6])
        mv = sb("mv", [ROWS, TILES, 2])
        ve = sb("ve", [ROWS, TILES])
        root = sb("root", [ROWS, TILES])
        y = sb("y", [ROWS, TILES])
        q = sb("q", [ROWS, TILES])

        def moments(dve):
            for t in range(TILES):
                last = nc.vector.bn_stats(stats[:, t, :], src[:, t, :])
            last.then_inc(core.vector_done.sem, 1)
            dve.wait_ge(core.vector_done.sem, core.vector_done.up())
            for t in range(TILES):
                last = nc.vector.bn_aggr(mv[:, t, :], stats[:, t, :])
            last.then_inc(core.vector_done.sem, 1)
            dve.wait_ge(core.vector_done.sem, core.vector_done.up())
            nc.vector.tensor_scalar(ve[:, :], mv[:, :, 1], eps, None, ALU.add).then_inc(core.vector_done.sem, 1)
            dve.wait_ge(core.vector_done.sem, core.vector_done.up())

        with nc.Block() as block:

            @block.vector
            def _(dve):
                moments(dve)

            @block.sync
            def _(sync):
                for dst, src in loads:
                    sync.dma_start(dst, src).then_inc(core.landed.sem, 16)
                sync.wait_ge(core.landed.sem, core.landed.up(16 * len(loads)))

        with nc.Block() as block:

            @block.scalar
            def _(act):
                nc.scalar.activation(root[:, :], ve[:, :], ACT.Sqrt).then_inc(core.scalar_done.sem, 1)
                act.wait_ge(core.scalar_done.sem, core.scalar_done.up())


        def apply(dve):
            nc.vector.reciprocal(y[:, :], root[:, :]).then_inc(core.vector_done.sem, 1)
            dve.wait_ge(core.vector_done.sem, core.vector_done.up())
            nc.vector.tensor_tensor(q[:, :], y[:, :], y[:, :], ALU.mult).then_inc(core.vector_done.sem, 1)
            dve.wait_ge(core.vector_done.sem, core.vector_done.up())
            nc.vector.tensor_tensor(q[:, :], q[:, :], ve[:, :], ALU.mult).then_inc(core.vector_done.sem, 1)
            dve.wait_ge(core.vector_done.sem, core.vector_done.up())
            nc.vector.tensor_scalar(q[:, :], q[:, :], -0.5, 1.5, ALU.mult, ALU.add).then_inc(core.vector_done.sem, 1)
            dve.wait_ge(core.vector_done.sem, core.vector_done.up())
            nc.vector.tensor_tensor(y[:, :], y[:, :], q[:, :], ALU.mult).then_inc(core.vector_done.sem, 1)
            dve.wait_ge(core.vector_done.sem, core.vector_done.up())
            for t in range(TILES):
                last = nc.vector.tensor_scalar(xn[:, t, :], src[:, t, :], mv[:, t, 0:1], y[:, t:t + 1],
                                               ALU.subtract, ALU.mult)
            last.then_inc(core.vector_done.sem, 1)
            dve.wait_ge(core.vector_done.sem, core.vector_done.up())
            if gain is not None:
                for t in range(TILES):
                    last = nc.vector.tensor_tensor(xn[:, t, :], xn[:, t, :], gain[:, :], ALU.mult)
                last.then_inc(core.vector_done.sem, 1)
                dve.wait_ge(core.vector_done.sem, core.vector_done.up())
                for t in range(TILES):
                    last = nc.vector.tensor_tensor(xn[:, t, :], xn[:, t, :], shift[:, :], ALU.add)
                last.then_inc(core.vector_done.sem, 1)
                dve.wait_ge(core.vector_done.sem, core.vector_done.up())

        with nc.Block() as block:

            @block.vector
            def _(dve):
                apply(dve)

    turn_phase(core, c, xn, xnT, CH)


def turn_phase(core, c, rows, out, chunks, loads=()):
    nc = core.nc
    banks, where = [], []
    for t in range(TILES):
        for m in range(0, chunks, 4):
            k = min(4, chunks - m)
            banks.append([turned(128, ROWS, rows[:, t, chunk(m + i)], c.ident[0:ROWS, 0:ROWS], at=128 * i)
                          for i in range(k)])
            where.append((out[:, m:m + k, rows_of(t)], k))
    odd = len(banks) // 2
    filled, freed_v, freed_s = (core.bank_filled.span(len(banks)), core.vector_freed.span(len(banks) - odd),
                                core.scalar_freed.span(odd))
    with nc.Block() as block:

        @block.tensor
        def _(pe):
            for j, products in enumerate(banks):
                if j >= BANKS and j % 2 == 0:
                    pe.wait_ge(core.vector_freed.sem, freed_v + (j - BANKS) // 2 + 1)
                if j >= BANKS and j % 2 == 1:
                    pe.wait_ge(core.scalar_freed.sem, freed_s + (j - BANKS) // 2 + 1)
                fill(nc, core.bank(j), products).then_inc(core.bank_filled.sem, 1)

        @block.vector
        def _(dve):
            for j in range(0, len(banks), 2):
                dst, k = where[j]
                dve.wait_ge(core.bank_filled.sem, filled + j + 1)
                nc.vector.tensor_copy(dst, core.bank(j).rearrange("p (c n) -> p c n", c=4)[:, 0:k, 0:ROWS]).then_inc(
                    core.vector_freed.sem, 1)

        @block.scalar
        def _(act):
            for j in range(1, len(banks), 2):
                dst, k = where[j]
                act.wait_ge(core.bank_filled.sem, filled + j + 1)
                nc.scalar.activation(dst, core.bank(j).rearrange("p (c n) -> p c n", c=4)[:, 0:k, 0:ROWS],
                                     ACT.Copy).then_inc(core.scalar_freed.sem, 1)

        @block.sync
        def _(sync):
            for dst, src in loads:
                sync.dma_start(dst, src).then_inc(core.landed.sem, 16)
            if loads:
                sync.wait_ge(core.landed.sem, core.landed.up(16 * len(loads)))


def row_products(xT, W, cols=DIM, chunks=CH):
    return [[product(ROWS, [(xT[:, k, rows_of(t)], W[:, k, :]) for k in range(chunks)], cols)]
            for t in range(TILES)]


def w_view(w):
    return w.rearrange("(c p) n -> p c n", p=128)


def bcast(v, parts=ROWS):
    return v.rearrange("(a n) -> a n", a=1).to_broadcast([parts, v.shape[0]])




def adjacency_phases(core, c, d, ctx):
    nc = core.nc
    EB = EDGE_TILES // 2
    with ExitStack() as local:
        sb = Scope(nc, local, "adj_")
        raw = sb("raw", [EB, 2, 2, ROWS], I32)
        rows = sb("rows", [EB, 3, 2, ROWS])
        cols = sb("cols", [ROWS, 3, EDGE_TILES])
        w = sb("w", [ROWS, 3, EDGE_TILES])
        piece = sb("piece", [ROWS, EDGE_TILES], BF16)
        node_i = sb("node_i", [ROWS, NODES], I32)
        node = sb("node", [ROWS, NODES], F16)
        oh_src = sb("oh_src", [ROWS, 2, NODES], BF16)
        oh_dst = sb("oh_dst", [ROWS, 2, 3, NODES], BF16)
        zero = sb("zero", [ROWS, BANK], BF16)

        def edge_rows(v):
            return v.rearrange("(j r p) -> r j p", j=2, p=ROWS)

        loads = [(raw[:, 0, :, :], edge_rows(d["src"])), (raw[:, 1, :, :], edge_rows(d["dst"])),
                 (rows[:, 2, :, :], edge_rows(d["edge_weight"]))]
        with nc.Block() as block:

            @block.gpsimd
            def _(gp):
                nc.gpsimd.iota(node_i[:, :], [[1, NODES]], base=0, channel_multiplier=0).then_inc(core.pool_done.sem, 1)
                gp.wait_ge(core.pool_done.sem, core.pool_done.up())
                nc.gpsimd.memset(zero[:, :], 0.0).then_inc(core.pool_done.sem, 1)
                gp.wait_ge(core.pool_done.sem, core.pool_done.up())

            @block.sync
            def _(sync):
                for dst, src in loads:
                    sync.dma_start(dst, src).then_inc(core.landed.sem, 16)
                sync.wait_ge(core.landed.sem, core.landed.up(16 * len(loads)))


        def to_float(dve):
            nc.vector.tensor_copy(node[:, :], node_i[:, :])
            nc.vector.tensor_copy(rows[:, 0:2, :, :].rearrange("p a j n -> p (a j n)"),
                                         raw[:, :, :, :].rearrange("p a j n -> p (a j n)")).then_inc(core.vector_done.sem, 1)
            dve.wait_ge(core.vector_done.sem, core.vector_done.up())

        with nc.Block() as block:

            @block.vector
            def _(dve):
                to_float(dve)

        banks = [[turned(ROWS, EB, rows[:, a, j, :], c.ident[0:EB, 0:EB], at=j * EB) for j in range(2)]
                 for a in range(3)]
        filled, freed = core.bank_filled.span(len(banks)), core.vector_freed.span(len(banks))
        with nc.Block() as block:

            @block.tensor
            def _(pe):
                for j, products in enumerate(banks):
                    if j >= BANKS:
                        pe.wait_ge(core.vector_freed.sem, freed + j - BANKS + 1)
                    fill(nc, core.bank(j), products).then_inc(core.bank_filled.sem, 1)

            @block.vector
            def _(dve):
                for j in range(len(banks)):
                    dve.wait_ge(core.bank_filled.sem, filled + j + 1)
                    if j:
                        dve.wait_ge(core.vector_freed.sem, freed + j)
                    nc.vector.tensor_copy(
                        cols[:, j, :], core.bank(j)[0:ROWS, 0:EDGE_TILES]).then_inc(
                        core.vector_freed.sem, 1)


        def split(dve):
            nc.vector.tensor_copy(piece[:, :], cols[:, 2, :]).then_inc(core.vector_done.sem, 1)
            dve.wait_ge(core.vector_done.sem, core.vector_done.up())
            nc.vector.tensor_copy(w[:, 0, :], piece[:, :]).then_inc(core.vector_done.sem, 1)
            dve.wait_ge(core.vector_done.sem, core.vector_done.up())
            nc.vector.tensor_tensor(w[:, 2, :], cols[:, 2, :], w[:, 0, :], ALU.subtract).then_inc(core.vector_done.sem, 1)
            dve.wait_ge(core.vector_done.sem, core.vector_done.up())
            nc.vector.tensor_copy(piece[:, :], w[:, 2, :]).then_inc(core.vector_done.sem, 1)
            dve.wait_ge(core.vector_done.sem, core.vector_done.up())
            nc.vector.tensor_copy(w[:, 1, :], piece[:, :]).then_inc(core.vector_done.sem, 1)
            dve.wait_ge(core.vector_done.sem, core.vector_done.up())
            nc.vector.tensor_tensor(w[:, 2, :], w[:, 2, :], w[:, 1, :], ALU.subtract).then_inc(core.vector_done.sem, 1)
            dve.wait_ge(core.vector_done.sem, core.vector_done.up())

        with nc.Block() as block:

            @block.vector
            def _(dve):
                split(dve)


        flat = core.psum[0:ROWS, :, :].rearrange("p b n -> p (b n)")
        for weighted, out in ((False, c.CT), (True, c.AT)):
            parts = 3 if weighted else 1
            made, used, summed = core.made, core.used, core.summed
            made0, used0, summed0 = made.span(EDGE_TILES), used.span(EDGE_TILES + 2), summed.span(1)
            with nc.Block() as block:

                @block.vector
                def _(dve):
                    with dve.Fori(0, EDGE_TILES // 2) as i:
                        for b in range(2):
                            t = i * 2 + b
                            dve.wait_ge(used.sem, t + (used0 + 1))
                            nc.vector.tensor_scalar(oh_src[:, b, :], node[:, :], cols[:, 0, bass.ds(t, 1)],
                                                    None, ALU.is_equal)
                            for q in range(parts):
                                if weighted:
                                    last = nc.vector.tensor_scalar(
                                        oh_dst[:, b, q, :], node[:, :], cols[:, 1, bass.ds(t, 1)],
                                        w[:, q, bass.ds(t, 1)], ALU.is_equal, ALU.mult)
                                else:
                                    last = nc.vector.tensor_scalar(
                                        oh_dst[:, b, q, :], node[:, :], cols[:, 1, bass.ds(t, 1)],
                                        None, ALU.is_equal)
                            last.then_inc(made.sem, 1)
                    dve.wait_ge(summed.sem, summed0 + 1)
                    for k in range(TILES):
                        last = nc.vector.tensor_copy(
                            out[:, :, rows_of(k)],
                            flat[:, k * TILES * 128:(k + 1) * TILES * 128].rearrange(
                                "p (s n) -> p s n", s=TILES)[:, :, 0:ROWS])

                @block.tensor
                def _(pe):
                    for b in range(BANKS - 1):
                        last = nc.tensor.matmul(core.psum[0:ROWS, b, :], zero[:, 0:ROWS], zero[:, :],
                                                start=True, stop=False, skip_group_check=True)
                    last.then_inc(used.sem, 2)
                    with pe.Fori(0, EDGE_TILES // 2) as i:
                        for b in range(2):
                            pe.wait_ge(made.sem, i * 2 + (made0 + b + 1))
                            for k in range(TILES):
                                for s in range(TILES):
                                    for q in range(parts):
                                        last = nc.tensor.matmul(
                                            flat[:, (k * TILES + s) * 128:(k * TILES + s) * 128 + ROWS],
                                            oh_src[:, b, rows_of(s)], oh_dst[:, b, q, rows_of(k)],
                                            start=False, stop=False, skip_group_check=True)
                            last.then_inc(used.sem, 1)
                    nc.tensor.matmul(core.psum[0:ROWS, BANKS - 1, 0:BANK], zero[:, 0:ROWS], zero[:, :],
                                     start=True, stop=True).then_inc(summed.sem, 1)




def layer0_gnn(core, c, d):
    nc = core.nc
    with ExitStack() as ctx:
        sb = Scope(nc, ctx, "g0_")
        W = [sb(f"W{k}", [128, CH, DIM]) for k in range(4)]
        diag = sb("diag", [128, NODES])
        b1 = sb("b1", [128, CH])
        b2 = sb("b2", [ROWS, DIM])
        scaled = sb("scaled", [128, CH, NODES])
        hw = sb("hw", [ROWS, TILES, DIM])
        h1T = sb("h1T", [128, CH, NODES])
        u = sb("u", [ROWS, DIM])
        names = ["W0_1", "W1_1", "W0_2", "W1_2"]
        loads = [(W[k][:, :, :], w_view(d["L0_gnn_" + names[k]])) for k in range(4)]
        loads += [(diag[:, :], bcast(d["node_vec"], 128)), (b1[:, :], d["L0_gnn_b1"]),
                  (b2[:, :], bcast(d["L0_gnn_b2"]))]
        with nc.Block() as block:

            @block.sync
            def _(sync):
                for dst, src in loads:
                    sync.dma_start(dst, src).then_inc(core.landed.sem, 16)
                sync.wait_ge(core.landed.sem, core.landed.up(16 * len(loads)))


        def scale_nodes(srcT):
            def f(dve):
                for k in range(CH):
                    last = nc.vector.tensor_tensor(scaled[:, k, :], srcT[:, k, :], diag[:, :], ALU.mult)
                last.then_inc(core.vector_done.sem, 1)
                dve.wait_ge(core.vector_done.sem, core.vector_done.up())
            return f

        with nc.Block() as block:

            @block.vector
            def _(dve):
                scale_nodes(c.xnT)(dve)


        def keep_rows(act, j, bank):
            return nc.scalar.activation(hw[:, j, :], bank[0:ROWS, :], ACT.Copy)

        banks = row_products(c.xnT, W[1])
        filled, freed = core.bank_filled.span(len(banks)), core.scalar_freed.span(len(banks))
        with nc.Block() as block:

            @block.tensor
            def _(pe):
                for j, products in enumerate(banks):
                    if j >= BANKS:
                        pe.wait_ge(core.scalar_freed.sem, freed + j - BANKS + 1)
                    fill(nc, core.bank(j), products).then_inc(core.bank_filled.sem, 1)

            @block.scalar
            def _(act):
                for j in range(len(banks)):
                    act.wait_ge(core.bank_filled.sem, filled + j + 1)
                    keep_rows(act, j, core.bank(j)).then_inc(core.scalar_freed.sem, 1)

        banks = []
        for m in range(CH):
            banks += halves(128, lambda a, b: [(W[0][:, k, chunk(m)], scaled[:, k, a:b]) for k in range(CH)]
                            + [(hw[:, s, chunk(m)], c.AT[:, s, a:b]) for s in range(TILES)])

        def relu_h1(act, j, bank):
            m, (a, b) = j // 2, HALVES[j % 2]
            return nc.scalar.activation(h1T[:, m, a:b], bank[:, 0:b - a], ACT.Relu, bias=b1[:, m:m + 1])

        filled, freed = core.bank_filled.span(len(banks)), core.scalar_freed.span(len(banks))
        with nc.Block() as block:

            @block.tensor
            def _(pe):
                for j, products in enumerate(banks):
                    if j >= BANKS:
                        pe.wait_ge(core.scalar_freed.sem, freed + j - BANKS + 1)
                    fill(nc, core.bank(j), products).then_inc(core.bank_filled.sem, 1)

            @block.scalar
            def _(act):
                for j in range(len(banks)):
                    act.wait_ge(core.bank_filled.sem, filled + j + 1)
                    relu_h1(act, j, core.bank(j)).then_inc(core.scalar_freed.sem, 1)

        with nc.Block() as block:

            @block.vector
            def _(dve):
                scale_nodes(h1T)(dve)

        banks = row_products(h1T, W[3])
        filled, freed = core.bank_filled.span(len(banks)), core.scalar_freed.span(len(banks))
        with nc.Block() as block:

            @block.tensor
            def _(pe):
                for j, products in enumerate(banks):
                    if j >= BANKS:
                        pe.wait_ge(core.scalar_freed.sem, freed + j - BANKS + 1)
                    fill(nc, core.bank(j), products).then_inc(core.bank_filled.sem, 1)

            @block.scalar
            def _(act):
                for j in range(len(banks)):
                    act.wait_ge(core.bank_filled.sem, filled + j + 1)
                    keep_rows(act, j, core.bank(j)).then_inc(core.scalar_freed.sem, 1)

        banks = [[product(ROWS, [(scaled[:, k, rows_of(t)], W[2][:, k, :]) for k in range(CH)]
                          + [(c.AT[:, s, rows_of(t)], hw[:, s, :]) for s in range(TILES)], DIM)]
                 for t in range(TILES)]

        def finish(dve, t, bank):
            nc.vector.tensor_tensor(u[:, :], bank[0:ROWS, :], b2[:, :], ALU.add).then_inc(core.vector_done.sem, 1)
            dve.wait_ge(core.vector_done.sem, core.vector_done.up())
            nc.vector.scalar_tensor_tensor(out=u[:, :], in0=u[:, :], scalar=0.0, in1=c.xn[:, t, :],
                                                  op0=ALU.max, op1=ALU.add).then_inc(core.vector_done.sem, 1)
            dve.wait_ge(core.vector_done.sem, core.vector_done.up())
            return nc.vector.scalar_tensor_tensor(out=c.x[:, t, :], in0=u[:, :], scalar=0.5,
                                                  in1=c.x[:, t, :], op0=ALU.mult, op1=ALU.add)

        filled, freed = core.bank_filled.span(len(banks)), core.vector_freed.span(len(banks))
        with nc.Block() as block:

            @block.tensor
            def _(pe):
                for j, products in enumerate(banks):
                    if j >= BANKS:
                        pe.wait_ge(core.vector_freed.sem, freed + j - BANKS + 1)
                    fill(nc, core.bank(j), products).then_inc(core.bank_filled.sem, 1)

            @block.vector
            def _(dve):
                for j in range(len(banks)):
                    dve.wait_ge(core.bank_filled.sem, filled + j + 1)
                    if j:
                        dve.wait_ge(core.vector_freed.sem, freed + j)
                    finish(dve, j, core.bank(j)).then_inc(core.vector_freed.sem, 1)


def add_biased(core, c, u, bias, extra):
    nc = core.nc

    def f(dve, t, bank):
        nc.vector.tensor_tensor(u[:, :], bank[0:ROWS, :], bias[:, :], ALU.add).then_inc(core.vector_done.sem, 1)
        dve.wait_ge(core.vector_done.sem, core.vector_done.up())
        if extra is not None:
            nc.vector.tensor_tensor(u[:, :], u[:, :], extra[:, t, :], ALU.add).then_inc(core.vector_done.sem, 1)
            dve.wait_ge(core.vector_done.sem, core.vector_done.up())
        return nc.vector.tensor_tensor(c.x[:, t, :], c.x[:, t, :], u[:, :], ALU.add)
    return f


def layer0_mix(core, c, d):
    nc = core.nc
    EPS = 1e-6
    TH = TILES * HEADS
    with ExitStack() as ctx:
        sb = Scope(nc, ctx, "m0_")
        W = {k: sb("W" + k, [128, CH, DIM]) for k in "qkvo"}
        B = {k: sb("b" + k, [ROWS, DIM]) for k in "qkvo"}
        temp = sb("temp", [ROWS, 1])
        qkv = sb("qkv", [ROWS, 3, TILES, DIM])
        qk = sb("qk", [ROWS, TILES, DIM])
        oT = sb("oT", [128, CH, NODES])
        u = sb("u", [ROWS, DIM])
        names = ["Sqk", "Sq", "Sk", "aq", "ak", "flow", "sink", "src", "f", "big", "t1", "e"]
        s = {n: sb(n, [ROWS, TH]) for n in names}
        loads = [(W[k][:, :, :], w_view(d["L0_mix_W" + k])) for k in "qkvo"]
        loads += [(B[k][:, :], bcast(d["L0_mix_b" + k])) for k in "qkvo"]
        loads += [(temp[:, :], bcast(d["L0_mix_temperature"]))]
        with nc.Block() as block:

            @block.sync
            def _(sync):
                for dst, src in loads:
                    sync.dma_start(dst, src).then_inc(core.landed.sem, 16)
                sync.wait_ge(core.landed.sem, core.landed.up(16 * len(loads)))


        banks = []
        for k in "qkv":
            banks += row_products(c.xnT, W[k])

        def with_bias(dve, j, bank):
            return nc.vector.tensor_tensor(qkv[:, j // TILES, j % TILES, :], bank[0:ROWS, :],
                                           B["qkv"[j // TILES]][:, :], ALU.add)

        filled, freed = core.bank_filled.span(len(banks)), core.vector_freed.span(len(banks))
        with nc.Block() as block:

            @block.tensor
            def _(pe):
                for j, products in enumerate(banks):
                    if j >= BANKS:
                        pe.wait_ge(core.vector_freed.sem, freed + j - BANKS + 1)
                    fill(nc, core.bank(j), products).then_inc(core.bank_filled.sem, 1)

            @block.vector
            def _(dve):
                for j in range(len(banks)):
                    dve.wait_ge(core.bank_filled.sem, filled + j + 1)
                    if j:
                        dve.wait_ge(core.vector_freed.sem, freed + j)
                    with_bias(dve, j, core.bank(j)).then_inc(core.vector_freed.sem, 1)

        with nc.Block() as block:

            @block.scalar
            def _(act):
                nc.scalar.activation(
                    qkv[:, 0:2, :, :].rearrange("p a t n -> p (a t n)"),
                    qkv[:, 0:2, :, :].rearrange("p a t n -> p (a t n)"), ACT.Sigmoid).then_inc(core.scalar_done.sem, 1)
                act.wait_ge(core.scalar_done.sem, core.scalar_done.up())


        def by_head(ap):
            return ap.rearrange("p t (h e) -> p (t h) e", h=HEADS)

        def tt(dve, out, a, b, op):
            nc.vector.tensor_tensor(s[out][:, :], s[a][:, :], s[b][:, :], op).then_inc(core.vector_done.sem, 1)
            dve.wait_ge(core.vector_done.sem, core.vector_done.up())

        def ts(dve, out, a, s1, s2, op0, op1):
            nc.vector.tensor_scalar(s[out][:, :], s[a][:, :], s1, s2, op0, op1).then_inc(core.vector_done.sem, 1)
            dve.wait_ge(core.vector_done.sem, core.vector_done.up())

        def flows(dve):
            nc.vector.tensor_tensor(qk[:, :, :], qkv[:, 0, :, :], qkv[:, 1, :, :], ALU.mult).then_inc(core.vector_done.sem, 1)
            dve.wait_ge(core.vector_done.sem, core.vector_done.up())
            nc.vector.tensor_reduce(s["Sqk"][:, :], by_head(qk[:, :, :]), AX.X, ALU.add)
            nc.vector.tensor_reduce(s["Sq"][:, :], by_head(qkv[:, 0, :, :]), AX.X, ALU.add)
            nc.vector.tensor_reduce(s["Sk"][:, :], by_head(qkv[:, 1, :, :]), AX.X, ALU.add).then_inc(core.vector_done.sem, 1)
            dve.wait_ge(core.vector_done.sem, core.vector_done.up())
            ts(dve, "t1", "Sq", EPS, None, ALU.mult, ALU.bypass)
            tt(dve, "aq", "Sqk", "t1", ALU.add)
            ts(dve, "e", "Sk", EPS, None, ALU.mult, ALU.bypass)
            tt(dve, "ak", "Sqk", "e", ALU.add)
            tt(dve, "flow", "aq", "e", ALU.add)
            ts(dve, "flow", "flow", HDIM * EPS * EPS + EPS, None, ALU.add, ALU.bypass)
            nc.vector.reciprocal(s["f"][:, :], s["flow"][:, :]).then_inc(core.vector_done.sem, 1)
            dve.wait_ge(core.vector_done.sem, core.vector_done.up())
            tt(dve, "sink", "f", "ak", ALU.mult)
            tt(dve, "sink", "sink", "t1", ALU.add)
            ts(dve, "sink", "sink", HDIM * EPS * EPS + EPS, None, ALU.add, ALU.bypass)
            tt(dve, "src", "f", "aq", ALU.mult)
            tt(dve, "src", "src", "e", ALU.add)
            ts(dve, "src", "src", HDIM * EPS * EPS + EPS, None, ALU.add, ALU.bypass)
            ts(dve, "src", "src", 1.0, -1.0, ALU.min, ALU.max)
            nc.vector.reciprocal(temp[:, :], temp[:, :]).then_inc(core.vector_done.sem, 1)
            dve.wait_ge(core.vector_done.sem, core.vector_done.up())
            ts(dve, "src", "src", temp[:, 0:1], None, ALU.mult, ALU.bypass)
            tt(dve, "big", "src", "src", ALU.subtract)

        with nc.Block() as block:

            @block.vector
            def _(dve):
                flows(dve)


        def acts(act):
            nc.scalar.activation(s["e"][:, :], s["big"][:, :], ACT.Exp)
            nc.scalar.activation(s["sink"][:, :], s["sink"][:, :], ACT.Sigmoid).then_inc(core.scalar_done.sem, 1)
            act.wait_ge(core.scalar_done.sem, core.scalar_done.up())

        with nc.Block() as block:

            @block.scalar
            def _(act):
                acts(act)


        def weigh(dve):
            nc.vector.reciprocal(s["t1"][:, :], s["e"][:, :]).then_inc(core.vector_done.sem, 1)
            dve.wait_ge(core.vector_done.sem, core.vector_done.up())
            tt(dve, "e", "e", "t1", ALU.mult)
            ts(dve, "e", "e", float(DIM), None, ALU.mult, ALU.bypass)
            tt(dve, "f", "f", "sink", ALU.mult)
            tt(dve, "f", "f", "e", ALU.mult)
            tt(dve, "f", "f", "Sqk", ALU.mult)
            nc.vector.tensor_tensor(
                by_head(qk[:, :, :]), by_head(qkv[:, 2, :, :]),
                s["f"][:, :].unsqueeze(2).to_broadcast([ROWS, TH, HDIM]), ALU.mult).then_inc(core.vector_done.sem, 1)
            dve.wait_ge(core.vector_done.sem, core.vector_done.up())

        with nc.Block() as block:

            @block.vector
            def _(dve):
                weigh(dve)

        turn_phase(core, c, qk, oT, CH)
        add_to_x = add_biased(core, c, u, B["o"], c.xn)
        banks = row_products(oT, W["o"])
        filled, freed = core.bank_filled.span(len(banks)), core.vector_freed.span(len(banks))
        with nc.Block() as block:

            @block.tensor
            def _(pe):
                for j, products in enumerate(banks):
                    if j >= BANKS:
                        pe.wait_ge(core.vector_freed.sem, freed + j - BANKS + 1)
                    fill(nc, core.bank(j), products).then_inc(core.bank_filled.sem, 1)

            @block.vector
            def _(dve):
                for j in range(len(banks)):
                    dve.wait_ge(core.bank_filled.sem, filled + j + 1)
                    if j:
                        dve.wait_ge(core.vector_freed.sem, freed + j)
                    add_to_x(dve, j, core.bank(j)).then_inc(core.vector_freed.sem, 1)


def quantise_phase(core, c, w, chunks, width, group_scale):
    nc = core.nc
    with ExitStack() as ctx:
        sb = Scope(nc, ctx, "quant_")
        size = sb("size", [128, width])
        sc = sb("sc", [128, BANK])
        up = sb("up", [128, BANK])
        down = sb("down", [128, BANK])
        cuts = [(a, min(a + BANK, width)) for a in range(0, width, BANK)]
        for k in range(chunks):
            with nc.Block() as block:

                @block.scalar
                def _(act):
                    nc.scalar.activation(size[:, :], w[:, k, :], ACT.Abs).then_inc(core.scalar_done.sem, 1)
                    act.wait_ge(core.scalar_done.sem, core.scalar_done.up())

            banks = [[product(128, [(c.ones[:, :], size[:, a:b])], b - a)] for a, b in cuts]

            def f(dve, j, bank):
                a, b = cuts[j]
                n, wk = b - a, w[:, k, a:b]
                nc.vector.tensor_scalar(sc[:, 0:n], bank[:, 0:n], 1.0 / 128, 1e-5, ALU.mult, ALU.add).then_inc(core.vector_done.sem, 1)
                dve.wait_ge(core.vector_done.sem, core.vector_done.up())
                nc.vector.scalar_tensor_tensor(out=up[:, 0:n], in0=wk, scalar=2.0, in1=sc[:, 0:n],
                                               op0=ALU.mult, op1=ALU.is_gt)
                nc.vector.scalar_tensor_tensor(out=down[:, 0:n], in0=wk, scalar=-2.0, in1=sc[:, 0:n],
                                                      op0=ALU.mult, op1=ALU.is_gt).then_inc(core.vector_done.sem, 1)
                dve.wait_ge(core.vector_done.sem, core.vector_done.up())
                nc.vector.tensor_tensor(up[:, 0:n], up[:, 0:n], down[:, 0:n], ALU.subtract).then_inc(core.vector_done.sem, 1)
                dve.wait_ge(core.vector_done.sem, core.vector_done.up())
                last = nc.vector.tensor_tensor(wk, up[:, 0:n], sc[:, 0:n], ALU.mult)
                last.then_inc(core.vector_done.sem, 1)
                dve.wait_ge(core.vector_done.sem, core.vector_done.up())
                return nc.vector.tensor_copy(up[:, 0:1], bank[:, 0:1])

            filled, freed = core.bank_filled.span(len(banks)), core.vector_freed.span(len(banks))
            with nc.Block() as block:

                @block.tensor
                def _(pe):
                    for j, products in enumerate(banks):
                        if j >= BANKS:
                            pe.wait_ge(core.vector_freed.sem, freed + j - BANKS + 1)
                        fill(nc, core.bank(j), products).then_inc(core.bank_filled.sem, 1)

                @block.vector
                def _(dve):
                    for j in range(len(banks)):
                        dve.wait_ge(core.bank_filled.sem, filled + j + 1)
                        if j:
                            dve.wait_ge(core.vector_freed.sem, freed + j)
                        f(dve, j, core.bank(j)).then_inc(core.vector_freed.sem, 1)


def layer0_ffn(core, c, d):
    nc = core.nc
    FT = FFN0 // 128
    with ExitStack() as ctx:
        sb = Scope(nc, ctx, "f0_")
        gate = sb("gate", [128, CH, FFN0])
        up = sb("up", [128, CH, FFN0])
        down = sb("down", [128, FT, DIM])
        hT = sb("hT", [128, FT, NODES])
        loads = [(gate[:, :, :], w_view(d["L0_ffn_w_gate"])), (up[:, :, :], w_view(d["L0_ffn_w_up"])),
                 (down[:, :, :], w_view(d["L0_ffn_w_down"]))]
        norm_phases(core, c, c.x, c.xn, c.xnT, loads=loads)
        quantise_phase(core, c, gate, CH, FFN0, True)
        quantise_phase(core, c, up, CH, FFN0, True)
        quantise_phase(core, c, down, FT, DIM, True)
        for w, is_gate in ((gate, True), (up, False)):
            banks = []
            for f in range(FT):
                banks += halves(128, lambda a, b: [(w[:, k, chunk(f)], c.xnT[:, k, a:b]) for k in range(CH)])

            def silu(act, j, bank):
                f, (a, b) = j // 2, HALVES[j % 2]
                return nc.scalar.activation(hT[:, f, a:b], bank[:, 0:b - a], ACT.Silu)

            def times_up(dve, j, bank):
                f, (a, b) = j // 2, HALVES[j % 2]
                return nc.vector.tensor_tensor(hT[:, f, a:b], hT[:, f, a:b], bank[:, 0:b - a], ALU.mult)

            if is_gate:
                filled, freed = core.bank_filled.span(len(banks)), core.scalar_freed.span(len(banks))
                with nc.Block() as block:

                    @block.tensor
                    def _(pe):
                        for j, products in enumerate(banks):
                            if j >= BANKS:
                                pe.wait_ge(core.scalar_freed.sem, freed + j - BANKS + 1)
                            fill(nc, core.bank(j), products).then_inc(core.bank_filled.sem, 1)

                    @block.scalar
                    def _(act):
                        for j in range(len(banks)):
                            act.wait_ge(core.bank_filled.sem, filled + j + 1)
                            silu(act, j, core.bank(j)).then_inc(core.scalar_freed.sem, 1)

            else:
                filled, freed = core.bank_filled.span(len(banks)), core.vector_freed.span(len(banks))
                with nc.Block() as block:

                    @block.tensor
                    def _(pe):
                        for j, products in enumerate(banks):
                            if j >= BANKS:
                                pe.wait_ge(core.vector_freed.sem, freed + j - BANKS + 1)
                            fill(nc, core.bank(j), products).then_inc(core.bank_filled.sem, 1)

                    @block.vector
                    def _(dve):
                        for j in range(len(banks)):
                            dve.wait_ge(core.bank_filled.sem, filled + j + 1)
                            if j:
                                dve.wait_ge(core.vector_freed.sem, freed + j)
                            times_up(dve, j, core.bank(j)).then_inc(core.vector_freed.sem, 1)

        banks = row_products(hT, down, chunks=FT)
        filled, freed = core.bank_filled.span(len(banks)), core.vector_freed.span(len(banks))
        with nc.Block() as block:

            @block.tensor
            def _(pe):
                for j, products in enumerate(banks):
                    if j >= BANKS:
                        pe.wait_ge(core.vector_freed.sem, freed + j - BANKS + 1)
                    fill(nc, core.bank(j), products).then_inc(core.bank_filled.sem, 1)

            @block.vector
            def _(dve):
                for j in range(len(banks)):
                    dve.wait_ge(core.bank_filled.sem, filled + j + 1)
                    if j:
                        dve.wait_ge(core.vector_freed.sem, freed + j)
                    nc.vector.tensor_tensor(
                        c.x[:, j, :], c.x[:, j, :], core.bank(j)[0:ROWS, :], ALU.add).then_inc(
                        core.vector_freed.sem, 1)




def layer1_gnn(core, c, d):
    nc = core.nc
    with ExitStack() as ctx:
        sb = Scope(nc, ctx, "g1_")
        W = sb("W", [128, 2 * CH, DIM])
        b = sb("b", [ROWS, DIM])
        rdeg = sb("rdeg", [128, NODES])
        meanT = sb("meanT", [128, CH, NODES])
        u = sb("u", [ROWS, DIM])
        loads = [(W[:, :, :], w_view(d["L1_gnn_W"])), (b[:, :], bcast(d["L1_gnn_b"]))]
        norm_phases(core, c, c.x, c.xn, c.xnT, loads=loads)
        banks = halves(128, lambda a, b: [(c.ones[0:ROWS, :], c.CT[:, s, a:b]) for s in range(TILES)])

        def degree(dve, j, bank):
            a, e = HALVES[j]
            nc.vector.tensor_scalar(rdeg[:, a:e], bank[:, 0:e - a], 1.0, None, ALU.max).then_inc(core.vector_done.sem, 1)
            dve.wait_ge(core.vector_done.sem, core.vector_done.up())
            last = nc.vector.reciprocal(rdeg[:, a:e], rdeg[:, a:e])
            return last

        filled, freed = core.bank_filled.span(len(banks)), core.vector_freed.span(len(banks))
        with nc.Block() as block:

            @block.tensor
            def _(pe):
                for j, products in enumerate(banks):
                    if j >= BANKS:
                        pe.wait_ge(core.vector_freed.sem, freed + j - BANKS + 1)
                    fill(nc, core.bank(j), products).then_inc(core.bank_filled.sem, 1)

            @block.vector
            def _(dve):
                for j in range(len(banks)):
                    dve.wait_ge(core.bank_filled.sem, filled + j + 1)
                    if j:
                        dve.wait_ge(core.vector_freed.sem, freed + j)
                    degree(dve, j, core.bank(j)).then_inc(core.vector_freed.sem, 1)

        banks = []
        for m in range(CH):
            banks += halves(128, lambda a, b: [(c.xn[:, s, chunk(m)], c.CT[:, s, a:b]) for s in range(TILES)])

        def mean(dve, j, bank):
            m, (a, e) = j // 2, HALVES[j % 2]
            return nc.vector.tensor_tensor(meanT[:, m, a:e], bank[:, 0:e - a], rdeg[:, a:e], ALU.mult)

        filled, freed = core.bank_filled.span(len(banks)), core.vector_freed.span(len(banks))
        with nc.Block() as block:

            @block.tensor
            def _(pe):
                for j, products in enumerate(banks):
                    if j >= BANKS:
                        pe.wait_ge(core.vector_freed.sem, freed + j - BANKS + 1)
                    fill(nc, core.bank(j), products).then_inc(core.bank_filled.sem, 1)

            @block.vector
            def _(dve):
                for j in range(len(banks)):
                    dve.wait_ge(core.bank_filled.sem, filled + j + 1)
                    if j:
                        dve.wait_ge(core.vector_freed.sem, freed + j)
                    mean(dve, j, core.bank(j)).then_inc(core.vector_freed.sem, 1)

        banks = [[product(ROWS, [(c.xnT[:, k, rows_of(t)], W[:, k, :]) for k in range(CH)]
                          + [(meanT[:, k, rows_of(t)], W[:, CH + k, :]) for k in range(CH)], DIM)]
                 for t in range(TILES)]

        def finish(dve, t, bank):
            nc.vector.tensor_tensor(u[:, :], bank[0:ROWS, :], b[:, :], ALU.add).then_inc(core.vector_done.sem, 1)
            dve.wait_ge(core.vector_done.sem, core.vector_done.up())
            return nc.vector.scalar_tensor_tensor(out=c.x[:, t, :], in0=u[:, :], scalar=0.0,
                                                  in1=c.x[:, t, :], op0=ALU.max, op1=ALU.add)

        filled, freed = core.bank_filled.span(len(banks)), core.vector_freed.span(len(banks))
        with nc.Block() as block:

            @block.tensor
            def _(pe):
                for j, products in enumerate(banks):
                    if j >= BANKS:
                        pe.wait_ge(core.vector_freed.sem, freed + j - BANKS + 1)
                    fill(nc, core.bank(j), products).then_inc(core.bank_filled.sem, 1)

            @block.vector
            def _(dve):
                for j in range(len(banks)):
                    dve.wait_ge(core.bank_filled.sem, filled + j + 1)
                    if j:
                        dve.wait_ge(core.vector_freed.sem, freed + j)
                    finish(dve, j, core.bank(j)).then_inc(core.vector_freed.sem, 1)


def linear_attention(core, c, QT, K, V1, sink, eps, accumulate):
    nc = core.nc
    with ExitStack() as ctx:
        sb = Scope(nc, ctx, "la_")
        kv = sb("kv", [128, PAIRS, 130])
        r = sb("r", [ROWS, 2, 2])
        with nc.Block() as block:

            @block.gpsimd
            def _(gp):
                nc.gpsimd.memset(kv[:, :, :], 0.0).then_inc(core.pool_done.sem, 1)
                gp.wait_ge(core.pool_done.sem, core.pool_done.up())

        banks = [[product(128, [(K[:, t, chunk(p)], V1[:, t, p, :]) for t in range(TILES)], 129)]
                 for p in range(PAIRS)]

        def blocks(dve, p, bank):
            for i in range(2):
                h = slice(HDIM * i, HDIM * (i + 1))
                nc.vector.tensor_copy(kv[h, p, h], bank[h, h])
                last = nc.vector.tensor_copy(kv[h, p, 128 + i:129 + i], bank[h, 128:129])
            return last

        filled, freed = core.bank_filled.span(len(banks)), core.vector_freed.span(len(banks))
        with nc.Block() as block:

            @block.tensor
            def _(pe):
                for j, products in enumerate(banks):
                    if j >= BANKS:
                        pe.wait_ge(core.vector_freed.sem, freed + j - BANKS + 1)
                    fill(nc, core.bank(j), products).then_inc(core.bank_filled.sem, 1)

            @block.vector
            def _(dve):
                for j in range(len(banks)):
                    dve.wait_ge(core.bank_filled.sem, filled + j + 1)
                    if j:
                        dve.wait_ge(core.vector_freed.sem, freed + j)
                    blocks(dve, j, core.bank(j)).then_inc(core.vector_freed.sem, 1)

        banks = [[product(ROWS, [(QT[:, p, rows_of(t)], kv[:, p, :])], 130)]
                 for t in range(TILES) for p in range(PAIRS)]

        def divide(dve, j, bank):
            t, p = j // PAIRS, j % PAIRS
            rj = r[:, j % 2, :]
            if eps:
                nc.vector.tensor_scalar(rj, bank[0:ROWS, 128:130], eps, None, ALU.add).then_inc(core.vector_done.sem, 1)
                dve.wait_ge(core.vector_done.sem, core.vector_done.up())
                nc.vector.reciprocal(rj, rj).then_inc(core.vector_done.sem, 1)
                dve.wait_ge(core.vector_done.sem, core.vector_done.up())
            else:
                nc.vector.reciprocal(rj, bank[0:ROWS, 128:130]).then_inc(core.vector_done.sem, 1)
                dve.wait_ge(core.vector_done.sem, core.vector_done.up())
            for i in range(2):
                dst = sink[:, t, 128 * p + HDIM * i:128 * p + HDIM * (i + 1)]
                num = bank[0:ROWS, HDIM * i:HDIM * (i + 1)]
                if accumulate:
                    last = nc.vector.scalar_tensor_tensor(out=dst, in0=num, scalar=rj[:, i:i + 1], in1=dst,
                                                          op0=ALU.mult, op1=ALU.add)
                else:
                    last = nc.vector.tensor_scalar(dst, num, rj[:, i:i + 1], None, ALU.mult)
            return last

        filled, freed = core.bank_filled.span(len(banks)), core.vector_freed.span(len(banks))
        with nc.Block() as block:

            @block.tensor
            def _(pe):
                for j, products in enumerate(banks):
                    if j >= BANKS:
                        pe.wait_ge(core.vector_freed.sem, freed + j - BANKS + 1)
                    fill(nc, core.bank(j), products).then_inc(core.bank_filled.sem, 1)

            @block.vector
            def _(dve):
                for j in range(len(banks)):
                    dve.wait_ge(core.bank_filled.sem, filled + j + 1)
                    if j:
                        dve.wait_ge(core.vector_freed.sem, freed + j)
                    divide(dve, j, core.bank(j)).then_inc(core.vector_freed.sem, 1)


def layer1_mix(core, c, d):
    nc = core.nc
    with ExitStack() as ctx:
        sb = Scope(nc, ctx, "m1_")
        Wq = sb("Wq", [128, CH, DIM])
        Wkv = sb("Wkv", [128, CH, 2 * DIM])
        QT = sb("QT", [128, CH, NODES])
        QT2 = sb("QT2", [128, CH, NODES])
        K = sb("K", [ROWS, TILES, DIM])
        K2 = sb("K2", [ROWS, TILES, DIM])
        V1 = sb("V1", [ROWS, TILES, PAIRS, 129])
        with nc.Block() as block:

            @block.gpsimd
            def _(gp):
                nc.gpsimd.memset(V1[:, :, :, 128:129], 1.0).then_inc(core.pool_done.sem, 1)
                gp.wait_ge(core.pool_done.sem, core.pool_done.up())

            @block.sync
            def _(sync):
                moves = [(Wq[:, :, :], w_view(d["L1_mix_Wq"])), (Wkv[:, :, :], w_view(d["L1_mix_Wkv"]))]
                for dst, src in moves:
                    sync.dma_start(dst, src).then_inc(core.landed.sem, 16)
                sync.wait_ge(core.landed.sem, core.landed.up(16 * len(moves)))

        banks = []
        for m in range(CH):
            banks += halves(128, lambda a, b: [(Wq[:, k, chunk(m)], c.xnT[:, k, a:b]) for k in range(CH)])
        nq = len(banks)
        for part in range(2):
            banks += row_products(c.xnT, Wkv[:, :, part * DIM:(part + 1) * DIM])

        def parts(dve, j, bank):
            if j >= nq + TILES:
                return nc.vector.tensor_copy(V1[:, j - nq - TILES, :, 0:128],
                                             bank[0:ROWS, :].rearrange("p (a n) -> p a n", a=PAIRS))
            if j < nq:
                m, (a, b) = j // 2, HALVES[j % 2]
                lo, hi, y = QT[:, m, a:b], QT2[:, m, a:b], bank[:, 0:b - a]
            else:
                lo, hi, y = K[:, j - nq, :], K2[:, j - nq, :], bank[0:ROWS, :]
            nc.vector.tensor_scalar(lo, y, 0.0, None, ALU.min)
            return nc.vector.tensor_scalar(hi, y, 0.0, None, ALU.max)

        filled, freed = core.bank_filled.span(len(banks)), core.vector_freed.span(len(banks))
        with nc.Block() as block:

            @block.tensor
            def _(pe):
                for j, products in enumerate(banks):
                    if j >= BANKS:
                        pe.wait_ge(core.vector_freed.sem, freed + j - BANKS + 1)
                    fill(nc, core.bank(j), products).then_inc(core.bank_filled.sem, 1)

            @block.vector
            def _(dve):
                for j in range(len(banks)):
                    dve.wait_ge(core.bank_filled.sem, filled + j + 1)
                    if j:
                        dve.wait_ge(core.vector_freed.sem, freed + j)
                    parts(dve, j, core.bank(j)).then_inc(core.vector_freed.sem, 1)


        def exps(act):
            nc.scalar.activation(QT[:, :, :], QT[:, :, :], ACT.Exp)
            nc.scalar.activation(K[:, :, :], K[:, :, :], ACT.Exp).then_inc(core.scalar_done.sem, 1)
            act.wait_ge(core.scalar_done.sem, core.scalar_done.up())

        with nc.Block() as block:

            @block.scalar
            def _(act):
                exps(act)


        def sums(dve):
            nc.vector.tensor_tensor(QT[:, :, :], QT[:, :, :], QT2[:, :, :], ALU.add)
            nc.vector.tensor_tensor(K[:, :, :], K[:, :, :], K2[:, :, :], ALU.add).then_inc(core.vector_done.sem, 1)
            dve.wait_ge(core.vector_done.sem, core.vector_done.up())

        with nc.Block() as block:

            @block.vector
            def _(dve):
                sums(dve)

        linear_attention(core, c, QT, K, V1, c.x, 1e-6, True)


def layer1_ffn(core, c, d):
    nc = core.nc
    FT = FF1 // 128
    with ExitStack() as ctx:
        sb = Scope(nc, ctx, "e1_")
        Wg = sb("Wg", [128, CH, EXP1])
        S = sb("S", [ROWS, TILES, EXP1])
        row = sb("row", [ROWS, TILES])
        rank = sb("rank", [ROWS, 3, TILES, EXP1])
        junk = sb("junk", [ROWS, 2, TILES, ROWS], BF16)
        tie = sb("tie", [ROWS, 2, ROWS], BF16)
        place_i = sb("place_i", [ROWS, TOP1], I32)
        place = sb("place", [ROWS, TOP1])
        W1 = sb("W1", [128, 2, CH, FF1])
        W2 = sb("W2", [128, 2, FT, DIM])
        b1 = sb("b1", [128, EXP1, FT])
        b2 = sb("b2", [TOPC, EXP1, DIM])
        P = sb("P", [ROWS, TILES, TOP1])
        G = sb("G", [ROWS, TILES, TOP1])
        GT = sb("GT", [TOPC, 2, NODES])
        xgT = sb("xgT", [128, CH, TOP1])
        hT = sb("hT", [128, FT, TOP1])
        O = sb("O", [TOPC, 2, DIM])
        loads = [(Wg[:, :, :], w_view(d["L1_ffn_Wg"])),
                 (b1[:, :, :], d["L1_ffn_b1"]),
                 (b2[:, :, :], d["L1_ffn_b2"].rearrange("(a e) n -> a e n", a=1).to_broadcast([TOPC, EXP1, DIM]))]

        def expert_loads(e):
            return [(W1[:, e % 2, :, :], w_view(d["L1_ffn_W1"][e])), (W2[:, e % 2, :, :], w_view(d["L1_ffn_W2"][e]))]

        norm_phases(core, c, c.x, c.xn, c.xnT, loads=loads)
        banks = row_products(c.xnT, Wg, cols=EXP1)
        filled, freed = core.bank_filled.span(len(banks)), core.vector_freed.span(len(banks))
        with nc.Block() as block:

            @block.tensor
            def _(pe):
                for j, products in enumerate(banks):
                    if j >= BANKS:
                        pe.wait_ge(core.vector_freed.sem, freed + j - BANKS + 1)
                    fill(nc, core.bank(j), products).then_inc(core.bank_filled.sem, 1)

            @block.vector
            def _(dve):
                for j in range(len(banks)):
                    dve.wait_ge(core.bank_filled.sem, filled + j + 1)
                    if j:
                        dve.wait_ge(core.vector_freed.sem, freed + j)
                    nc.vector.tensor_copy(
                        S[:, j, :], core.bank(j)[0:ROWS, 0:EXP1]).then_inc(
                        core.vector_freed.sem, 1)

            @block.gpsimd
            def _(gp):
                nc.gpsimd.iota(place_i[:, :], [[1, TOP1]], base=0, channel_multiplier=0).then_inc(core.pool_done.sem, 1)
                gp.wait_ge(core.pool_done.sem, core.pool_done.up())


        def spread(v):
            return v[:, :].unsqueeze(2).to_broadcast([ROWS, TILES, EXP1])

        def less_max(dve):
            nc.vector.tensor_copy(place[:, :], place_i[:, :])
            nc.vector.memset(rank[:, :, :, :], 0.0)
            nc.vector.tensor_reduce(row[:, :], S[:, :, :], AX.X, ALU.max).then_inc(core.vector_done.sem, 1)
            dve.wait_ge(core.vector_done.sem, core.vector_done.up())
            nc.vector.tensor_tensor(S[:, :, :], S[:, :, :], spread(row), ALU.subtract).then_inc(core.vector_done.sem, 1)
            dve.wait_ge(core.vector_done.sem, core.vector_done.up())

        with nc.Block() as block:

            @block.vector
            def _(dve):
                less_max(dve)

            @block.sync
            def _(sync):
                moves = expert_loads(0)
                for dst, src in moves:
                    sync.dma_start(dst, src).then_inc(core.landed.sem, 16)
                sync.wait_ge(core.landed.sem, core.landed.up(16 * len(moves)))

        with nc.Block() as block:

            @block.scalar
            def _(act):
                nc.scalar.activation(S[:, :, :], S[:, :, :], ACT.Exp).then_inc(core.scalar_done.sem, 1)
                act.wait_ge(core.scalar_done.sem, core.scalar_done.up())


        def normed(dve):
            nc.vector.tensor_reduce(row[:, :], S[:, :, :], AX.X, ALU.add).then_inc(core.vector_done.sem, 1)
            dve.wait_ge(core.vector_done.sem, core.vector_done.up())
            nc.vector.reciprocal(row[:, :], row[:, :]).then_inc(core.vector_done.sem, 1)
            dve.wait_ge(core.vector_done.sem, core.vector_done.up())
            nc.vector.tensor_tensor(S[:, :, :], S[:, :, :], spread(row), ALU.mult).then_inc(core.vector_done.sem, 1)
            dve.wait_ge(core.vector_done.sem, core.vector_done.up())

        with nc.Block() as block:

            @block.vector
            def _(dve):
                normed(dve)


        spread, ranked = core.spread, core.ranked
        with nc.Block() as block:

            @block.tensor
            def _(pe):
                for e in range(EXP1):
                    if e >= 4:
                        pe.wait_ge(ranked.sem, e - 3)
                    for t in range(TILES):
                        k = (e % 4) * 2 + t // 4
                        at = t % 4 * 128
                        last = nc.tensor.transpose(core.psum[0:ROWS, k, at:at + ROWS],
                                                   S[:, t, e:e + 1].to_broadcast([ROWS, ROWS]),
                                                   c.ident[0:ROWS, 0:ROWS])
                    last.then_inc(spread.sem, 1)

            @block.vector
            def _(dve):
                for e in range(EXP1):
                    dve.wait_ge(spread.sem, e + 1)
                    k = (e % 4) * 2
                    others = core.psum[0:ROWS, k:k + 2, :].rearrange("p b (t n) -> p (b t) n", n=128)
                    for t in range(TILES):
                        own = S[:, t, e:e + 1]
                        if t:
                            nc.vector.tensor_scalar(
                                junk[:, t % 2, 0:t, :], others[:, 0:t, 0:ROWS], own, 0.0, ALU.is_ge, ALU.add,
                                accum_out=rank[:, 0, t, e:e + 1]).then_inc(core.vector_done.sem, 1)
                            dve.wait_ge(core.vector_done.sem, core.vector_done.up() - 2)
                        nc.vector.tensor_scalar(
                            junk[:, t % 2, t:TILES, :], others[:, t:TILES, 0:ROWS], own, 0.0, ALU.is_gt, ALU.add,
                            accum_out=rank[:, 1, t, e:e + 1]).then_inc(core.vector_done.sem, 1)
                        dve.wait_ge(core.vector_done.sem, core.vector_done.up() - 2)
                        nc.vector.scalar_tensor_tensor(
                            out=tie[:, t % 2, :], in0=others[:, t, 0:ROWS], scalar=own,
                            in1=c.below[0:ROWS, 0:ROWS], op0=ALU.is_equal, op1=ALU.mult,
                            accum_out=rank[:, 2, t, e:e + 1]).then_inc(core.vector_done.sem, 1)
                        dve.wait_ge(core.vector_done.sem, core.vector_done.up() - 2)
                    dve.wait_ge(core.vector_done.sem, core.vector_done.count)
                    nc.vector.engine_nop().then_inc(ranked.sem, 1)

            @block.sync
            def _(sync):
                moves = expert_loads(1)
                for dst, src in moves:
                    sync.dma_start(dst, src).then_inc(core.landed.sem, 16)
                sync.wait_ge(core.landed.sem, core.landed.up(16 * len(moves)))


        def total(dve):
            nc.vector.tensor_tensor(rank[:, 0, :, :], rank[:, 0, :, :], rank[:, 1, :, :], ALU.add).then_inc(core.vector_done.sem, 1)
            dve.wait_ge(core.vector_done.sem, core.vector_done.up())
            nc.vector.tensor_tensor(rank[:, 0, :, :], rank[:, 0, :, :], rank[:, 2, :, :], ALU.add).then_inc(core.vector_done.sem, 1)
            dve.wait_ge(core.vector_done.sem, core.vector_done.up())

        with nc.Block() as block:

            @block.vector
            def _(dve):
                total(dve)


        for e in range(EXP1):
            def choose(dve):
                for t in range(TILES):
                    nc.vector.tensor_scalar(P[:, t, :], place[:, :], rank[:, 0, t, e:e + 1], None, ALU.is_equal)
                    last = nc.vector.tensor_scalar(G[:, t, :], place[:, :], rank[:, 0, t, e:e + 1],
                                                   S[:, t, e:e + 1], ALU.is_equal, ALU.mult)
                last.then_inc(core.vector_done.sem, 1)
                dve.wait_ge(core.vector_done.sem, core.vector_done.up())

            with nc.Block() as block:

                @block.vector
                def _(dve):
                    choose(dve)

            banks = [[product(128, [(c.xn[:, t, chunk(k)], P[:, t, :]) for t in range(TILES)], TOP1)]
                     for k in range(CH)]
            banks += [[turned(TOPC, ROWS, G[:, t, i * TOPC:(i + 1) * TOPC], c.ident[0:ROWS, 0:ROWS], at=128 * i)
                       for i in range(2)] for t in range(TILES)]

            def gathered(act, j, bank):
                if j < CH:
                    return nc.scalar.activation(xgT[:, j, :], bank[:, 0:TOP1], ACT.Copy)
                return nc.scalar.activation(
                    GT[:, :, rows_of(j - CH)],
                    bank[0:TOPC, 0:256].rearrange("p (i n) -> p i n", i=2)[:, :, 0:ROWS], ACT.Copy)

            filled, freed = core.bank_filled.span(len(banks)), core.scalar_freed.span(len(banks))
            with nc.Block() as block:

                @block.tensor
                def _(pe):
                    for j, products in enumerate(banks):
                        if j >= BANKS:
                            pe.wait_ge(core.scalar_freed.sem, freed + j - BANKS + 1)
                        fill(nc, core.bank(j), products).then_inc(core.bank_filled.sem, 1)

                @block.scalar
                def _(act):
                    for j in range(len(banks)):
                        act.wait_ge(core.bank_filled.sem, filled + j + 1)
                        gathered(act, j, core.bank(j)).then_inc(core.scalar_freed.sem, 1)

            banks = [[product(128, [(W1[:, e % 2, k, chunk(f)], xgT[:, k, :]) for k in range(CH)], TOP1)]
                     for f in range(FT)]
            filled, freed = core.bank_filled.span(len(banks)), core.scalar_freed.span(len(banks))
            with nc.Block() as block:

                @block.tensor
                def _(pe):
                    for j, products in enumerate(banks):
                        if j >= BANKS:
                            pe.wait_ge(core.scalar_freed.sem, freed + j - BANKS + 1)
                        fill(nc, core.bank(j), products).then_inc(core.bank_filled.sem, 1)

                @block.scalar
                def _(act):
                    for j in range(len(banks)):
                        act.wait_ge(core.bank_filled.sem, filled + j + 1)
                        nc.scalar.activation(
                            hT[:, j, :], core.bank(j)[:, 0:TOP1], ACT.Gelu, bias=b1[:, e, j:j + 1]).then_inc(
                            core.scalar_freed.sem, 1)

            banks = [[product(TOPC, [(hT[:, f, i * TOPC:(i + 1) * TOPC], W2[:, e % 2, f, :]) for f in range(FT)],
                              DIM)] for i in range(2)]
            filled, freed = core.bank_filled.span(len(banks)), core.vector_freed.span(len(banks))
            with nc.Block() as block:

                @block.tensor
                def _(pe):
                    for j, products in enumerate(banks):
                        if j >= BANKS:
                            pe.wait_ge(core.vector_freed.sem, freed + j - BANKS + 1)
                        fill(nc, core.bank(j), products).then_inc(core.bank_filled.sem, 1)

                @block.vector
                def _(dve):
                    for j in range(len(banks)):
                        dve.wait_ge(core.bank_filled.sem, filled + j + 1)
                        if j:
                            dve.wait_ge(core.vector_freed.sem, freed + j)
                        nc.vector.tensor_tensor(
                            O[:, j, :], core.bank(j)[0:TOPC, :], b2[:, e, :], ALU.add).then_inc(
                            core.vector_freed.sem, 1)

            banks = [[product(ROWS, [(GT[:, i, rows_of(t)], O[:, i, :]) for i in range(2)], DIM)]
                     for t in range(TILES)]
            filled, freed = core.bank_filled.span(len(banks)), core.vector_freed.span(len(banks))
            with nc.Block() as block:

                @block.tensor
                def _(pe):
                    for j, products in enumerate(banks):
                        if j >= BANKS:
                            pe.wait_ge(core.vector_freed.sem, freed + j - BANKS + 1)
                        fill(nc, core.bank(j), products).then_inc(core.bank_filled.sem, 1)

                @block.vector
                def _(dve):
                    for j in range(len(banks)):
                        dve.wait_ge(core.bank_filled.sem, filled + j + 1)
                        if j:
                            dve.wait_ge(core.vector_freed.sem, freed + j)
                        nc.vector.tensor_tensor(
                            c.x[:, j, :], c.x[:, j, :], core.bank(j)[0:ROWS, :], ALU.add).then_inc(
                            core.vector_freed.sem, 1)

                @block.sync
                def _(sync):
                    moves = expert_loads(e + 2) if e + 2 < EXP1 else ()
                    for dst, src in moves:
                        sync.dma_start(dst, src).then_inc(core.landed.sem, 16)
                    sync.wait_ge(core.landed.sem, core.landed.up(16 * len(moves)))




def gat_layer(core, c, d, k, inT, chunks, h, masked, out, names, ctx_tag):
    nc = core.nc
    with ExitStack() as ctx:
        sb = Scope(nc, ctx, ctx_tag)
        W = sb("W", [128, chunks, GAT_DIM])
        att = sb("att", [ROWS, 2, GAT_DIM])
        b = sb("b", [ROWS, GAT_DIM])
        with nc.Block() as block:

            @block.sync
            def _(sync):
                moves = [(W[:, :, :], w_view(d[names[0]])), (att[:, 0, :], bcast(d[names[1]])),
                         (att[:, 1, :], bcast(d[names[2]])), (b[:, :], bcast(d[names[3]]))]
                for dst, src in moves:
                    sync.dma_start(dst, src).then_inc(core.landed.sem, 16)
                sync.wait_ge(core.landed.sem, core.landed.up(16 * len(moves)))

        banks = []
        for t in range(TILES):
            for j in range(2):
                banks.append([product(ROWS, [(inT[:, q, rows_of(t)], W[:, q, j * DIM:(j + 1) * DIM])
                                             for q in range(chunks)], DIM)])
        filled, freed = core.bank_filled.span(len(banks)), core.scalar_freed.span(len(banks))
        with nc.Block() as block:

            @block.tensor
            def _(pe):
                for j, products in enumerate(banks):
                    if j >= BANKS:
                        pe.wait_ge(core.scalar_freed.sem, freed + j - BANKS + 1)
                    fill(nc, core.bank(j), products).then_inc(core.bank_filled.sem, 1)

            @block.scalar
            def _(act):
                for j in range(len(banks)):
                    act.wait_ge(core.bank_filled.sem, filled + j + 1)
                    nc.scalar.activation(
                        h[:, j // 2, 2 * (j % 2):2 * (j % 2) + 2, 0:GAT_HID],
                        core.bank(j)[0:ROWS, :].rearrange("p (a n) -> p a n", a=2), ACT.Copy).then_inc(
                        core.scalar_freed.sem, 1)

        gat_heads(core, c, h, att, b, masked, out)


def gat_heads(core, c, h, att, b, masked, out):
    nc = core.nc
    with ExitStack() as ctx:
        sb = Scope(nc, ctx, "gat_")
        a = sb("a", [ROWS, 2, TILES, GAT_HEADS])
        junk = sb("junk", [ROWS, 2, GAT_HID])
        top = sb("top", [ROWS, TILES])
        top2 = sb("top2", [ROWS, TILES])
        z = sb("z", [ROWS, NODES])
        u = sb("u", [ROWS, TILES, NODES])
        mB = sb("mB", [ROWS, NODES])
        r = sb("r", [ROWS, 2])

        def scores(dve):
            start = core.vector_done.count
            for w in range(2):
                for t in range(TILES):
                    for hd in range(GAT_HEADS):
                        last = nc.vector.tensor_tensor_reduce(
                            out=junk[:, hd % 2, :], in0=h[:, t, hd, 0:GAT_HID],
                            in1=att[:, w, hd * GAT_HID:(hd + 1) * GAT_HID], scale=1.0, scalar=0.0,
                            op0=ALU.mult, op1=ALU.add, accum_out=a[:, w, t, hd:hd + 1])
                        last.then_inc(core.vector_done.sem, 1)
                        if core.vector_done.up() > start + 1:
                            dve.wait_ge(core.vector_done.sem, core.vector_done.count - 1)
            dve.wait_ge(core.vector_done.sem, core.vector_done.count)

        with nc.Block() as block:

            @block.vector
            def _(dve):
                scores(dve)


        def spread_banks(col):
            return [[turned(ROWS, ROWS, col(t).to_broadcast([ROWS, ROWS]), c.ident[0:ROWS, 0:ROWS],
                            at=128 * (t - t0)) for t in range(t0, min(t0 + 4, TILES))] for t0 in (0, 4)]

        def nodes_of(j, v):
            n = 4 if j == 0 else TILES - 4
            return v[:, 4 * j * ROWS:(4 * j + n) * ROWS].rearrange("p (t n) -> p t n", n=ROWS), n

        for hd in range(GAT_HEADS):
            banks = spread_banks(lambda t: a[:, 0, t, hd:hd + 1])
            filled, freed = core.bank_filled.span(len(banks)), core.vector_freed.span(len(banks))
            with nc.Block() as block:

                @block.tensor
                def _(pe):
                    for j, products in enumerate(banks):
                        if j >= BANKS:
                            pe.wait_ge(core.vector_freed.sem, freed + j - BANKS + 1)
                        fill(nc, core.bank(j), products).then_inc(core.bank_filled.sem, 1)

                @block.vector
                def _(dve):
                    for j in range(len(banks)):
                        dve.wait_ge(core.bank_filled.sem, filled + j + 1)
                        if j:
                            dve.wait_ge(core.vector_freed.sem, freed + j)
                        nc.vector.tensor_copy(
                            nodes_of(j, mB)[0],
                            core.bank(j)[0:ROWS, :].rearrange("p (t n) -> p t n", n=128)[:, 0:nodes_of(j, mB)[1], 0:ROWS]).then_inc(
                            core.vector_freed.sem, 1)


            def highest(dve):
                for t in range(TILES):
                    nc.vector.tensor_tensor(z[:, :], mB[:, :], masked[:, t, :], ALU.add).then_inc(core.vector_done.sem, 1)
                    dve.wait_ge(core.vector_done.sem, core.vector_done.up())
                    nc.vector.tensor_reduce(top[:, t:t + 1], z[:, :], AX.X, ALU.max).then_inc(core.vector_done.sem, 1)
                    dve.wait_ge(core.vector_done.sem, core.vector_done.up())
                nc.vector.tensor_tensor(top[:, :], top[:, :], a[:, 1, :, hd], ALU.add).then_inc(core.vector_done.sem, 1)
                dve.wait_ge(core.vector_done.sem, core.vector_done.up())
                nc.vector.tensor_scalar(top2[:, :], top[:, :], 0.2, None, ALU.mult).then_inc(core.vector_done.sem, 1)
                dve.wait_ge(core.vector_done.sem, core.vector_done.up())
                nc.vector.tensor_tensor(top[:, :], top[:, :], top2[:, :], ALU.max).then_inc(core.vector_done.sem, 1)
                dve.wait_ge(core.vector_done.sem, core.vector_done.up())

            with nc.Block() as block:

                @block.vector
                def _(dve):
                    highest(dve)

            banks = spread_banks(lambda t: a[:, 1, t, hd:hd + 1]) + spread_banks(lambda t: top[:, t:t + 1])

            def sums(act, j, bank):
                n = nodes_of(j % 2, mB)[1]
                src = bank[0:ROWS, :].rearrange("p (t n) -> p t n", n=128)[:, 0:n, 0:ROWS]
                if j >= 2:
                    return nc.scalar.activation(nodes_of(j - 2, mB)[0], src, ACT.Copy)
                for t in range(TILES):
                    last = nc.scalar.activation(nodes_of(j, u[:, t, :])[0], src, ACT.Identity,
                                                bias=a[:, 0, t, hd:hd + 1])
                return last

            filled, freed = core.bank_filled.span(len(banks)), core.scalar_freed.span(len(banks))
            with nc.Block() as block:

                @block.tensor
                def _(pe):
                    for j, products in enumerate(banks):
                        if j >= BANKS:
                            pe.wait_ge(core.scalar_freed.sem, freed + j - BANKS + 1)
                        fill(nc, core.bank(j), products).then_inc(core.bank_filled.sem, 1)

                @block.scalar
                def _(act):
                    for j in range(len(banks)):
                        act.wait_ge(core.bank_filled.sem, filled + j + 1)
                        sums(act, j, core.bank(j)).then_inc(core.scalar_freed.sem, 1)

            mBB = mB[:, :].unsqueeze(1).to_broadcast([ROWS, TILES, NODES])

            def less_max(dve):
                nc.vector.scalar_tensor_tensor(out=u[:, :, :], in0=u[:, :, :], scalar=0.2, in1=u[:, :, :],
                                                      op0=ALU.mult, op1=ALU.max).then_inc(core.vector_done.sem, 1)
                dve.wait_ge(core.vector_done.sem, core.vector_done.up())
                nc.vector.tensor_tensor(u[:, :, :], u[:, :, :], mBB, ALU.min).then_inc(core.vector_done.sem, 1)
                dve.wait_ge(core.vector_done.sem, core.vector_done.up())
                nc.vector.tensor_tensor(u[:, :, :], u[:, :, :], mBB, ALU.subtract).then_inc(core.vector_done.sem, 1)
                dve.wait_ge(core.vector_done.sem, core.vector_done.up())

            with nc.Block() as block:

                @block.vector
                def _(dve):
                    less_max(dve)

            with nc.Block() as block:

                @block.scalar
                def _(act):
                    nc.scalar.activation(u[:, :, :], u[:, :, :], ACT.Exp).then_inc(core.scalar_done.sem, 1)
                    act.wait_ge(core.scalar_done.sem, core.scalar_done.up())

            with nc.Block() as block:

                @block.vector
                def _(dve):
                    nc.vector.tensor_tensor(
                        u[:, :, :], u[:, :, :], c.CT[:, :, :], ALU.mult).then_inc(core.vector_done.sem, 1)
                    dve.wait_ge(core.vector_done.sem, core.vector_done.up())

            banks = [[product(ROWS, [(u[:, s, rows_of(t)], h[:, s, hd, :]) for s in range(TILES)], GAT_HID + 1)]
                     for t in range(TILES)]

            def combine(dve, t, bank):
                dst = out[:, t, hd * GAT_HID:(hd + 1) * GAT_HID]
                rt = r[:, t % 2:t % 2 + 1]
                nc.vector.tensor_scalar(rt, bank[0:ROWS, GAT_HID:GAT_HID + 1], 1e-16, None, ALU.add).then_inc(core.vector_done.sem, 1)
                dve.wait_ge(core.vector_done.sem, core.vector_done.up())
                nc.vector.reciprocal(rt, rt).then_inc(core.vector_done.sem, 1)
                dve.wait_ge(core.vector_done.sem, core.vector_done.up())
                nc.vector.scalar_tensor_tensor(out=dst, in0=bank[0:ROWS, 0:GAT_HID], scalar=rt,
                                                      in1=b[:, hd * GAT_HID:(hd + 1) * GAT_HID],
                                                      op0=ALU.mult, op1=ALU.add).then_inc(core.vector_done.sem, 1)
                dve.wait_ge(core.vector_done.sem, core.vector_done.up())
                return nc.vector.tensor_scalar(dst, dst, 0.0, None, ALU.max)

            filled, freed = core.bank_filled.span(len(banks)), core.vector_freed.span(len(banks))
            with nc.Block() as block:

                @block.tensor
                def _(pe):
                    for j, products in enumerate(banks):
                        if j >= BANKS:
                            pe.wait_ge(core.vector_freed.sem, freed + j - BANKS + 1)
                        fill(nc, core.bank(j), products).then_inc(core.bank_filled.sem, 1)

                @block.vector
                def _(dve):
                    for j in range(len(banks)):
                        dve.wait_ge(core.bank_filled.sem, filled + j + 1)
                        if j:
                            dve.wait_ge(core.vector_freed.sem, freed + j)
                        combine(dve, j, core.bank(j)).then_inc(core.vector_freed.sem, 1)


def layer2_gnn(core, c, d):
    nc = core.nc
    with ExitStack() as ctx:
        sb = Scope(nc, ctx, "g2_")
        masked = sb("masked", [ROWS, TILES, NODES])
        out = sb("out", [ROWS, TILES, GAT_DIM])
        h = sb("h", [ROWS, TILES, GAT_HEADS, GAT_HID + 1])

        def own_loops(dve):
            for t in range(TILES):
                last = nc.vector.tensor_tensor(c.CT[:, t, rows_of(t)], c.CT[:, t, rows_of(t)],
                                               c.ident[0:ROWS, 0:ROWS], ALU.add)
            last.then_inc(core.vector_done.sem, 1)
            dve.wait_ge(core.vector_done.sem, core.vector_done.up())
            nc.vector.memset(h[:, :, :, GAT_HID:GAT_HID + 1], 1.0).then_inc(core.vector_done.sem, 1)
            dve.wait_ge(core.vector_done.sem, core.vector_done.up())

        with nc.Block() as block:

            @block.vector
            def _(dve):
                own_loops(dve)

        banks, where = [], []
        for t in range(TILES):
            for s0 in (0, 4):
                n = min(4, TILES - s0)
                banks.append([turned(ROWS, ROWS, c.CT[:, s, rows_of(t)], c.ident[0:ROWS, 0:ROWS],
                                     at=128 * (s - s0)) for s in range(s0, s0 + n)])
                where.append((t, s0, n))

        def mask(dve, j, bank):
            t, s0, n = where[j]
            src = bank[0:ROWS, :].rearrange("p (t n) -> p t n", n=128)[:, 0:n, 0:ROWS]
            dst = masked[:, t, s0 * ROWS:(s0 + n) * ROWS].rearrange("p (t n) -> p t n", n=ROWS)
            return nc.vector.tensor_scalar(dst, src, 0.0, -1e30, ALU.is_equal, ALU.mult)

        filled, freed = core.bank_filled.span(len(banks)), core.vector_freed.span(len(banks))
        with nc.Block() as block:

            @block.tensor
            def _(pe):
                for j, products in enumerate(banks):
                    if j >= BANKS:
                        pe.wait_ge(core.vector_freed.sem, freed + j - BANKS + 1)
                    fill(nc, core.bank(j), products).then_inc(core.bank_filled.sem, 1)

            @block.vector
            def _(dve):
                for j in range(len(banks)):
                    dve.wait_ge(core.bank_filled.sem, filled + j + 1)
                    if j:
                        dve.wait_ge(core.vector_freed.sem, freed + j)
                    mask(dve, j, core.bank(j)).then_inc(core.vector_freed.sem, 1)

        norm_phases(core, c, c.x, c.xn, c.xnT)
        n1 = ["L2_gnn_W1", "L2_gnn_att_src1", "L2_gnn_att_dst1", "L2_gnn_b1"]
        n2 = ["L2_gnn_W2", "L2_gnn_att_src2", "L2_gnn_att_dst2", "L2_gnn_b2"]
        gat_layer(core, c, d, 1, c.xnT, CH, h, masked, out, n1, "ga_")
        with ExitStack() as inner:
            outT = Scope(nc, inner, "gb_")("outT", [128, 2 * CH, NODES])
            turn_phase(core, c, out, outT, 2 * CH)
            W = None
            gat_layer_weights(core, c, d, outT, h, n2)
        with ExitStack() as inner:
            sb2 = Scope(nc, inner, "gh_")
            att = sb2("att", [ROWS, 2, GAT_DIM])
            b = sb2("b", [ROWS, GAT_DIM])
            with nc.Block() as block:

                @block.sync
                def _(sync):
                    moves = [(att[:, 0, :], bcast(d[n2[1]])), (att[:, 1, :], bcast(d[n2[2]])),
                             (b[:, :], bcast(d[n2[3]]))]
                    for dst, src in moves:
                        sync.dma_start(dst, src).then_inc(core.landed.sem, 16)
                    sync.wait_ge(core.landed.sem, core.landed.up(16 * len(moves)))

            gat_heads(core, c, h, att, b, masked, out)
        with ExitStack() as inner:
            sb2 = Scope(nc, inner, "gf_")
            outT = sb2("outT", [128, 2 * CH, NODES])
            W = sb2("W", [128, 2 * CH, DIM])
            bf = sb2("bf", [ROWS, DIM])
            u = sb2("u", [ROWS, DIM])
            turn_phase(core, c, out, outT, 2 * CH, loads=[(W[:, :, :], w_view(d["L2_gnn_fcW"])),
                                                         (bf[:, :], bcast(d["L2_gnn_fcb"]))])
            add_to_x = add_biased(core, c, u, bf, None)
            banks = row_products(outT, W, chunks=2 * CH)
            filled, freed = core.bank_filled.span(len(banks)), core.vector_freed.span(len(banks))
            with nc.Block() as block:

                @block.tensor
                def _(pe):
                    for j, products in enumerate(banks):
                        if j >= BANKS:
                            pe.wait_ge(core.vector_freed.sem, freed + j - BANKS + 1)
                        fill(nc, core.bank(j), products).then_inc(core.bank_filled.sem, 1)

                @block.vector
                def _(dve):
                    for j in range(len(banks)):
                        dve.wait_ge(core.bank_filled.sem, filled + j + 1)
                        if j:
                            dve.wait_ge(core.vector_freed.sem, freed + j)
                        add_to_x(dve, j, core.bank(j)).then_inc(core.vector_freed.sem, 1)


def gat_layer_weights(core, c, d, inT, h, names):
    nc = core.nc
    chunks = 2 * CH
    with ExitStack() as ctx:
        W = Scope(nc, ctx, "gw_")("W", [128, chunks, DIM])
        for half in range(2):
            with nc.Block() as block:

                @block.sync
                def _(sync):
                    moves = [(W[:, :, :], w_view(d[names[0]])[:, :, half * DIM:(half + 1) * DIM])]
                    for dst, src in moves:
                        sync.dma_start(dst, src).then_inc(core.landed.sem, 16)
                    sync.wait_ge(core.landed.sem, core.landed.up(16 * len(moves)))

            banks = row_products(inT, W, chunks=chunks)
            filled, freed = core.bank_filled.span(len(banks)), core.scalar_freed.span(len(banks))
            with nc.Block() as block:

                @block.tensor
                def _(pe):
                    for j, products in enumerate(banks):
                        if j >= BANKS:
                            pe.wait_ge(core.scalar_freed.sem, freed + j - BANKS + 1)
                        fill(nc, core.bank(j), products).then_inc(core.bank_filled.sem, 1)

                @block.scalar
                def _(act):
                    for j in range(len(banks)):
                        act.wait_ge(core.bank_filled.sem, filled + j + 1)
                        nc.scalar.activation(
                            h[:, j, 2 * half:2 * half + 2, 0:GAT_HID], core.bank(j)[0:ROWS, :].rearrange("p (a n) -> p a n", a=2), ACT.Copy).then_inc(
                            core.scalar_freed.sem, 1)


def layer2_mix(core, c, d):
    nc = core.nc
    EPS, CLAMP = 1e-8, 50.0
    with ExitStack() as ctx:
        sb = Scope(nc, ctx, "m2_")
        W = {k: sb("W" + k, [128, CH, DIM]) for k in "qkvo"}
        om = {k: sb("om" + k, [128, 128]) for k in "qk"}
        both = sb("both", [128, 128])
        T = {k: sb("T" + k, [128, CH, NODES]) for k in "qk"}
        sq = sb("sq", [128, CH, NODES])
        K = sb("K", [ROWS, TILES, DIM])
        V1 = sb("V1", [ROWS, TILES, PAIRS, 129])
        o_rows = sb("o", [ROWS, TILES, DIM])

        def clear(gp):
            for k in "qk":
                nc.gpsimd.memset(om[k][:, :], 0.0)
            nc.gpsimd.memset(both[:, :], 0.0)
            last = nc.gpsimd.memset(V1[:, :, :, 128:129], 1.0)
            last.then_inc(core.pool_done.sem, 1)
            gp.wait_ge(core.pool_done.sem, core.pool_done.up())
            for i in range(2):
                h = slice(HDIM * i, HDIM * (i + 1))
                last = nc.gpsimd.memset(both[h, h], 1.0)
            last.then_inc(core.pool_done.sem, 1)
            gp.wait_ge(core.pool_done.sem, core.pool_done.up())

        with nc.Block() as block:

            @block.gpsimd
            def _(gp):
                clear(gp)

        loads = [(W[k][:, :, :], w_view(d["L2_mix_W" + k])) for k in "qkvo"]
        for k in "qk":
            for i in range(2):
                h = slice(HDIM * i, HDIM * (i + 1))
                loads.append((om[k][h, h], d["L2_mix_omega_" + k]))
        with nc.Block() as block:

            @block.sync
            def _(sync):
                for dst, src in loads:
                    sync.dma_start(dst, src).then_inc(core.landed.sem, 16)
                sync.wait_ge(core.landed.sem, core.landed.up(16 * len(loads)))

        banks = []
        for k in "qk":
            for m in range(CH):
                banks += halves(128, lambda a, b: [(W[k][:, q, chunk(m)], c.xnT[:, q, a:b]) for q in range(CH)])
        nq = len(banks)
        banks += row_products(c.xnT, W["v"])

        def keep(act, j, bank):
            if j >= nq:
                return nc.scalar.activation(V1[:, j - nq, :, 0:128],
                                            bank[0:ROWS, :].rearrange("p (a n) -> p a n", a=PAIRS), ACT.Copy)
            k, m, (a, b) = "qk"[j // (2 * CH)], j // 2 % CH, HALVES[j % 2]
            return nc.scalar.activation(T[k][:, m, a:b], bank[:, 0:b - a], ACT.Copy, scale=HDIM ** -0.5)

        filled, freed = core.bank_filled.span(len(banks)), core.scalar_freed.span(len(banks))
        with nc.Block() as block:

            @block.tensor
            def _(pe):
                for j, products in enumerate(banks):
                    if j >= BANKS:
                        pe.wait_ge(core.scalar_freed.sem, freed + j - BANKS + 1)
                    fill(nc, core.bank(j), products).then_inc(core.bank_filled.sem, 1)

            @block.scalar
            def _(act):
                for j in range(len(banks)):
                    act.wait_ge(core.bank_filled.sem, filled + j + 1)
                    keep(act, j, core.bank(j)).then_inc(core.scalar_freed.sem, 1)

        for k in "qk":
            with nc.Block() as block:

                @block.vector
                def _(dve):
                    nc.vector.tensor_tensor(
                        sq[:, :, :], T[k][:, :, :], T[k][:, :, :], ALU.mult).then_inc(core.vector_done.sem, 1)
                    dve.wait_ge(core.vector_done.sem, core.vector_done.up())

            banks = []
            for m in range(CH):
                banks += halves(128, lambda a, b: [(om[k][:, :], T[k][:, m, a:b])])
                banks += halves(128, lambda a, b: [(both[:, :], sq[:, m, a:b])])

            def features(dve, j, bank):
                m, part, (a, b) = j // 4, j // 2 % 2, HALVES[j % 2]
                if part == 0:
                    return nc.vector.tensor_scalar(T[k][:, m, a:b], bank[:, 0:b - a], CLAMP, None, ALU.min)
                return nc.vector.tensor_scalar(sq[:, m, a:b], bank[:, 0:b - a], EPS * EPS, None, ALU.max)

            filled, freed = core.bank_filled.span(len(banks)), core.vector_freed.span(len(banks))
            with nc.Block() as block:

                @block.tensor
                def _(pe):
                    for j, products in enumerate(banks):
                        if j >= BANKS:
                            pe.wait_ge(core.vector_freed.sem, freed + j - BANKS + 1)
                        fill(nc, core.bank(j), products).then_inc(core.bank_filled.sem, 1)

                @block.vector
                def _(dve):
                    for j in range(len(banks)):
                        dve.wait_ge(core.bank_filled.sem, filled + j + 1)
                        if j:
                            dve.wait_ge(core.vector_freed.sem, freed + j)
                        features(dve, j, core.bank(j)).then_inc(core.vector_freed.sem, 1)


            def exps(act):
                nc.scalar.activation(sq[:, :, :], sq[:, :, :], ACT.Exp, scale=-0.5)
                nc.scalar.activation(T[k][:, :, :], T[k][:, :, :], ACT.Exp).then_inc(core.scalar_done.sem, 1)
                act.wait_ge(core.scalar_done.sem, core.scalar_done.up())

            with nc.Block() as block:

                @block.scalar
                def _(act):
                    exps(act)

            with nc.Block() as block:

                @block.vector
                def _(dve):
                    nc.vector.scalar_tensor_tensor(
                        out=T[k][:, :, :], in0=sq[:, :, :], scalar=EPS, in1=T[k][:, :, :], op0=ALU.max, op1=ALU.mult).then_inc(core.vector_done.sem, 1)
                    dve.wait_ge(core.vector_done.sem, core.vector_done.up())

        banks = [[turned(ROWS, 128, T["k"][:, m, rows_of(t)], c.ident[:, :], at=128 * m) for m in range(CH)]
                 for t in range(TILES)]
        filled, freed = core.bank_filled.span(len(banks)), core.scalar_freed.span(len(banks))
        with nc.Block() as block:

            @block.tensor
            def _(pe):
                for j, products in enumerate(banks):
                    if j >= BANKS:
                        pe.wait_ge(core.scalar_freed.sem, freed + j - BANKS + 1)
                    fill(nc, core.bank(j), products).then_inc(core.bank_filled.sem, 1)

            @block.scalar
            def _(act):
                for j in range(len(banks)):
                    act.wait_ge(core.bank_filled.sem, filled + j + 1)
                    nc.scalar.activation(
                        K[:, j, :], core.bank(j)[0:ROWS, :], ACT.Copy).then_inc(
                        core.scalar_freed.sem, 1)

        linear_attention(core, c, T["q"], K, V1, o_rows, 0.0, False)
        turn_phase(core, c, o_rows, sq, CH)
        banks = row_products(sq, W["o"])
        filled, freed = core.bank_filled.span(len(banks)), core.vector_freed.span(len(banks))
        with nc.Block() as block:

            @block.tensor
            def _(pe):
                for j, products in enumerate(banks):
                    if j >= BANKS:
                        pe.wait_ge(core.vector_freed.sem, freed + j - BANKS + 1)
                    fill(nc, core.bank(j), products).then_inc(core.bank_filled.sem, 1)

            @block.vector
            def _(dve):
                for j in range(len(banks)):
                    dve.wait_ge(core.bank_filled.sem, filled + j + 1)
                    if j:
                        dve.wait_ge(core.vector_freed.sem, freed + j)
                    nc.vector.tensor_tensor(
                        c.x[:, j, :], c.x[:, j, :], core.bank(j)[0:ROWS, :], ALU.add).then_inc(
                        core.vector_freed.sem, 1)


def layer2_ffn(core, c, d, ctx):
    nc = core.nc
    FT = FF2 // 128
    sorted_x, sorted_y = c.sorted_x, c.sorted_y
    with ExitStack() as local:
        sb = Scope(nc, local, "e2_")
        pos = sb("pos", [ROWS, TILES], I32)
        slot_i = sb("slot_i", [1, SLOTS], I32)
        scattered = local.enter_context(nc.semaphore("tokens_scattered"))
        gathered = local.enter_context(nc.semaphore("results_gathered"))
        norm_phases(core, c, c.x, c.xn, c.xnT)
        with ExitStack() as inner:
            sb2 = Scope(nc, inner, "r2_")
            Wr = sb2("Wr", [128, CH, EXP2 - 1])
            br = sb2("br", [ROWS, EXP2 - 1])
            right = sb2("right", [ROWS, TILES, EXP2 - 1])
            leaf = sb2("leaf", [ROWS, 2, TILES, EXP2])
            rank = sb2("rank", [ROWS, TILES, EXP2])
            count = sb2("count", [ROWS, EXP2])
            used = sb2("used", [ROWS, EXP2])
            ends = sb2("ends", [ROWS, 2, EXP2])
            posf = sb2("posf", [ROWS, TILES])
            slot_n = sb2("slot_n", [1, SLOTS], I32)
            slot_f = sb2("slot_f", [1, SLOTS])
            slot_c = sb2("slot_c", [1, SLOTS, EXP2])
            zero = sb2("zero", [128, DIM])
            with nc.Block() as block:

                @block.gpsimd
                def _(gp):
                    nc.gpsimd.iota(slot_n[:, :], [[1, SLOTS]], base=0, channel_multiplier=0).then_inc(core.pool_done.sem, 1)
                    gp.wait_ge(core.pool_done.sem, core.pool_done.up())
                    nc.gpsimd.memset(zero[:, :], 0.0).then_inc(core.pool_done.sem, 1)
                    gp.wait_ge(core.pool_done.sem, core.pool_done.up())

                @block.sync
                def _(sync):
                    moves = [(Wr[:, :, :], w_view(d["L2_ffn_Wr"])), (br[:, :], bcast(d["L2_ffn_br"]))]
                    for dst, src in moves:
                        sync.dma_start(dst, src).then_inc(core.landed.sem, 16)
                    sync.wait_ge(core.landed.sem, core.landed.up(16 * len(moves)))

            with nc.Block() as block:

                @block.sync
                def _(sync):
                    moves = [(sorted_x[s * SLOT:(s + 1) * SLOT, :], zero[:, :]) for s in range(SLOTS)]
                    for dst, src in moves:
                        sync.dma_start(dst, src).then_inc(core.landed.sem, 16)
                    sync.wait_ge(core.landed.sem, core.landed.up(16 * len(moves)))

            banks = row_products(c.xnT, Wr, cols=EXP2 - 1)
            filled, freed = core.bank_filled.span(len(banks)), core.vector_freed.span(len(banks))
            with nc.Block() as block:

                @block.tensor
                def _(pe):
                    for j, products in enumerate(banks):
                        if j >= BANKS:
                            pe.wait_ge(core.vector_freed.sem, freed + j - BANKS + 1)
                        fill(nc, core.bank(j), products).then_inc(core.bank_filled.sem, 1)

                @block.vector
                def _(dve):
                    for j in range(len(banks)):
                        dve.wait_ge(core.bank_filled.sem, filled + j + 1)
                        if j:
                            dve.wait_ge(core.vector_freed.sem, freed + j)
                        nc.vector.tensor_tensor(right[:, j, :], core.bank(j)[0:ROWS, 0:EXP2 - 1], br[:, :], ALU.add).then_inc(
                            core.vector_freed.sem, 1)


            def descend(dve):
                nc.vector.tensor_scalar(right[:, :, :], right[:, :, :], 0.0, None, ALU.is_gt).then_inc(core.vector_done.sem, 1)
                dve.wait_ge(core.vector_done.sem, core.vector_done.up())
                nc.vector.memset(leaf[:, 0, :, 0:1], 1.0).then_inc(core.vector_done.sem, 1)
                dve.wait_ge(core.vector_done.sem, core.vector_done.up())
                depth = EXP2.bit_length() - 1
                for lv in range(depth):
                    n = 2 ** lv
                    old, new = leaf[:, lv % 2, :, 0:n], leaf[:, (lv + 1) % 2, :, 0:2 * n].rearrange(
                        "p t (n b) -> p t n b", b=2)
                    nc.vector.tensor_tensor(new[:, :, :, 1], old, right[:, :, n - 1:2 * n - 1], ALU.mult).then_inc(core.vector_done.sem, 1)
                    dve.wait_ge(core.vector_done.sem, core.vector_done.up())
                    nc.vector.tensor_tensor(new[:, :, :, 0], old, new[:, :, :, 1], ALU.subtract).then_inc(core.vector_done.sem, 1)
                    dve.wait_ge(core.vector_done.sem, core.vector_done.up())
            with nc.Block() as block:

                @block.vector
                def _(dve):
                    descend(dve)

            oh = leaf[:, (EXP2.bit_length() - 1) % 2, :, :]
            banks = [[product(ROWS, [(c.above[0:ROWS, 0:ROWS], oh[:, t, :])]
                              + [(c.ones[0:ROWS, 0:ROWS], oh[:, s, :]) for s in range(t)], EXP2)]
                     for t in range(TILES)]
            banks.append([product(ROWS, [(c.ones[0:ROWS, 0:ROWS], oh[:, s, :]) for s in range(TILES)], EXP2)])
            filled, freed = core.bank_filled.span(len(banks)), core.vector_freed.span(len(banks))
            with nc.Block() as block:

                @block.tensor
                def _(pe):
                    for j, products in enumerate(banks):
                        if j >= BANKS:
                            pe.wait_ge(core.vector_freed.sem, freed + j - BANKS + 1)
                        fill(nc, core.bank(j), products).then_inc(core.bank_filled.sem, 1)

                @block.vector
                def _(dve):
                    for j in range(len(banks)):
                        dve.wait_ge(core.bank_filled.sem, filled + j + 1)
                        if j:
                            dve.wait_ge(core.vector_freed.sem, freed + j)
                        nc.vector.tensor_copy(
                            rank[:, j, :] if j < TILES else count[:, :], core.bank(j)[0:ROWS, 0:EXP2]).then_inc(
                            core.vector_freed.sem, 1)


            def assign(dve):
                nc.vector.tensor_scalar(used[:, :], count[:, :], 0.0, None, ALU.is_gt).then_inc(core.vector_done.sem, 1)
                dve.wait_ge(core.vector_done.sem, core.vector_done.up())
                for k in range(1, (NODES + SLOT - 1) // SLOT):
                    nc.vector.scalar_tensor_tensor(out=used[:, :], in0=count[:, :], scalar=float(k * SLOT),
                                                          in1=used[:, :], op0=ALU.is_gt, op1=ALU.add).then_inc(core.vector_done.sem, 1)
                    dve.wait_ge(core.vector_done.sem, core.vector_done.up())
                nc.vector.tensor_copy(ends[:, 0, :], used[:, :]).then_inc(core.vector_done.sem, 1)
                dve.wait_ge(core.vector_done.sem, core.vector_done.up())
                now, step = 0, 1
                while step < EXP2:
                    nc.vector.tensor_copy(ends[:, 1 - now, 0:step], ends[:, now, 0:step])
                    nc.vector.tensor_tensor(ends[:, 1 - now, step:EXP2], ends[:, now, step:EXP2],
                                                   ends[:, now, 0:EXP2 - step], ALU.add).then_inc(core.vector_done.sem, 1)
                    dve.wait_ge(core.vector_done.sem, core.vector_done.up())
                    now, step = 1 - now, step * 2
                end = ends[:, now, :]
                start = ends[:, 1 - now, :]
                nc.vector.tensor_tensor(start, end, used[:, :], ALU.subtract).then_inc(core.vector_done.sem, 1)
                dve.wait_ge(core.vector_done.sem, core.vector_done.up())
                nc.vector.tensor_scalar(start, start, float(SLOT), None, ALU.mult).then_inc(core.vector_done.sem, 1)
                dve.wait_ge(core.vector_done.sem, core.vector_done.up())
                nc.vector.tensor_tensor(rank[:, :, :], rank[:, :, :],
                                               start.unsqueeze(1).to_broadcast([ROWS, TILES, EXP2]), ALU.add).then_inc(core.vector_done.sem, 1)
                dve.wait_ge(core.vector_done.sem, core.vector_done.up())
                nc.vector.tensor_tensor(rank[:, :, :], rank[:, :, :], oh, ALU.mult).then_inc(core.vector_done.sem, 1)
                dve.wait_ge(core.vector_done.sem, core.vector_done.up())
                nc.vector.tensor_reduce(posf[:, :], rank[:, :, :], AX.X, ALU.add).then_inc(core.vector_done.sem, 1)
                dve.wait_ge(core.vector_done.sem, core.vector_done.up())
                nc.vector.tensor_copy(pos[:, :], posf[:, :])
                nc.vector.tensor_copy(slot_f[:, :], slot_n[:, :]).then_inc(core.vector_done.sem, 1)
                dve.wait_ge(core.vector_done.sem, core.vector_done.up())
                nc.vector.tensor_tensor(
                    slot_c[:, :, :], end[0:1, :].unsqueeze(1).to_broadcast([1, SLOTS, EXP2]),
                    slot_f[:, :].unsqueeze(2).to_broadcast([1, SLOTS, EXP2]), ALU.is_le).then_inc(core.vector_done.sem, 1)
                dve.wait_ge(core.vector_done.sem, core.vector_done.up())
                nc.vector.tensor_reduce(slot_f[:, :], slot_c[:, :, :], AX.X, ALU.add).then_inc(core.vector_done.sem, 1)
                dve.wait_ge(core.vector_done.sem, core.vector_done.up())
                nc.vector.tensor_scalar(slot_f[:, :], slot_f[:, :], float(EXP2 - 1), None, ALU.min).then_inc(core.vector_done.sem, 1)
                dve.wait_ge(core.vector_done.sem, core.vector_done.up())
                nc.vector.tensor_copy(slot_i[:, :], slot_f[:, :]).then_inc(core.vector_done.sem, 1)
                dve.wait_ge(core.vector_done.sem, core.vector_done.up())

            with nc.Block() as block:

                @block.vector
                def _(dve):
                    assign(dve)


        def scatter(gp):
            for t in range(TILES):
                nc.gpsimd.indirect_dma_start(
                    out=sorted_x[:, :], out_offset=bass.IndirectOffsetOnAxis(ap=pos[:, t:t + 1], axis=0),
                    in_=c.xn[:, t, :], in_offset=None).then_inc(scattered, 16)
            gp.wait_ge(scattered, 16 * TILES)

        with nc.Block() as block:

            @block.gpsimd
            def _(gp):
                scatter(gp)


        with ExitStack() as inner:
            sb2 = Scope(nc, inner, "s2_")
            W1 = sb2("W1", [128, 2, CH, FF2])
            W2 = sb2("W2", [128, FT, DIM])
            b1 = sb2("b1", [128, 2, FT])
            b2 = sb2("b2", [SLOT, 2, DIM])
            xg = sb2("xg", [SLOT, 2, DIM])
            xgT = sb2("xgT", [128, CH, SLOT])
            hT = sb2("hT", [128, FT, SLOT])
            y = sb2("y", [SLOT, 2, DIM])
            sems = {n: inner.enter_context(nc.semaphore("slot_" + n)) for n in
                    ["tokens_landed0", "tokens_landed1", "w1_landed0", "w1_landed1", "w2_landed", "turned", "turns_kept", "hidden", "gelu_done",
                     "summed", "y_ready", "y_stored"]}
            HB = 4
            with nc.Block() as block:

                @block.sync
                def _(sync):
                    with sync.Fori(0, SLOTS // 2) as i:
                        for b in range(2):
                            s = i * 2 + b
                            e = sync.value_load(slot_i[0:1, bass.ds(s, 1)], min_val=0, max_val=EXP2 - 1)
                            sync.wait_ge(sems["y_ready"], i * 2 + b + 1)
                            sync.dma_start(xg[:, b, :], sorted_x[bass.ds(s * SLOT, SLOT), :]).then_inc(
                                sems[f"tokens_landed{b}"], 16)
                            sync.dma_start(b1[:, b, :], d["L2_ffn_b1"][bass.ds(e, 1)].rearrange(
                                "a p f -> (a p) f")).then_inc(sems[f"tokens_landed{b}"], 16)
                            sync.dma_start(b2[:, b, :], d["L2_ffn_b2"][bass.ds(e, 1), :].to_broadcast(
                                [SLOT, DIM])).then_inc(sems[f"tokens_landed{b}"], 16)
                            sync.dma_start(W1[:, b, :, :], d["L2_ffn_W1"][bass.ds(e, 1)].rearrange(
                                "a (c p) n -> p (a c) n", p=128)).then_inc(sems[f"w1_landed{b}"], 16)
                            sync.wait_ge(sems["y_ready"], i * 2 + b + 2)
                            sync.dma_start(W2[:, :, :], d["L2_ffn_W2"][bass.ds(e, 1)].rearrange(
                                "a (f p) n -> p (a f) n", p=128)).then_inc(sems["w2_landed"], 16)

                @block.tensor
                def _(pe):
                    with pe.Fori(0, SLOTS // 2) as i:
                        for b in range(2):
                            pe.wait_ge(sems[f"tokens_landed{b}"], (i + 1) * 48)
                            for k in range(CH):
                                last = nc.tensor.transpose(core.psum[:, 0, chunk(k)], xg[:, b, chunk(k)],
                                                           c.ident[:, :])
                            last.then_inc(sems["turned"], 1)
                            pe.wait_ge(sems["turns_kept"], i * 2 + b + 1)
                            pe.wait_ge(sems[f"w1_landed{b}"], (i + 1) * 16)
                            for f in range(FT):
                                if f >= HB:
                                    pe.wait_ge(sems["gelu_done"], (i * 2 + b) * FT + f - HB + 1)
                                for k in range(CH):
                                    last = nc.tensor.matmul(core.psum[:, 1 + f % HB, 0:SLOT],
                                                            W1[:, b, k, chunk(f)], xgT[:, k, :],
                                                            start=(k == 0), stop=(k == CH - 1))
                                last.then_inc(sems["hidden"], 1)
                            pe.wait_ge(sems["w2_landed"], (i * 2 + b + 1) * 16)
                            pe.wait_ge(sems["y_ready"], i * 2 + b + 1)
                            for f in range(FT):
                                pe.wait_ge(sems["gelu_done"], (i * 2 + b) * FT + f + 1)
                                last = nc.tensor.matmul(core.psum[:, 5 + b, :], hT[:, f, :], W2[:, f, :],
                                                        start=(f == 0), stop=(f == FT - 1))
                            last.then_inc(sems["summed"], 1)

                @block.scalar
                def _(act):
                    with act.Fori(0, SLOTS // 2) as i:
                        for b in range(2):
                            act.wait_ge(sems["turned"], i * 2 + b + 1)
                            nc.scalar.activation(xgT[:, :, :], core.psum[:, 0, :].rearrange(
                                "p (c n) -> p c n", c=CH), ACT.Copy).then_inc(sems["turns_kept"], 1)
                            for f in range(FT):
                                act.wait_ge(sems["hidden"], (i * 2 + b) * FT + f + 1)
                                nc.scalar.activation(hT[:, f, :], core.psum[:, 1 + f % HB, 0:SLOT], ACT.Gelu,
                                                     bias=b1[:, b, f:f + 1]).then_inc(sems["gelu_done"], 1)

                @block.vector
                def _(dve):
                    dve.sem_inc(sems["y_ready"], 2)
                    with dve.Fori(0, SLOTS // 2) as i:
                        for b in range(2):
                            dve.wait_ge(sems["summed"], i * 2 + b + 1)
                            dve.wait_ge(sems["y_stored"], (i * 2 + b) * 16)
                            nc.vector.tensor_tensor(y[:, b, :], core.psum[:, 5 + b, :], b2[:, b, :],
                                                    ALU.add).then_inc(sems["y_ready"], 1)

                @block.gpsimd
                def _(gp):
                    with gp.Fori(0, SLOTS // 2) as i:
                        for b in range(2):
                            s = i * 2 + b
                            gp.wait_ge(sems["y_ready"], i * 2 + b + 3)
                            gp.dma_start(sorted_y[bass.ds(s * SLOT, SLOT), :], y[:, b, :]).then_inc(
                                sems["y_stored"], 16)
                    gp.wait_ge(sems["y_stored"], 16 * SLOTS)

        with ExitStack() as inner:
            yg = Scope(nc, inner, "y2_")("yg", [ROWS, TILES, DIM])

            def gather(gp):
                for t in range(TILES):
                    nc.gpsimd.indirect_dma_start(
                        out=yg[:, t, :], out_offset=None, in_=sorted_y[:, :],
                        in_offset=bass.IndirectOffsetOnAxis(ap=pos[:, t:t + 1], axis=0)).then_inc(gathered, 16)
                gp.wait_ge(gathered, 16 * TILES)

            with nc.Block() as block:

                @block.gpsimd
                def _(gp):
                    gather(gp)

            with nc.Block() as block:

                @block.vector
                def _(dve):
                    nc.vector.tensor_tensor(
                        c.x[:, :, :], c.x[:, :, :], yg[:, :, :], ALU.add).then_inc(core.vector_done.sem, 1)
                    dve.wait_ge(core.vector_done.sem, core.vector_done.up())




def layer3_gnn(core, c, d):
    nc = core.nc
    with ExitStack() as ctx:
        sb = Scope(nc, ctx, "g3_")
        W = sb("W", [128, CH, DIM])
        aggT = sb("aggT", [128, CH, NODES])
        norm_phases(core, c, c.x, c.xn, c.xnT, loads=[(W[:, :, :], w_view(d["L3_gnn_weight"]))])
        banks, where = [], []
        for t in range(TILES):
            for s0 in (0, 4):
                n = min(4, TILES - s0)
                banks.append([turned(ROWS, ROWS, c.AT[:, s, rows_of(t)], c.ident[0:ROWS, 0:ROWS],
                                     at=128 * (s - s0)) for s in range(s0, s0 + n)])
                where.append((t, s0, n))

        def keep_turned(act, j, bank):
            t, s0, n = where[j]
            return nc.scalar.activation(
                c.CT[:, t, s0 * ROWS:(s0 + n) * ROWS].rearrange("p (t n) -> p t n", n=ROWS),
                bank[0:ROWS, :].rearrange("p (t n) -> p t n", n=128)[:, 0:n, 0:ROWS], ACT.Copy)

        filled, freed = core.bank_filled.span(len(banks)), core.scalar_freed.span(len(banks))
        with nc.Block() as block:

            @block.tensor
            def _(pe):
                for j, products in enumerate(banks):
                    if j >= BANKS:
                        pe.wait_ge(core.scalar_freed.sem, freed + j - BANKS + 1)
                    fill(nc, core.bank(j), products).then_inc(core.bank_filled.sem, 1)

            @block.scalar
            def _(act):
                for j in range(len(banks)):
                    act.wait_ge(core.bank_filled.sem, filled + j + 1)
                    keep_turned(act, j, core.bank(j)).then_inc(core.scalar_freed.sem, 1)

        banks = []
        for m in range(CH):
            banks += halves(128, lambda a, b: [(c.xn[:, s, chunk(m)], c.CT[:, s, a:b]) for s in range(TILES)])
        filled, freed = core.bank_filled.span(len(banks)), core.scalar_freed.span(len(banks))
        with nc.Block() as block:

            @block.tensor
            def _(pe):
                for j, products in enumerate(banks):
                    if j >= BANKS:
                        pe.wait_ge(core.scalar_freed.sem, freed + j - BANKS + 1)
                    fill(nc, core.bank(j), products).then_inc(core.bank_filled.sem, 1)

            @block.scalar
            def _(act):
                for j in range(len(banks)):
                    act.wait_ge(core.bank_filled.sem, filled + j + 1)
                    nc.scalar.activation(
                        aggT[:, j // 2, HALVES[j % 2][0]:HALVES[j % 2][1]],
                        core.bank(j)[:, 0:HALVES[j % 2][1] - HALVES[j % 2][0]], ACT.Copy).then_inc(
                        core.scalar_freed.sem, 1)

        banks = row_products(aggT, W)
        filled, freed = core.bank_filled.span(len(banks)), core.vector_freed.span(len(banks))
        with nc.Block() as block:

            @block.tensor
            def _(pe):
                for j, products in enumerate(banks):
                    if j >= BANKS:
                        pe.wait_ge(core.vector_freed.sem, freed + j - BANKS + 1)
                    fill(nc, core.bank(j), products).then_inc(core.bank_filled.sem, 1)

            @block.vector
            def _(dve):
                for j in range(len(banks)):
                    dve.wait_ge(core.bank_filled.sem, filled + j + 1)
                    if j:
                        dve.wait_ge(core.vector_freed.sem, freed + j)
                    nc.vector.tensor_tensor(
                        c.x[:, j, :], c.x[:, j, :], core.bank(j)[0:ROWS, :], ALU.add).then_inc(
                        core.vector_freed.sem, 1)


def layer3_mix(core, c, d):
    nc = core.nc
    EPS = 1e-6
    N = "L3_mix_"
    with ExitStack() as ctx:
        sb = Scope(nc, ctx, "m3_")
        r2 = sb("r2", [ROWS, TILES, DIM])
        xa = sb("xa", [ROWS, TILES, DIM])
        xaT = sb("xaT", [128, CH, NODES])
        with ExitStack() as inner:
            sb2 = Scope(nc, inner, "a3_")
            gain = sb2("gain", [ROWS, DIM])
            shift = sb2("shift", [ROWS, DIM])
            W = {k: sb2("W" + k, [128, CH, DIM]) for k in "qkvo"}
            bT = {k: sb2("bT" + k, [128, CH]) for k in "qk"}
            B = {k: sb2("B" + k, [ROWS, DIM]) for k in "vo"}
            T = {k: sb2("T" + k, [128, CH, NODES]) for k in "qk"}
            R = {k: sb2("R" + k, [ROWS, TILES, DIM]) for k in "qk"}
            V = sb2("V", [ROWS, TILES, DIM])
            part = sb2("part", [128, 2, CH, 2])
            tot = sb2("tot", [128, 2, CH])
            wide = sb2("wide", [128, 2, CH, 2])
            kv = sb2("kv", [128, CH, 128])
            eps_tile = sb2("eps_tile", [128, ROWS])
            flow = sb2("flow", [ROWS, 2, TILES, HEADS])
            keep = sb2("keep", [ROWS, 2, TILES, HEADS])
            norm = sb2("norm", [ROWS, HEADS])

            def clear(gp):
                nc.gpsimd.memset(kv[:, :, :], 0.0)
                nc.gpsimd.memset(wide[:, :, :, :], 0.0)
                nc.gpsimd.memset(eps_tile[:, :], EPS).then_inc(core.pool_done.sem, 1)
                gp.wait_ge(core.pool_done.sem, core.pool_done.up())

            with nc.Block() as block:

                @block.gpsimd
                def _(gp):
                    clear(gp)

                @block.sync
                def _(sync):
                    moves = [(gain[:, :], bcast(d[N + "g1"])), (shift[:, :], bcast(d[N + "be1"]))]
                    for dst, src in moves:
                        sync.dma_start(dst, src).then_inc(core.landed.sem, 16)
                    sync.wait_ge(core.landed.sem, core.landed.up(16 * len(moves)))

            loads = [(W[k][:, :, :], w_view(d[N + "W" + k])) for k in "qkvo"]
            loads += [(bT[k][:, :], d[N + "b" + k]) for k in "qk"]
            loads += [(B[k][:, :], bcast(d[N + "b" + k])) for k in "vo"]
            norm_phases(core, c, c.xn, xa, xaT, loads=loads, gain=gain, shift=shift)
            banks = []
            for k in "qk":
                for m in range(CH):
                    banks += halves(128, lambda a, b: [(W[k][:, q, chunk(m)], xaT[:, q, a:b]) for q in range(CH)])

            def squash(act, j, bank):
                i, m, (a, b) = j // (2 * CH), j // 2 % CH, HALVES[j % 2]
                return nc.scalar.activation(T["qk"[i]][:, m, a:b], bank[:, 0:b - a], ACT.Sigmoid,
                                            bias=bT["qk"[i]][:, m:m + 1], accum_out=part[:, i, m, j % 2:j % 2 + 1])

            filled, freed = core.bank_filled.span(len(banks)), core.scalar_freed.span(len(banks))
            with nc.Block() as block:

                @block.tensor
                def _(pe):
                    for j, products in enumerate(banks):
                        if j >= BANKS:
                            pe.wait_ge(core.scalar_freed.sem, freed + j - BANKS + 1)
                        fill(nc, core.bank(j), products).then_inc(core.bank_filled.sem, 1)

                @block.scalar
                def _(act):
                    for j in range(len(banks)):
                        act.wait_ge(core.bank_filled.sem, filled + j + 1)
                        squash(act, j, core.bank(j)).then_inc(core.scalar_freed.sem, 1)

            banks = row_products(xaT, W["v"])
            filled, freed = core.bank_filled.span(len(banks)), core.vector_freed.span(len(banks))
            with nc.Block() as block:

                @block.tensor
                def _(pe):
                    for j, products in enumerate(banks):
                        if j >= BANKS:
                            pe.wait_ge(core.vector_freed.sem, freed + j - BANKS + 1)
                        fill(nc, core.bank(j), products).then_inc(core.bank_filled.sem, 1)

                @block.vector
                def _(dve):
                    for j in range(len(banks)):
                        dve.wait_ge(core.bank_filled.sem, filled + j + 1)
                        if j:
                            dve.wait_ge(core.vector_freed.sem, freed + j)
                        nc.vector.tensor_tensor(
                            V[:, j, :], core.bank(j)[0:ROWS, :], B["v"][:, :], ALU.add).then_inc(
                            core.vector_freed.sem, 1)

            banks = [[turned(ROWS, 128, T[k][:, m, rows_of(t)], c.ident[:, :], at=128 * m) for m in range(CH)]
                     for k in "qk" for t in range(TILES)]
            filled, freed = core.bank_filled.span(len(banks)), core.scalar_freed.span(len(banks))
            with nc.Block() as block:

                @block.tensor
                def _(pe):
                    for j, products in enumerate(banks):
                        if j >= BANKS:
                            pe.wait_ge(core.scalar_freed.sem, freed + j - BANKS + 1)
                        fill(nc, core.bank(j), products).then_inc(core.bank_filled.sem, 1)

                @block.scalar
                def _(act):
                    for j in range(len(banks)):
                        act.wait_ge(core.bank_filled.sem, filled + j + 1)
                        nc.scalar.activation(
                            R["qk"[j // TILES]][:, j % TILES, :], core.bank(j)[0:ROWS, :], ACT.Copy).then_inc(
                            core.scalar_freed.sem, 1)


            def widen(dve, of):
                for i in range(2):
                    for half in range(2):
                        h = slice(HDIM * half, HDIM * (half + 1))
                        last = nc.vector.tensor_scalar(wide[h, i, :, half], of[h, 1 - i, :], EPS, None, ALU.add)
                last.then_inc(core.vector_done.sem, 1)
                dve.wait_ge(core.vector_done.sem, core.vector_done.up())

            def first(dve):
                nc.vector.tensor_tensor(tot[:, :, :], part[:, :, :, 0], part[:, :, :, 1], ALU.add).then_inc(core.vector_done.sem, 1)
                dve.wait_ge(core.vector_done.sem, core.vector_done.up())
                widen(dve, tot)

            with nc.Block() as block:

                @block.vector
                def _(dve):
                    first(dve)


            def dot_banks():
                return [[product(ROWS, [(eps_tile[:, :], wide[:, i, p, :]),
                                        (T["qk"[i]][:, p, rows_of(t)], wide[:, i, p, :])], 2, at=8 * i + 2 * p)
                         for i in range(2) for p in range(PAIRS)] for t in range(TILES)]

            def inverse(dve, t, bank):
                return nc.vector.reciprocal(flow[:, :, t, :], bank[0:ROWS, 0:16].rearrange("p (i h) -> p i h", i=2))

            banks = dot_banks()
            filled, freed = core.bank_filled.span(len(banks)), core.vector_freed.span(len(banks))
            with nc.Block() as block:

                @block.tensor
                def _(pe):
                    for j, products in enumerate(banks):
                        if j >= BANKS:
                            pe.wait_ge(core.vector_freed.sem, freed + j - BANKS + 1)
                        fill(nc, core.bank(j), products).then_inc(core.bank_filled.sem, 1)

                @block.vector
                def _(dve):
                    for j in range(len(banks)):
                        dve.wait_ge(core.bank_filled.sem, filled + j + 1)
                        if j:
                            dve.wait_ge(core.vector_freed.sem, freed + j)
                        inverse(dve, j, core.bank(j)).then_inc(core.vector_freed.sem, 1)

            banks = [[product(128, [(R["qk"[i]][:, t, chunk(p)], flow[:, i, t, :]) for t in range(TILES)], HEADS,
                              at=8 * p) for p in range(PAIRS)] for i in range(2)]

            def pick(dve, i, bank):
                v = bank[:, 0:32].rearrange("p (a h) -> p a h", a=PAIRS)
                for p in range(PAIRS):
                    for half in range(2):
                        h = slice(HDIM * half, HDIM * (half + 1))
                        last = nc.vector.tensor_copy(tot[h, i, p:p + 1], v[h, p, 2 * p + half:2 * p + half + 1])
                return last

            filled, freed = core.bank_filled.span(len(banks)), core.vector_freed.span(len(banks))
            with nc.Block() as block:

                @block.tensor
                def _(pe):
                    for j, products in enumerate(banks):
                        if j >= BANKS:
                            pe.wait_ge(core.vector_freed.sem, freed + j - BANKS + 1)
                        fill(nc, core.bank(j), products).then_inc(core.bank_filled.sem, 1)

                @block.vector
                def _(dve):
                    for j in range(len(banks)):
                        dve.wait_ge(core.bank_filled.sem, filled + j + 1)
                        if j:
                            dve.wait_ge(core.vector_freed.sem, freed + j)
                        pick(dve, j, core.bank(j)).then_inc(core.vector_freed.sem, 1)

            with nc.Block() as block:

                @block.vector
                def _(dve):
                    widen(dve, tot)

            banks = dot_banks()
            filled, freed = core.bank_filled.span(len(banks)), core.vector_freed.span(len(banks))
            with nc.Block() as block:

                @block.tensor
                def _(pe):
                    for j, products in enumerate(banks):
                        if j >= BANKS:
                            pe.wait_ge(core.vector_freed.sem, freed + j - BANKS + 1)
                        fill(nc, core.bank(j), products).then_inc(core.bank_filled.sem, 1)

                @block.vector
                def _(dve):
                    for j in range(len(banks)):
                        dve.wait_ge(core.bank_filled.sem, filled + j + 1)
                        if j:
                            dve.wait_ge(core.vector_freed.sem, freed + j)
                        nc.vector.tensor_copy(
                            keep[:, :, j, :], core.bank(j)[0:ROWS, 0:16].rearrange("p (i h) -> p i h", i=2)).then_inc(
                            core.vector_freed.sem, 1)

            with nc.Block() as block:

                @block.vector
                def _(dve):
                    nc.vector.tensor_scalar(
                        keep[:, 1, :, :], keep[:, 1, :, :], 1.0, -1.0, ALU.min, ALU.max).then_inc(core.vector_done.sem, 1)
                    dve.wait_ge(core.vector_done.sem, core.vector_done.up())


            def acts(act):
                nc.scalar.activation(keep[:, 0, :, :], keep[:, 0, :, :], ACT.Sigmoid)
                nc.scalar.activation(keep[:, 1, :, :], keep[:, 1, :, :], ACT.Exp).then_inc(core.scalar_done.sem, 1)
                act.wait_ge(core.scalar_done.sem, core.scalar_done.up())

            with nc.Block() as block:

                @block.scalar
                def _(act):
                    acts(act)

            banks = [[product(ROWS, [(c.ones[0:ROWS, 0:ROWS], keep[:, 1, t, :]) for t in range(TILES)], HEADS)]]
            filled, freed = core.bank_filled.span(len(banks)), core.vector_freed.span(len(banks))
            with nc.Block() as block:

                @block.tensor
                def _(pe):
                    for j, products in enumerate(banks):
                        if j >= BANKS:
                            pe.wait_ge(core.vector_freed.sem, freed + j - BANKS + 1)
                        fill(nc, core.bank(j), products).then_inc(core.bank_filled.sem, 1)

                @block.vector
                def _(dve):
                    for j in range(len(banks)):
                        dve.wait_ge(core.bank_filled.sem, filled + j + 1)
                        if j:
                            dve.wait_ge(core.vector_freed.sem, freed + j)
                        nc.vector.reciprocal(norm[:, :], core.bank(j)[0:ROWS, 0:HEADS]).then_inc(
                            core.vector_freed.sem, 1)


            def weigh(dve):
                nc.vector.tensor_scalar(norm[:, :], norm[:, :], float(NODES), None, ALU.mult).then_inc(core.vector_done.sem, 1)
                dve.wait_ge(core.vector_done.sem, core.vector_done.up())
                for t in range(TILES):
                    last = nc.vector.tensor_tensor(keep[:, 1, t, :], keep[:, 1, t, :], norm[:, :], ALU.mult)
                last.then_inc(core.vector_done.sem, 1)
                dve.wait_ge(core.vector_done.sem, core.vector_done.up())
                nc.vector.tensor_tensor(flow[:, 0, :, :], flow[:, 0, :, :], keep[:, 0, :, :], ALU.mult).then_inc(core.vector_done.sem, 1)
                dve.wait_ge(core.vector_done.sem, core.vector_done.up())
                for t in range(TILES):
                    last = nc.vector.tensor_tensor(
                        V[:, t, :].rearrange("p (h e) -> p h e", h=HEADS), V[:, t, :].rearrange("p (h e) -> p h e", h=HEADS),
                        keep[:, 1, t, :].unsqueeze(2).to_broadcast([ROWS, HEADS, HDIM]), ALU.mult)
                last.then_inc(core.vector_done.sem, 1)
                dve.wait_ge(core.vector_done.sem, core.vector_done.up())

            with nc.Block() as block:

                @block.vector
                def _(dve):
                    weigh(dve)

            banks = [[product(128, [(R["k"][:, t, chunk(p)], V[:, t, chunk(p)]) for t in range(TILES)], 128)]
                     for p in range(PAIRS)]

            def blocks(dve, p, bank):
                for half in range(2):
                    h = slice(HDIM * half, HDIM * (half + 1))
                    last = nc.vector.tensor_copy(kv[h, p, h], bank[h, h])
                return last

            filled, freed = core.bank_filled.span(len(banks)), core.vector_freed.span(len(banks))
            with nc.Block() as block:

                @block.tensor
                def _(pe):
                    for j, products in enumerate(banks):
                        if j >= BANKS:
                            pe.wait_ge(core.vector_freed.sem, freed + j - BANKS + 1)
                        fill(nc, core.bank(j), products).then_inc(core.bank_filled.sem, 1)

                @block.vector
                def _(dve):
                    for j in range(len(banks)):
                        dve.wait_ge(core.bank_filled.sem, filled + j + 1)
                        if j:
                            dve.wait_ge(core.vector_freed.sem, freed + j)
                        blocks(dve, j, core.bank(j)).then_inc(core.vector_freed.sem, 1)

            banks = [[product(ROWS, [(T["q"][:, p, rows_of(t)], kv[:, p, :])], 128, at=128 * p)
                      for p in range(PAIRS)] for t in range(TILES)]
            filled, freed = core.bank_filled.span(len(banks)), core.vector_freed.span(len(banks))
            with nc.Block() as block:

                @block.tensor
                def _(pe):
                    for j, products in enumerate(banks):
                        if j >= BANKS:
                            pe.wait_ge(core.vector_freed.sem, freed + j - BANKS + 1)
                        fill(nc, core.bank(j), products).then_inc(core.bank_filled.sem, 1)

                @block.vector
                def _(dve):
                    for j in range(len(banks)):
                        dve.wait_ge(core.bank_filled.sem, filled + j + 1)
                        if j:
                            dve.wait_ge(core.vector_freed.sem, freed + j)
                        nc.vector.tensor_tensor(
                            R["q"][:, j, :].rearrange("p (h e) -> p h e", h=HEADS), core.bank(j)[0:ROWS, :].rearrange("p (h e) -> p h e", h=HEADS),
                            flow[:, 0, j, :].unsqueeze(2).to_broadcast([ROWS, HEADS, HDIM]), ALU.mult).then_inc(
                            core.vector_freed.sem, 1)

            turn_phase(core, c, R["q"], xaT, CH)

            def residual(dve, t, bank):
                nc.vector.tensor_tensor(r2[:, t, :], bank[0:ROWS, :], B["o"][:, :], ALU.add).then_inc(core.vector_done.sem, 1)
                dve.wait_ge(core.vector_done.sem, core.vector_done.up())
                return nc.vector.tensor_tensor(r2[:, t, :], r2[:, t, :], c.xn[:, t, :], ALU.add)

            banks = row_products(xaT, W["o"])
            filled, freed = core.bank_filled.span(len(banks)), core.vector_freed.span(len(banks))
            with nc.Block() as block:

                @block.tensor
                def _(pe):
                    for j, products in enumerate(banks):
                        if j >= BANKS:
                            pe.wait_ge(core.vector_freed.sem, freed + j - BANKS + 1)
                        fill(nc, core.bank(j), products).then_inc(core.bank_filled.sem, 1)

                @block.vector
                def _(dve):
                    for j in range(len(banks)):
                        dve.wait_ge(core.bank_filled.sem, filled + j + 1)
                        if j:
                            dve.wait_ge(core.vector_freed.sem, freed + j)
                        residual(dve, j, core.bank(j)).then_inc(core.vector_freed.sem, 1)

        with ExitStack() as inner:
            sb2 = Scope(nc, inner, "b3_")
            gain = sb2("gain", [ROWS, DIM])
            shift = sb2("shift", [ROWS, DIM])
            W1 = sb2("W1", [128, CH, FF3])
            W2 = sb2("W2", [FF3, DIM])
            b1 = sb2("b1", [FF3, 1])
            b2 = sb2("b2", [ROWS, DIM])
            hT = sb2("hT", [FF3, NODES])
            u = sb2("u", [ROWS, DIM])
            loads = [(gain[:, :], bcast(d[N + "g2"])), (shift[:, :], bcast(d[N + "be2"])),
                     (W1[:, :, :], w_view(d[N + "W1"])), (W2[:, :], d[N + "W2"]),
                     (b1[:, :], d[N + "b1"]), (b2[:, :], bcast(d[N + "b2"]))]
            with nc.Block() as block:

                @block.sync
                def _(sync):
                    for dst, src in loads:
                        sync.dma_start(dst, src).then_inc(core.landed.sem, 16)
                    sync.wait_ge(core.landed.sem, core.landed.up(16 * len(loads)))

            norm_phases(core, c, r2, xa, xaT, gain=gain, shift=shift)
            banks = halves(128, lambda a, b: [(W1[:, k, :], xaT[:, k, a:b]) for k in range(CH)])
            filled, freed = core.bank_filled.span(len(banks)), core.scalar_freed.span(len(banks))
            with nc.Block() as block:

                @block.tensor
                def _(pe):
                    for j, products in enumerate(banks):
                        if j >= BANKS:
                            pe.wait_ge(core.scalar_freed.sem, freed + j - BANKS + 1)
                        fill(nc, core.bank(j), products).then_inc(core.bank_filled.sem, 1)

                @block.scalar
                def _(act):
                    for j in range(len(banks)):
                        act.wait_ge(core.bank_filled.sem, filled + j + 1)
                        nc.scalar.activation(
                            hT[:, HALVES[j][0]:HALVES[j][1]], core.bank(j)[:, 0:HALVES[j][1] - HALVES[j][0]], ACT.Gelu, bias=b1[:, 0:1]).then_inc(
                            core.scalar_freed.sem, 1)

            banks = [[product(ROWS, [(hT[:, rows_of(t)], W2[:, :])], DIM)] for t in range(TILES)]
            add_to_x = add_biased(core, c, u, b2, r2)
            filled, freed = core.bank_filled.span(len(banks)), core.vector_freed.span(len(banks))
            with nc.Block() as block:

                @block.tensor
                def _(pe):
                    for j, products in enumerate(banks):
                        if j >= BANKS:
                            pe.wait_ge(core.vector_freed.sem, freed + j - BANKS + 1)
                        fill(nc, core.bank(j), products).then_inc(core.bank_filled.sem, 1)

                @block.vector
                def _(dve):
                    for j in range(len(banks)):
                        dve.wait_ge(core.bank_filled.sem, filled + j + 1)
                        if j:
                            dve.wait_ge(core.vector_freed.sem, freed + j)
                        add_to_x(dve, j, core.bank(j)).then_inc(core.vector_freed.sem, 1)


def layer3_ffn(core, c, d):
    nc = core.nc
    EPS = 1e-5
    with ExitStack() as ctx:
        sb = Scope(nc, ctx, "f3_")
        up = sb("up", [128, CH, FF3])
        down = sb("down", [FF3, DIM])
        size = sb("size", [128, 2])
        scale = sb("scale", [128, 2])
        t1 = sb("t1", [128, DIM])
        t2 = sb("t2", [128, DIM])
        upq = sb("upq", [128, CH, FF3])
        downq = sb("downq", [FF3, DIM])
        xq = sb("xq", [ROWS, TILES, DIM])
        xqT = sb("xqT", [128, CH, NODES])
        h = sb("h", [ROWS, TILES, FF3])
        hT = sb("hT", [FF3, NODES])
        big = sb("big", [ROWS, TILES])
        inv = sb("inv", [ROWS, TILES])
        out_scale = sb("out_scale", [ROWS, TILES])
        norm_phases(core, c, c.x, c.xn, c.xnT, loads=[(up[:, :, :], w_view(d["L3_ffn_w_up"])),
                                                     (down[:, :], d["L3_ffn_w_down"])])

        def sizes(dve):
            nc.vector.tensor_reduce(size[:, 0:1], up[:, :, :].rearrange("p c n -> p (c n)"), AX.X, ALU.add,
                                    apply_absolute_value=True)
            nc.vector.tensor_reduce(size[:, 1:2], down[:, :], AX.X, ALU.add, apply_absolute_value=True).then_inc(core.vector_done.sem, 1)
            dve.wait_ge(core.vector_done.sem, core.vector_done.up())

        with nc.Block() as block:

            @block.vector
            def _(dve):
                sizes(dve)

        banks = [[product(128, [(c.ones[:, :], size[:, :])], 2)]]
        filled, freed = core.bank_filled.span(len(banks)), core.vector_freed.span(len(banks))
        with nc.Block() as block:

            @block.tensor
            def _(pe):
                for j, products in enumerate(banks):
                    if j >= BANKS:
                        pe.wait_ge(core.vector_freed.sem, freed + j - BANKS + 1)
                    fill(nc, core.bank(j), products).then_inc(core.bank_filled.sem, 1)

            @block.vector
            def _(dve):
                for j in range(len(banks)):
                    dve.wait_ge(core.bank_filled.sem, filled + j + 1)
                    if j:
                        dve.wait_ge(core.vector_freed.sem, freed + j)
                    nc.vector.tensor_scalar(scale[:, :], core.bank(j)[:, 0:2], 1.0 / (DIM * FF3), EPS, ALU.mult, ALU.max).then_inc(
                        core.vector_freed.sem, 1)


        def round_weights(dve):
            for i, (w, q) in enumerate(((up[:, :, :].rearrange("p c n -> p (c n)"),
                                         upq[:, :, :].rearrange("p c n -> p (c n)")), (down[:, :], downq[:, :]))):
                nc.vector.tensor_scalar(t1[:, :], w, 2.0, scale[:, i:i + 1], ALU.mult, ALU.is_gt).then_inc(core.vector_done.sem, 1)
                dve.wait_ge(core.vector_done.sem, core.vector_done.up())
                nc.vector.tensor_scalar(t2[:, :], w, -2.0, scale[:, i:i + 1], ALU.mult, ALU.is_gt).then_inc(core.vector_done.sem, 1)
                dve.wait_ge(core.vector_done.sem, core.vector_done.up())
                nc.vector.tensor_tensor(q, t1[:, :], t2[:, :], ALU.subtract).then_inc(core.vector_done.sem, 1)
                dve.wait_ge(core.vector_done.sem, core.vector_done.up())

        with nc.Block() as block:

            @block.vector
            def _(dve):
                round_weights(dve)


        def quantise(dve, src, dst, width, i):
            nc.vector.tensor_reduce(big[:, :], src, AX.X, ALU.max, apply_absolute_value=True).then_inc(core.vector_done.sem, 1)
            dve.wait_ge(core.vector_done.sem, core.vector_done.up())
            nc.vector.tensor_scalar(big[:, :], big[:, :], EPS, None, ALU.max).then_inc(core.vector_done.sem, 1)
            dve.wait_ge(core.vector_done.sem, core.vector_done.up())
            nc.vector.reciprocal(inv[:, :], big[:, :]).then_inc(core.vector_done.sem, 1)
            dve.wait_ge(core.vector_done.sem, core.vector_done.up())
            nc.vector.tensor_scalar(inv[:, :], inv[:, :], 127.0, None, ALU.mult).then_inc(core.vector_done.sem, 1)
            dve.wait_ge(core.vector_done.sem, core.vector_done.up())
            nc.vector.reciprocal(out_scale[:, :], inv[:, :]).then_inc(core.vector_done.sem, 1)
            dve.wait_ge(core.vector_done.sem, core.vector_done.up())
            nc.vector.tensor_scalar(out_scale[:, :], out_scale[:, :], scale[0:ROWS, i:i + 1], None, ALU.mult).then_inc(core.vector_done.sem, 1)
            dve.wait_ge(core.vector_done.sem, core.vector_done.up())
            for t in range(TILES):
                last = nc.vector.tensor_scalar(dst[:, t, :], src[:, t, :], inv[:, t:t + 1], ROUND, ALU.mult, ALU.add)
            last.then_inc(core.vector_done.sem, 1)
            dve.wait_ge(core.vector_done.sem, core.vector_done.up())
            for t in range(TILES):
                last = nc.vector.tensor_scalar(dst[:, t, :], dst[:, t, :], ROUND, 127.0, ALU.subtract, ALU.min)
            last.then_inc(core.vector_done.sem, 1)
            dve.wait_ge(core.vector_done.sem, core.vector_done.up())
            nc.vector.tensor_scalar(dst, dst, -128.0, None, ALU.max).then_inc(core.vector_done.sem, 1)
            dve.wait_ge(core.vector_done.sem, core.vector_done.up())

        with nc.Block() as block:

            @block.vector
            def _(dve):
                quantise(dve, c.xn[:, :, :], xq[:, :, :], DIM, 0)

        turn_phase(core, c, xq, xqT, CH)
        banks = row_products(xqT, upq, cols=FF3)

        def hidden(dve, t, bank):
            nc.vector.tensor_scalar(h[:, t, :], bank[0:ROWS, 0:FF3], out_scale[:, t:t + 1], 0.0, ALU.mult, ALU.max).then_inc(core.vector_done.sem, 1)
            dve.wait_ge(core.vector_done.sem, core.vector_done.up())
            nc.vector.tensor_scalar(h[:, t, :], h[:, t, :], 127.0, ROUND, ALU.min, ALU.add).then_inc(core.vector_done.sem, 1)
            dve.wait_ge(core.vector_done.sem, core.vector_done.up())
            return nc.vector.tensor_scalar(h[:, t, :], h[:, t, :], ROUND, None, ALU.subtract)

        filled, freed = core.bank_filled.span(len(banks)), core.vector_freed.span(len(banks))
        with nc.Block() as block:

            @block.tensor
            def _(pe):
                for j, products in enumerate(banks):
                    if j >= BANKS:
                        pe.wait_ge(core.vector_freed.sem, freed + j - BANKS + 1)
                    fill(nc, core.bank(j), products).then_inc(core.bank_filled.sem, 1)

            @block.vector
            def _(dve):
                for j in range(len(banks)):
                    dve.wait_ge(core.bank_filled.sem, filled + j + 1)
                    if j:
                        dve.wait_ge(core.vector_freed.sem, freed + j)
                    hidden(dve, j, core.bank(j)).then_inc(core.vector_freed.sem, 1)

        with nc.Block() as block:

            @block.vector
            def _(dve):
                quantise(dve, h[:, :, :], h[:, :, :], FF3, 1)

        banks = [[turned(FF3, ROWS, h[:, t, :], c.ident[0:ROWS, 0:ROWS])] for t in range(TILES)]
        filled, freed = core.bank_filled.span(len(banks)), core.scalar_freed.span(len(banks))
        with nc.Block() as block:

            @block.tensor
            def _(pe):
                for j, products in enumerate(banks):
                    if j >= BANKS:
                        pe.wait_ge(core.scalar_freed.sem, freed + j - BANKS + 1)
                    fill(nc, core.bank(j), products).then_inc(core.bank_filled.sem, 1)

            @block.scalar
            def _(act):
                for j in range(len(banks)):
                    act.wait_ge(core.bank_filled.sem, filled + j + 1)
                    nc.scalar.activation(hT[:, rows_of(j)], core.bank(j)[:, 0:ROWS], ACT.Copy).then_inc(
                        core.scalar_freed.sem, 1)

        banks = [[product(ROWS, [(hT[:, rows_of(t)], downq[:, :])], DIM)] for t in range(TILES)]
        filled, freed = core.bank_filled.span(len(banks)), core.vector_freed.span(len(banks))
        with nc.Block() as block:

            @block.tensor
            def _(pe):
                for j, products in enumerate(banks):
                    if j >= BANKS:
                        pe.wait_ge(core.vector_freed.sem, freed + j - BANKS + 1)
                    fill(nc, core.bank(j), products).then_inc(core.bank_filled.sem, 1)

            @block.vector
            def _(dve):
                for j in range(len(banks)):
                    dve.wait_ge(core.bank_filled.sem, filled + j + 1)
                    if j:
                        dve.wait_ge(core.vector_freed.sem, freed + j)
                    nc.vector.scalar_tensor_tensor(
                        out=c.x[:, j, :], in0=core.bank(j)[0:ROWS, :], scalar=out_scale[:, j:j + 1], in1=c.x[:, j, :],
                        op0=ALU.mult, op1=ALU.add).then_inc(
                        core.vector_freed.sem, 1)


class Shared:
    pass


STAGES = 8


def build(nc, d, out, stages=STAGES, first=1):
    with ExitStack() as ctx:
        core = Core(nc, ctx)
        c = Shared()
        sb = Scope(nc, ctx, "")
        c.x = sb("x_rows", [ROWS, TILES, DIM])
        c.xn = sb("xn_rows", [ROWS, TILES, DIM])
        c.xnT = sb("xn_turned", [128, CH, NODES])
        c.AT = sb("weights_from_to", [ROWS, TILES, NODES])
        c.CT = sb("edges_from_to", [ROWS, TILES, NODES])
        c.ident = sb("ident", [128, 128])
        c.ones = sb("ones", [128, 128])
        c.below = sb("below", [128, 128])
        c.above = sb("above", [128, 128])
        c.sorted_x = nc.dram_tensor("sorted_x", [SLOTS * SLOT, DIM], F32, kind="Internal").ap()
        c.sorted_y = nc.dram_tensor("sorted_y", [SLOTS * SLOT, DIM], F32, kind="Internal").ap()

        def constants(gp):
            nc.gpsimd.memset(c.ones[:, :], 1.0)
            nc.gpsimd.memset(c.ident[:, :], 0.0)
            nc.gpsimd.memset(c.below[:, :], 0.0)
            nc.gpsimd.memset(c.above[:, :], 0.0).then_inc(core.pool_done.sem, 1)
            gp.wait_ge(core.pool_done.sem, core.pool_done.up())
            nc.gpsimd.affine_select(out=c.ident[:, :], in_=c.ident[:, :], compare_op=ALU.not_equal, fill=1.0,
                                    base=0, pattern=[[-1, 128]], channel_multiplier=1)
            nc.gpsimd.affine_select(out=c.below[:, :], in_=c.below[:, :], compare_op=ALU.is_ge, fill=1.0,
                                    base=0, pattern=[[1, 128]], channel_multiplier=-1)
            nc.gpsimd.affine_select(out=c.above[:, :], in_=c.above[:, :], compare_op=ALU.is_ge, fill=1.0,
                                           base=0, pattern=[[-1, 128]], channel_multiplier=1).then_inc(core.pool_done.sem, 1)
            gp.wait_ge(core.pool_done.sem, core.pool_done.up())

        with nc.Block() as block:

            @block.gpsimd
            def _(gp):
                constants(gp)

            @block.sync
            def _(sync):
                moves = [(c.x[:, :, :], d["x"].rearrange("(t p) n -> p t n", p=ROWS))]
                for dst, src in moves:
                    sync.dma_start(dst, src).then_inc(core.landed.sem, 16)
                sync.wait_ge(core.landed.sem, core.landed.up(16 * len(moves)))

        adjacency_phases(core, c, d, ctx)
        if stages >= 1 >= first:
            norm_phases(core, c, c.x, c.xn, c.xnT)
            layer0_gnn(core, c, d)
            layer0_mix(core, c, d)
        if stages >= 2 >= first:
            layer0_ffn(core, c, d)
        if stages >= 3 >= first:
            layer1_gnn(core, c, d)
            layer1_mix(core, c, d)
        if stages >= 4 >= first:
            layer1_ffn(core, c, d)
        if stages >= 5 >= first:
            layer2_gnn(core, c, d)
            layer2_mix(core, c, d)
        if stages >= 6 >= first:
            layer2_ffn(core, c, d, ctx)
        if stages >= 7 >= first:
            layer3_gnn(core, c, d)
            layer3_mix(core, c, d)
        if stages >= 8 >= first:
            layer3_ffn(core, c, d)
        with nc.Block() as block:

            @block.sync
            def _(sync):
                moves = [(out.rearrange("(t p) n -> p t n", p=ROWS), c.x[:, :, :])]
                for dst, src in moves:
                    sync.dma_start(dst, src).then_inc(core.landed.sem, 16)
                sync.wait_ge(core.landed.sem, core.landed.up(16 * len(moves)))


TURNED = ["L0_ffn_w_gate", "L0_ffn_w_up", "L0_ffn_w_down", "L1_mix_Wq", "L1_mix_Wkv", "L2_ffn_Wr",
          "L3_gnn_weight", "L3_ffn_w_up", "L3_ffn_w_down"]
PER_PARTITION = ["L0_gnn_b1", "L3_mix_bq", "L3_mix_bk", "L3_mix_b1"]
NAMES = """x src dst edge_weight node_vec L0_gnn_W0_1 L0_gnn_W1_1 L0_gnn_b1 L0_gnn_W0_2 L0_gnn_W1_2 L0_gnn_b2
L0_mix_Wq L0_mix_bq L0_mix_Wk L0_mix_bk L0_mix_Wv L0_mix_bv L0_mix_Wo L0_mix_bo L0_mix_temperature
L0_ffn_w_gate L0_ffn_w_up L0_ffn_w_down L1_gnn_W L1_gnn_b L1_mix_Wq L1_mix_Wkv L1_ffn_Wg L1_ffn_W1 L1_ffn_b1
L1_ffn_W2 L1_ffn_b2 L2_gnn_W1 L2_gnn_att_src1 L2_gnn_att_dst1 L2_gnn_b1 L2_gnn_W2 L2_gnn_att_src2
L2_gnn_att_dst2 L2_gnn_b2 L2_gnn_fcW L2_gnn_fcb L2_mix_Wq L2_mix_Wk L2_mix_Wv L2_mix_Wo L2_mix_omega_q
L2_mix_omega_k L2_ffn_Wr L2_ffn_br L2_ffn_W1 L2_ffn_b1 L2_ffn_W2 L2_ffn_b2 L3_gnn_weight L3_mix_Wq L3_mix_bq
L3_mix_Wk L3_mix_bk L3_mix_Wv L3_mix_bv L3_mix_Wo L3_mix_bo L3_mix_W1 L3_mix_b1 L3_mix_W2 L3_mix_b2 L3_mix_g1
L3_mix_be1 L3_mix_g2 L3_mix_be2 L3_ffn_w_up L3_ffn_w_down""".split()


def lay_out(inputs):
    arrays = {}
    for name in NAMES:
        a = np.asarray(inputs[name])
        if name in TURNED:
            a = a.T
        if "_att_" in name:
            a = a.reshape(-1)
        if name in PER_PARTITION:
            a = a.reshape(-1, 128).T
        if name == "L1_ffn_b1":
            a = a.reshape(EXP1, FF1 // 128, 128).transpose(2, 0, 1)
        if name == "L2_ffn_b1":
            a = a.reshape(EXP2, FF2 // 128, 128).transpose(0, 2, 1)
        arrays["in_" + name] = np.ascontiguousarray(a)
    return arrays


def kernel(**inputs):
    import concourse.bacc as _bacc
    from concourse.bass_utils import run_bass_kernel_spmd as _run

    nc = _bacc.Bacc("TRN2", target_bir_lowering=False, num_devices=1)
    arrays = lay_out(inputs)
    d = {}
    for name in NAMES:
        a = arrays["in_" + name]
        d[name] = nc.dram_tensor("in_" + name, a.shape, mybir.dt.from_np(a.dtype), kind="ExternalInput").ap()
    out = nc.dram_tensor("out_x", (NODES, DIM), F32, kind="ExternalOutput").ap()
    build(nc, d, out)
    r = _run(nc, [arrays], core_ids=[0])
    return r.results[0]["out_x"]
```

```python
from contextlib import ExitStack

import numpy as np
import concourse.bass as bass
from concourse import mybir

ALU = mybir.AluOpType
ACT = mybir.ActivationFunctionType
AX = mybir.AxisListType
F32 = mybir.dt.float32
F16 = mybir.dt.float16
BF16 = mybir.dt.bfloat16
I32 = mybir.dt.int32
U32 = mybir.dt.uint32

NODES = 625
ROWS = 125
TILES = NODES // ROWS
DIM = 512
CH = DIM // 128
HALVES = [(0, 313), (313, NODES)]
EDGES = 20000
EDGE_TILES = EDGES // ROWS
EDGE_PAIRS = EDGE_TILES // 2
BANKS = 8
BANK = 512
HEADS, HDIM = 8, 64
PAIRS = HEADS // 2

FFN0 = 1408
EXP1, FF1 = 8, 1024
TOP1 = max(NODES * 2 // EXP1, 1)
TOPC = TOP1 // 2
GAT_HEADS, GAT_HID = 4, 256
GAT_DIM = GAT_HEADS * GAT_HID
EXP2, FF2 = 16, 2048
SLOT = 128
SLOTS = EXP2 + NODES // SLOT
FF3 = 128
ROUND = 1.5 * 2 ** 23


class Signal:

    def __init__(self, sem):
        self.sem, self.count = sem, 0

    def up(self, by=1):
        self.count += by
        return self.count

    def span(self, raises):
        self.count += raises
        return self.count - raises


class Core:

    def __init__(self, nc, ctx):
        def signal(name):
            return Signal(ctx.enter_context(nc.semaphore(name)))

        self.nc = nc
        self.psum = ctx.enter_context(nc.psum_tensor("psum", [128, BANKS, BANK], F32))
        self.bank_filled = signal("bank_filled")
        self.vector_freed = signal("vector_freed_bank")
        self.scalar_freed = signal("scalar_freed_bank")
        self.vector_done = signal("vector_done")
        self.scalar_done = signal("scalar_done")
        self.pool_done = signal("pool_done")
        self.landed = signal("loads_landed")
        self.spread = signal("probabilities_spread")
        self.ranked = signal("expert_ranked")

    def bank(self, j):
        return self.psum[:, j % BANKS, :]


def product(rows, terms, cols=None, at=0):
    return ("sum", rows, at, cols, terms)


def turned(rows, cols, source, ident, at=0):
    return ("turn", rows, at, cols, (source, ident))


def fill(nc, bank, products):
    for kind, rows, at, cols, terms in products:
        if kind == "turn":
            last = nc.tensor.transpose(bank[0:rows, at:at + cols], terms[0], terms[1])
            continue
        for n, (lhs, rhs) in enumerate(terms):
            last = nc.tensor.matmul(bank[0:rows, at:at + cols], lhs, rhs,
                                    start=(n == 0), stop=(n == len(terms) - 1))
    return last


def halves(m_rows, terms_of):
    return [[product(m_rows, terms_of(a, b), b - a)] for a, b in HALVES]


def rows_of(t):
    return slice(t * ROWS, (t + 1) * ROWS)


def chunk(c):
    return slice(c * 128, (c + 1) * 128)


class Scope:

    made = 0

    def __init__(self, nc, ctx, tag):
        Scope.made += 1
        self.nc, self.ctx, self.tag = nc, ctx, f"{tag}{Scope.made}_"

    def __call__(self, name, shape, dt=F32):
        return self.ctx.enter_context(self.nc.sbuf_tensor(self.tag + name, shape, dt))


def norm_phases(core, c, src, xn, xnT, loads=(), eps=1e-5, gain=None, shift=None):
    nc = core.nc
    with ExitStack() as ctx:
        sb = Scope(nc, ctx, "norm_")
        stats = sb("stats", [ROWS, TILES, 6])
        mv = sb("mv", [ROWS, TILES, 2])
        ve = sb("ve", [ROWS, TILES])
        root = sb("root", [ROWS, TILES])
        y = sb("y", [ROWS, TILES])
        q = sb("q", [ROWS, TILES])

        def moments(dve):
            for t in range(TILES):
                last = nc.vector.bn_stats(stats[:, t, :], src[:, t, :])
            last.then_inc(core.vector_done.sem, 1)
            dve.wait_ge(core.vector_done.sem, core.vector_done.up())
            for t in range(TILES):
                last = nc.vector.bn_aggr(mv[:, t, :], stats[:, t, :])
            last.then_inc(core.vector_done.sem, 1)
            dve.wait_ge(core.vector_done.sem, core.vector_done.up())
            nc.vector.tensor_scalar(ve[:, :], mv[:, :, 1], eps, None, ALU.add).then_inc(core.vector_done.sem, 1)
            dve.wait_ge(core.vector_done.sem, core.vector_done.up())

        with nc.Block() as block:

            @block.vector
            def _(dve):
                moments(dve)

            @block.sync
            def _(sync):
                for dst, src in loads:
                    sync.dma_start(dst, src).then_inc(core.landed.sem, 16)
                if gain is not None:
                    sync.wait_ge(core.landed.sem, core.landed.count + 16 * len(loads))

        with nc.Block() as block:

            @block.scalar
            def _(act):
                nc.scalar.activation(root[:, :], ve[:, :], ACT.Sqrt).then_inc(core.scalar_done.sem, 1)
                act.wait_ge(core.scalar_done.sem, core.scalar_done.up())


        def apply(dve):
            nc.vector.reciprocal(y[:, :], root[:, :]).then_inc(core.vector_done.sem, 1)
            dve.wait_ge(core.vector_done.sem, core.vector_done.up())
            nc.vector.tensor_tensor(q[:, :], y[:, :], y[:, :], ALU.mult).then_inc(core.vector_done.sem, 1)
            dve.wait_ge(core.vector_done.sem, core.vector_done.up())
            nc.vector.tensor_tensor(q[:, :], q[:, :], ve[:, :], ALU.mult).then_inc(core.vector_done.sem, 1)
            dve.wait_ge(core.vector_done.sem, core.vector_done.up())
            nc.vector.tensor_scalar(q[:, :], q[:, :], -0.5, 1.5, ALU.mult, ALU.add).then_inc(core.vector_done.sem, 1)
            dve.wait_ge(core.vector_done.sem, core.vector_done.up())
            nc.vector.tensor_tensor(y[:, :], y[:, :], q[:, :], ALU.mult).then_inc(core.vector_done.sem, 1)
            dve.wait_ge(core.vector_done.sem, core.vector_done.up())
            for t in range(TILES):
                last = nc.vector.tensor_scalar(xn[:, t, :], src[:, t, :], mv[:, t, 0:1], y[:, t:t + 1],
                                               ALU.subtract, ALU.mult)
            last.then_inc(core.vector_done.sem, 1)
            dve.wait_ge(core.vector_done.sem, core.vector_done.up())
            if gain is not None:
                for t in range(TILES):
                    last = nc.vector.tensor_tensor(xn[:, t, :], xn[:, t, :], gain[:, :], ALU.mult)
                last.then_inc(core.vector_done.sem, 1)
                dve.wait_ge(core.vector_done.sem, core.vector_done.up())
                for t in range(TILES):
                    last = nc.vector.tensor_tensor(xn[:, t, :], xn[:, t, :], shift[:, :], ALU.add)
                last.then_inc(core.vector_done.sem, 1)
                dve.wait_ge(core.vector_done.sem, core.vector_done.up())

        with nc.Block() as block:

            @block.vector
            def _(dve):
                apply(dve)

    turn_phase(core, c, xn, xnT, CH, pending=len(loads))


def turn_phase(core, c, rows, out, chunks, loads=(), pending=0):
    nc = core.nc
    banks, where = [], []
    for t in range(TILES):
        for m in range(0, chunks, 4):
            k = min(4, chunks - m)
            banks.append([turned(128, ROWS, rows[:, t, chunk(m + i)], c.ident[0:ROWS, 0:ROWS], at=128 * i)
                          for i in range(k)])
            where.append((out[:, m:m + k, rows_of(t)], k))
    odd = len(banks) // 2
    filled, freed_v, freed_s = (core.bank_filled.span(len(banks)), core.vector_freed.span(len(banks) - odd),
                                core.scalar_freed.span(odd))
    with nc.Block() as block:

        @block.tensor
        def _(pe):
            for j, products in enumerate(banks):
                if j >= BANKS and j % 2 == 0:
                    pe.wait_ge(core.vector_freed.sem, freed_v + (j - BANKS) // 2 + 1)
                if j >= BANKS and j % 2 == 1:
                    pe.wait_ge(core.scalar_freed.sem, freed_s + (j - BANKS) // 2 + 1)
                fill(nc, core.bank(j), products).then_inc(core.bank_filled.sem, 1)

        @block.vector
        def _(dve):
            for j in range(0, len(banks), 2):
                dst, k = where[j]
                dve.wait_ge(core.bank_filled.sem, filled + j + 1)
                nc.vector.tensor_copy(dst, core.bank(j).rearrange("p (c n) -> p c n", c=4)[:, 0:k, 0:ROWS]).then_inc(
                    core.vector_freed.sem, 1)

        @block.scalar
        def _(act):
            for j in range(1, len(banks), 2):
                dst, k = where[j]
                act.wait_ge(core.bank_filled.sem, filled + j + 1)
                nc.scalar.activation(dst, core.bank(j).rearrange("p (c n) -> p c n", c=4)[:, 0:k, 0:ROWS],
                                     ACT.Copy).then_inc(core.scalar_freed.sem, 1)

        @block.sync
        def _(sync):
            for dst, src in loads:
                sync.dma_start(dst, src).then_inc(core.landed.sem, 16)
            if len(loads) + pending > 0:
                sync.wait_ge(core.landed.sem, core.landed.up(16 * (len(loads) + pending)))


def row_products(xT, W, cols=DIM, chunks=CH):
    return [[product(ROWS, [(xT[:, k, rows_of(t)], W[:, k, :]) for k in range(chunks)], cols)]
            for t in range(TILES)]


def w_view(w):
    return w.rearrange("(c p) n -> p c n", p=128)


def bcast(v, parts=ROWS):
    return v.rearrange("(a n) -> a n", a=1).to_broadcast([parts, v.shape[0]])




def adjacency_phases(core, c, d, ctx):
    nc = core.nc
    with ExitStack() as local:
        sb = Scope(nc, local, "adj_")
        raw = sb("raw", [EDGE_PAIRS, 2, 2, ROWS], I32)
        rows = sb("rows", [EDGE_PAIRS, 3, 2, ROWS])
        least = sb("least", [EDGE_PAIRS, 2])
        least_row = sb("least_row", [1, 2, EDGE_PAIRS])
        inside = sb("inside", [1, TILES, EDGE_PAIRS])
        after = sb("after", [1, EDGE_PAIRS])
        scratch = sb("scratch", [1, 2, TILES, EDGE_PAIRS])
        span = sb("span", [1, 2, TILES])
        span_i = sb("span_i", [1, 2, TILES], I32)
        cols = sb("cols", [ROWS, 3, EDGE_TILES])
        w = sb("w", [ROWS, 3, EDGE_TILES])
        piece = sb("piece", [ROWS, EDGE_TILES], BF16)
        node_i = sb("node_i", [ROWS, NODES], I32)
        node = sb("node", [ROWS, NODES], F16)
        oh_src = sb("oh_src", [ROWS, 2, NODES], BF16)
        oh_dst = sb("oh_dst", [ROWS, 2, 4, ROWS], BF16)
        zero = sb("zero", [ROWS, BANK], BF16)
        clear = sb("clear", [128, DIM])

        def edge_rows(v):
            return v.rearrange("(r j p) -> r j p", j=2, p=ROWS)

        with nc.Block() as block:

            @block.gpsimd
            def _(gp):
                nc.gpsimd.iota(node_i[:, :], [[1, NODES]], base=0, channel_multiplier=0)
                nc.gpsimd.memset(zero[:, :], 0.0)
                nc.gpsimd.memset(clear[:, :], 0.0)

            @block.sync
            def _(sync):
                moves = [(raw[:, 0, :, :], edge_rows(d["src"])), (raw[:, 1, :, :], edge_rows(d["dst"])),
                         (rows[:, 2, :, :], edge_rows(d["edge_weight"]))]
                for dst, src in moves:
                    sync.dma_start(dst, src).then_inc(core.landed.sem, 16)
                sync.wait_ge(core.landed.sem, core.landed.up(16 * len(moves)))

        with nc.Block() as block:

            @block.vector
            def _(dve):
                nc.vector.tensor_copy(node[:, :], node_i[:, :])
                nc.vector.tensor_copy(rows[:, 0:2, :, :].rearrange("p a j n -> p (a j n)"),
                                      raw[:, :, :, :].rearrange("p a j n -> p (a j n)")).then_inc(
                    core.vector_done.sem, 1)
                dve.wait_ge(core.vector_done.sem, core.vector_done.up())
                pair = rows[:, 1, :, :].rearrange("p j n -> p (j n)")
                nc.vector.tensor_reduce(least[:, 0:1], pair, AX.X, ALU.min)
                nc.vector.tensor_reduce(least[:, 1:2], pair, AX.X, ALU.max)

        banks = [[turned(ROWS, EDGE_PAIRS, rows[:, a, j, :], c.ident[0:EDGE_PAIRS, 0:EDGE_PAIRS],
                         at=j * EDGE_PAIRS) for j in range(2)] for a in range(3)]
        banks.append([turned(1, EDGE_PAIRS, least[:, i:i + 1], c.ident[0:EDGE_PAIRS, 0:EDGE_PAIRS],
                             at=i * EDGE_PAIRS) for i in range(2)])
        filled, freed = core.bank_filled.span(len(banks)), core.vector_freed.span(len(banks))
        with nc.Block() as block:

            @block.tensor
            def _(pe):
                for j, products in enumerate(banks):
                    fill(nc, core.bank(j), products).then_inc(core.bank_filled.sem, 1)

            @block.vector
            def _(dve):
                for a in range(3):
                    dve.wait_ge(core.bank_filled.sem, filled + a + 1)
                    nc.vector.tensor_copy(cols[:, a, :].rearrange("p (r j) -> p j r", j=2),
                                          core.bank(a)[0:ROWS, 0:EDGE_TILES].rearrange("p (j r) -> p j r", j=2)
                                          ).then_inc(core.vector_freed.sem, 1)
                dve.wait_ge(core.bank_filled.sem, filled + 4)
                nc.vector.tensor_copy(least_row[:, :, :],
                                      core.bank(3)[0:1, 0:EDGE_TILES].rearrange("p (i r) -> p i r", i=2)
                                      ).then_inc(core.vector_freed.sem, 1)
                dve.wait_ge(core.vector_freed.sem, freed + 4)
                nc.vector.tensor_scalar(after[:, :], node[0:1, 0:EDGE_PAIRS], -1.0, float(EDGE_PAIRS),
                                        ALU.mult, ALU.add)
                for k in range(TILES):
                    last = nc.vector.tensor_scalar(inside[:, k, :], least_row[:, 0, :], float((k + 1) * ROWS), None,
                                                   ALU.is_lt)
                last.then_inc(core.vector_done.sem, 1)
                dve.wait_ge(core.vector_done.sem, core.vector_done.up())
                for k in range(TILES):
                    last = nc.vector.scalar_tensor_tensor(out=inside[:, k, :], in0=least_row[:, 1, :],
                                                          scalar=float(k * ROWS), in1=inside[:, k, :],
                                                          op0=ALU.is_ge, op1=ALU.mult)
                last.then_inc(core.vector_done.sem, 1)
                dve.wait_ge(core.vector_done.sem, core.vector_done.up())
                nc.vector.tensor_tensor(scratch[:, 0, :, :], inside[:, :, :],
                                        after[:, :].unsqueeze(1).to_broadcast([1, TILES, EDGE_PAIRS]), ALU.mult)
                nc.vector.scalar_tensor_tensor(
                    out=scratch[:, 1, :, :], in0=node[0:1, 0:EDGE_PAIRS].unsqueeze(1).to_broadcast(
                        [1, TILES, EDGE_PAIRS]), scalar=1.0, in1=inside[:, :, :], op0=ALU.add,
                    op1=ALU.mult).then_inc(core.vector_done.sem, 1)
                dve.wait_ge(core.vector_done.sem, core.vector_done.up())
                nc.vector.tensor_reduce(span[:, :, :], scratch[:, :, :, :], AX.X, ALU.max).then_inc(
                    core.vector_done.sem, 1)
                dve.wait_ge(core.vector_done.sem, core.vector_done.up())
                nc.vector.tensor_scalar(span[:, 0, :], span[:, 0, :], -1.0, float(EDGE_PAIRS),
                                        ALU.mult, ALU.add).then_inc(core.vector_done.sem, 1)
                dve.wait_ge(core.vector_done.sem, core.vector_done.up())
                nc.vector.tensor_scalar(span[:, 0, :], span[:, 0, :], float(EDGE_PAIRS - 1), None,
                                        ALU.min).then_inc(core.vector_done.sem, 1)
                dve.wait_ge(core.vector_done.sem, core.vector_done.up())
                nc.vector.scalar_tensor_tensor(out=span[:, 1, :], in0=span[:, 0, :], scalar=1.0, in1=span[:, 1, :],
                                               op0=ALU.add, op1=ALU.max).then_inc(core.vector_done.sem, 1)
                dve.wait_ge(core.vector_done.sem, core.vector_done.up())
                nc.vector.tensor_tensor(span[:, 1, :], span[:, 1, :], span[:, 0, :], ALU.subtract).then_inc(
                    core.vector_done.sem, 1)
                dve.wait_ge(core.vector_done.sem, core.vector_done.up())
                nc.vector.tensor_copy(span_i[:, :, :], span[:, :, :])
                nc.vector.tensor_copy(piece[:, :], cols[:, 2, :]).then_inc(core.vector_done.sem, 1)
                dve.wait_ge(core.vector_done.sem, core.vector_done.up())
                nc.vector.tensor_copy(w[:, 0, :], piece[:, :]).then_inc(core.vector_done.sem, 1)
                dve.wait_ge(core.vector_done.sem, core.vector_done.up())
                nc.vector.tensor_tensor(w[:, 2, :], cols[:, 2, :], w[:, 0, :], ALU.subtract).then_inc(
                    core.vector_done.sem, 1)
                dve.wait_ge(core.vector_done.sem, core.vector_done.up())
                nc.vector.tensor_copy(piece[:, :], w[:, 2, :]).then_inc(core.vector_done.sem, 1)
                dve.wait_ge(core.vector_done.sem, core.vector_done.up())
                nc.vector.tensor_copy(w[:, 1, :], piece[:, :]).then_inc(core.vector_done.sem, 1)
                dve.wait_ge(core.vector_done.sem, core.vector_done.up())
                nc.vector.tensor_tensor(w[:, 2, :], w[:, 2, :], w[:, 1, :], ALU.subtract)

        made = [local.enter_context(nc.semaphore(f"one_hots_made{k}")) for k in range(TILES)]
        used = [local.enter_context(nc.semaphore(f"one_hots_used{k}")) for k in range(TILES)]
        summed = local.enter_context(nc.semaphore("window_summed"))
        taken = local.enter_context(nc.semaphore("window_taken"))
        with nc.Block() as block:

            @block.vector
            def _(dve):
                for k in range(TILES):
                    first = dve.value_load(span_i[0:1, 0, k:k + 1], min_val=0, max_val=EDGE_PAIRS - 1)
                    pairs = dve.value_load(span_i[0:1, 1, k:k + 1], min_val=1, max_val=EDGE_PAIRS)
                    with dve.Fori(0, pairs) as i:
                        for b in range(2):
                            t = nc.s_assert_within((first + i) * 2 + b, 0, EDGE_TILES - 1,
                                                   skip_runtime_bounds_check_because="first + pairs is at most EDGE_PAIRS")
                            dve.wait_ge(used[k], i * 2 + (b + 1))
                            nc.vector.tensor_scalar(oh_src[:, b, :], node[:, :], cols[:, 0, bass.ds(t, 1)],
                                                    None, ALU.is_equal)
                            nc.vector.tensor_scalar(oh_dst[:, b, 0, :], node[:, rows_of(k)],
                                                    cols[:, 1, bass.ds(t, 1)], None, ALU.is_equal)
                            for q in range(3):
                                last = nc.vector.tensor_scalar(
                                    oh_dst[:, b, 1 + q, :], node[:, rows_of(k)], cols[:, 1, bass.ds(t, 1)],
                                    w[:, q, bass.ds(t, 1)], ALU.is_equal, ALU.mult)
                            last.then_inc(made[k], 1)

            @block.tensor
            def _(pe):
                for k in range(TILES):
                    pairs = pe.value_load(span_i[0:1, 1, k:k + 1], min_val=1, max_val=EDGE_PAIRS)
                    if k >= 2:
                        pe.wait_ge(taken, k - 1)
                    for j in range(3):
                        last = nc.tensor.matmul(core.psum[0:ROWS, 3 * (k % 2) + j, :], zero[:, 0:ROWS], zero[:, :],
                                                start=True, stop=False, skip_group_check=True)
                    last.then_inc(used[k], 2)
                    with pe.Fori(0, pairs) as i:
                        for b in range(2):
                            pe.wait_ge(made[k], i * 2 + (b + 1))
                            for s in range(TILES):
                                bank = core.psum[0:ROWS, 3 * (k % 2) + s // 2, :]
                                at = s % 2 * 256
                                nc.tensor.matmul(bank[:, at:at + 2 * ROWS], oh_src[:, b, rows_of(s)],
                                                 oh_dst[:, b, 0:2, :].rearrange("p q n -> p (q n)"),
                                                 start=False, stop=False, skip_group_check=True)
                                for q in range(2):
                                    last = nc.tensor.matmul(bank[:, at + ROWS:at + 2 * ROWS],
                                                            oh_src[:, b, rows_of(s)], oh_dst[:, b, 2 + q, :],
                                                            start=False, stop=False, skip_group_check=True)
                            last.then_inc(used[k], 1)
                    nc.tensor.matmul(core.psum[0:ROWS, 6, :], zero[:, 0:ROWS], zero[:, :],
                                     start=True, stop=True).then_inc(summed, 1)

            @block.sync
            def _(sync):
                for slots in (c.sorted_x, c.sorted_y):
                    for k in range(SLOTS):
                        sync.dma_start(slots[k * SLOT:(k + 1) * SLOT, :], clear[:, :]).then_inc(core.landed.sem, 16)
                sync.wait_ge(core.landed.sem, core.landed.up(2 * 16 * SLOTS))

            @block.scalar
            def _(act):
                for k in range(TILES):
                    act.wait_ge(summed, k + 1)
                    blocks = core.psum[0:ROWS, 3 * (k % 2):3 * (k % 2) + 3, :].rearrange(
                        "p b (h n) -> p (b h) n", h=2)
                    nc.scalar.activation(c.CT[:, :, rows_of(k)], blocks[:, 0:TILES, 0:ROWS], ACT.Copy)
                    nc.scalar.activation(c.AT[:, :, rows_of(k)], blocks[:, 0:TILES, ROWS:2 * ROWS],
                                         ACT.Copy).then_inc(taken, 1)




def layer0_gnn(core, c, d):
    nc = core.nc
    with ExitStack() as ctx:
        sb = Scope(nc, ctx, "g0_")
        W = [sb(f"W{k}", [128, CH, DIM]) for k in range(4)]
        diag = sb("diag", [128, NODES])
        b1 = sb("b1", [128, CH])
        b2 = sb("b2", [ROWS, DIM])
        scaled = sb("scaled", [128, CH, NODES])
        hw = sb("hw", [ROWS, TILES, DIM])
        h1T = sb("h1T", [128, CH, NODES])
        u = sb("u", [ROWS, DIM])
        names = ["W0_1", "W1_1", "W0_2", "W1_2"]
        loads = [(W[k][:, :, :], w_view(d["L0_gnn_" + names[k]])) for k in range(4)]
        loads += [(diag[:, :], bcast(d["node_vec"], 128)), (b1[:, :], d["L0_gnn_b1"]),
                  (b2[:, :], bcast(d["L0_gnn_b2"]))]
        norm_phases(core, c, c.x, c.xn, c.xnT, loads=loads)

        def scale_nodes(srcT):
            def f(dve):
                for k in range(CH):
                    last = nc.vector.tensor_tensor(scaled[:, k, :], srcT[:, k, :], diag[:, :], ALU.mult)
                last.then_inc(core.vector_done.sem, 1)
                dve.wait_ge(core.vector_done.sem, core.vector_done.up())
            return f

        with nc.Block() as block:

            @block.vector
            def _(dve):
                scale_nodes(c.xnT)(dve)


        def keep_rows(act, j, bank):
            return nc.scalar.activation(hw[:, j, :], bank[0:ROWS, :], ACT.Copy)

        banks = row_products(c.xnT, W[1])
        filled, freed = core.bank_filled.span(len(banks)), core.scalar_freed.span(len(banks))
        with nc.Block() as block:

            @block.tensor
            def _(pe):
                for j, products in enumerate(banks):
                    if j >= BANKS:
                        pe.wait_ge(core.scalar_freed.sem, freed + j - BANKS + 1)
                    fill(nc, core.bank(j), products).then_inc(core.bank_filled.sem, 1)

            @block.scalar
            def _(act):
                for j in range(len(banks)):
                    act.wait_ge(core.bank_filled.sem, filled + j + 1)
                    keep_rows(act, j, core.bank(j)).then_inc(core.scalar_freed.sem, 1)

        banks = []
        for m in range(CH):
            banks += halves(128, lambda a, b: [(W[0][:, k, chunk(m)], scaled[:, k, a:b]) for k in range(CH)]
                            + [(hw[:, s, chunk(m)], c.AT[:, s, a:b]) for s in range(TILES)])

        def relu_h1(act, j, bank):
            m, (a, b) = j // 2, HALVES[j % 2]
            return nc.scalar.activation(h1T[:, m, a:b], bank[:, 0:b - a], ACT.Relu, bias=b1[:, m:m + 1])

        filled, freed = core.bank_filled.span(len(banks)), core.scalar_freed.span(len(banks))
        with nc.Block() as block:

            @block.tensor
            def _(pe):
                for j, products in enumerate(banks):
                    if j >= BANKS:
                        pe.wait_ge(core.scalar_freed.sem, freed + j - BANKS + 1)
                    fill(nc, core.bank(j), products).then_inc(core.bank_filled.sem, 1)

            @block.scalar
            def _(act):
                for j in range(len(banks)):
                    act.wait_ge(core.bank_filled.sem, filled + j + 1)
                    relu_h1(act, j, core.bank(j)).then_inc(core.scalar_freed.sem, 1)

        with nc.Block() as block:

            @block.vector
            def _(dve):
                scale_nodes(h1T)(dve)

        banks = row_products(h1T, W[3])
        filled, freed = core.bank_filled.span(len(banks)), core.scalar_freed.span(len(banks))
        with nc.Block() as block:

            @block.tensor
            def _(pe):
                for j, products in enumerate(banks):
                    if j >= BANKS:
                        pe.wait_ge(core.scalar_freed.sem, freed + j - BANKS + 1)
                    fill(nc, core.bank(j), products).then_inc(core.bank_filled.sem, 1)

            @block.scalar
            def _(act):
                for j in range(len(banks)):
                    act.wait_ge(core.bank_filled.sem, filled + j + 1)
                    keep_rows(act, j, core.bank(j)).then_inc(core.scalar_freed.sem, 1)

        banks = [[product(ROWS, [(scaled[:, k, rows_of(t)], W[2][:, k, :]) for k in range(CH)]
                          + [(c.AT[:, s, rows_of(t)], hw[:, s, :]) for s in range(TILES)], DIM)]
                 for t in range(TILES)]

        def finish(dve, t, bank):
            nc.vector.tensor_tensor(u[:, :], bank[0:ROWS, :], b2[:, :], ALU.add).then_inc(core.vector_done.sem, 1)
            dve.wait_ge(core.vector_done.sem, core.vector_done.up())
            nc.vector.scalar_tensor_tensor(out=u[:, :], in0=u[:, :], scalar=0.0, in1=c.xn[:, t, :],
                                                  op0=ALU.max, op1=ALU.add).then_inc(core.vector_done.sem, 1)
            dve.wait_ge(core.vector_done.sem, core.vector_done.up())
            return nc.vector.scalar_tensor_tensor(out=c.x[:, t, :], in0=u[:, :], scalar=0.5,
                                                  in1=c.x[:, t, :], op0=ALU.mult, op1=ALU.add)

        filled, freed = core.bank_filled.span(len(banks)), core.vector_freed.span(len(banks))
        with nc.Block() as block:

            @block.tensor
            def _(pe):
                for j, products in enumerate(banks):
                    if j >= BANKS:
                        pe.wait_ge(core.vector_freed.sem, freed + j - BANKS + 1)
                    fill(nc, core.bank(j), products).then_inc(core.bank_filled.sem, 1)

            @block.vector
            def _(dve):
                for j in range(len(banks)):
                    dve.wait_ge(core.bank_filled.sem, filled + j + 1)
                    if j:
                        dve.wait_ge(core.vector_freed.sem, freed + j)
                    finish(dve, j, core.bank(j)).then_inc(core.vector_freed.sem, 1)


def add_biased(core, c, u, bias, extra):
    nc = core.nc

    def f(dve, t, bank):
        nc.vector.tensor_tensor(u[:, :], bank[0:ROWS, :], bias[:, :], ALU.add).then_inc(core.vector_done.sem, 1)
        dve.wait_ge(core.vector_done.sem, core.vector_done.up())
        if extra is not None:
            nc.vector.tensor_tensor(u[:, :], u[:, :], extra[:, t, :], ALU.add).then_inc(core.vector_done.sem, 1)
            dve.wait_ge(core.vector_done.sem, core.vector_done.up())
        return nc.vector.tensor_tensor(c.x[:, t, :], c.x[:, t, :], u[:, :], ALU.add)
    return f


def layer0_mix(core, c, d):
    nc = core.nc
    EPS = 1e-6
    TH = TILES * HEADS
    with ExitStack() as ctx:
        sb = Scope(nc, ctx, "m0_")
        W = {k: sb("W" + k, [128, CH, DIM]) for k in "qkvo"}
        B = {k: sb("b" + k, [ROWS, DIM]) for k in "qkvo"}
        temp = sb("temp", [ROWS, 1])
        qkv = sb("qkv", [ROWS, 3, TILES, DIM])
        qk = sb("qk", [ROWS, TILES, DIM])
        oT = sb("oT", [128, CH, NODES])
        u = sb("u", [ROWS, DIM])
        names = ["Sqk", "Sq", "Sk", "aq", "ak", "flow", "sink", "src", "f", "big", "t1", "e"]
        s = {n: sb(n, [ROWS, TH]) for n in names}
        loads = [(W[k][:, :, :], w_view(d["L0_mix_W" + k])) for k in "qkvo"]
        loads += [(B[k][:, :], bcast(d["L0_mix_b" + k])) for k in "qkvo"]
        loads += [(temp[:, :], bcast(d["L0_mix_temperature"]))]
        with nc.Block() as block:

            @block.sync
            def _(sync):
                for dst, src in loads:
                    sync.dma_start(dst, src).then_inc(core.landed.sem, 16)
                sync.wait_ge(core.landed.sem, core.landed.up(16 * len(loads)))


        banks = []
        for k in "qkv":
            banks += row_products(c.xnT, W[k])

        def with_bias(dve, j, bank):
            return nc.vector.tensor_tensor(qkv[:, j // TILES, j % TILES, :], bank[0:ROWS, :],
                                           B["qkv"[j // TILES]][:, :], ALU.add)

        filled, freed = core.bank_filled.span(len(banks)), core.vector_freed.span(len(banks))
        with nc.Block() as block:

            @block.tensor
            def _(pe):
                for j, products in enumerate(banks):
                    if j >= BANKS:
                        pe.wait_ge(core.vector_freed.sem, freed + j - BANKS + 1)
                    fill(nc, core.bank(j), products).then_inc(core.bank_filled.sem, 1)

            @block.vector
            def _(dve):
                for j in range(len(banks)):
                    dve.wait_ge(core.bank_filled.sem, filled + j + 1)
                    if j:
                        dve.wait_ge(core.vector_freed.sem, freed + j)
                    with_bias(dve, j, core.bank(j)).then_inc(core.vector_freed.sem, 1)

        with nc.Block() as block:

            @block.scalar
            def _(act):
                nc.scalar.activation(
                    qkv[:, 0:2, :, :].rearrange("p a t n -> p (a t n)"),
                    qkv[:, 0:2, :, :].rearrange("p a t n -> p (a t n)"), ACT.Sigmoid).then_inc(core.scalar_done.sem, 1)
                act.wait_ge(core.scalar_done.sem, core.scalar_done.up())


        def by_head(ap):
            return ap.rearrange("p t (h e) -> p (t h) e", h=HEADS)

        def tt(dve, out, a, b, op):
            nc.vector.tensor_tensor(s[out][:, :], s[a][:, :], s[b][:, :], op).then_inc(core.vector_done.sem, 1)
            dve.wait_ge(core.vector_done.sem, core.vector_done.up())

        def ts(dve, out, a, s1, s2, op0, op1):
            nc.vector.tensor_scalar(s[out][:, :], s[a][:, :], s1, s2, op0, op1).then_inc(core.vector_done.sem, 1)
            dve.wait_ge(core.vector_done.sem, core.vector_done.up())

        def flows(dve):
            nc.vector.tensor_tensor(qk[:, :, :], qkv[:, 0, :, :], qkv[:, 1, :, :], ALU.mult).then_inc(core.vector_done.sem, 1)
            dve.wait_ge(core.vector_done.sem, core.vector_done.up())
            nc.vector.tensor_reduce(s["Sqk"][:, :], by_head(qk[:, :, :]), AX.X, ALU.add)
            nc.vector.tensor_reduce(s["Sq"][:, :], by_head(qkv[:, 0, :, :]), AX.X, ALU.add)
            nc.vector.tensor_reduce(s["Sk"][:, :], by_head(qkv[:, 1, :, :]), AX.X, ALU.add).then_inc(core.vector_done.sem, 1)
            dve.wait_ge(core.vector_done.sem, core.vector_done.up())
            ts(dve, "t1", "Sq", EPS, None, ALU.mult, ALU.bypass)
            tt(dve, "aq", "Sqk", "t1", ALU.add)
            ts(dve, "e", "Sk", EPS, None, ALU.mult, ALU.bypass)
            tt(dve, "ak", "Sqk", "e", ALU.add)
            tt(dve, "flow", "aq", "e", ALU.add)
            ts(dve, "flow", "flow", HDIM * EPS * EPS + EPS, None, ALU.add, ALU.bypass)
            nc.vector.reciprocal(s["f"][:, :], s["flow"][:, :]).then_inc(core.vector_done.sem, 1)
            dve.wait_ge(core.vector_done.sem, core.vector_done.up())
            tt(dve, "sink", "f", "ak", ALU.mult)
            tt(dve, "sink", "sink", "t1", ALU.add)
            ts(dve, "sink", "sink", HDIM * EPS * EPS + EPS, None, ALU.add, ALU.bypass)
            tt(dve, "src", "f", "aq", ALU.mult)
            tt(dve, "src", "src", "e", ALU.add)
            ts(dve, "src", "src", HDIM * EPS * EPS + EPS, None, ALU.add, ALU.bypass)
            ts(dve, "src", "src", 1.0, -1.0, ALU.min, ALU.max)
            nc.vector.reciprocal(temp[:, :], temp[:, :]).then_inc(core.vector_done.sem, 1)
            dve.wait_ge(core.vector_done.sem, core.vector_done.up())
            ts(dve, "src", "src", temp[:, 0:1], None, ALU.mult, ALU.bypass)
            tt(dve, "big", "src", "src", ALU.subtract)

        with nc.Block() as block:

            @block.vector
            def _(dve):
                flows(dve)


        def acts(act):
            nc.scalar.activation(s["e"][:, :], s["big"][:, :], ACT.Exp)
            nc.scalar.activation(s["sink"][:, :], s["sink"][:, :], ACT.Sigmoid).then_inc(core.scalar_done.sem, 1)
            act.wait_ge(core.scalar_done.sem, core.scalar_done.up())

        with nc.Block() as block:

            @block.scalar
            def _(act):
                acts(act)


        def weigh(dve):
            nc.vector.reciprocal(s["t1"][:, :], s["e"][:, :]).then_inc(core.vector_done.sem, 1)
            dve.wait_ge(core.vector_done.sem, core.vector_done.up())
            tt(dve, "e", "e", "t1", ALU.mult)
            ts(dve, "e", "e", float(DIM), None, ALU.mult, ALU.bypass)
            tt(dve, "f", "f", "sink", ALU.mult)
            tt(dve, "f", "f", "e", ALU.mult)
            tt(dve, "f", "f", "Sqk", ALU.mult)
            nc.vector.tensor_tensor(
                by_head(qk[:, :, :]), by_head(qkv[:, 2, :, :]),
                s["f"][:, :].unsqueeze(2).to_broadcast([ROWS, TH, HDIM]), ALU.mult).then_inc(core.vector_done.sem, 1)
            dve.wait_ge(core.vector_done.sem, core.vector_done.up())

        with nc.Block() as block:

            @block.vector
            def _(dve):
                weigh(dve)

        turn_phase(core, c, qk, oT, CH)
        add_to_x = add_biased(core, c, u, B["o"], c.xn)
        banks = row_products(oT, W["o"])
        filled, freed = core.bank_filled.span(len(banks)), core.vector_freed.span(len(banks))
        with nc.Block() as block:

            @block.tensor
            def _(pe):
                for j, products in enumerate(banks):
                    if j >= BANKS:
                        pe.wait_ge(core.vector_freed.sem, freed + j - BANKS + 1)
                    fill(nc, core.bank(j), products).then_inc(core.bank_filled.sem, 1)

            @block.vector
            def _(dve):
                for j in range(len(banks)):
                    dve.wait_ge(core.bank_filled.sem, filled + j + 1)
                    if j:
                        dve.wait_ge(core.vector_freed.sem, freed + j)
                    add_to_x(dve, j, core.bank(j)).then_inc(core.vector_freed.sem, 1)


def layer0_ffn(core, c, d):
    nc = core.nc
    FT = FFN0 // 128
    PER_CUT = BANK // 128
    with ExitStack() as ctx:
        sb = Scope(nc, ctx, "f0_")
        gate = sb("gate", [128, CH, FFN0])
        up = sb("up", [128, CH, FFN0])
        down = sb("down", [128, FT, DIM])
        hT = sb("hT", [128, FT, NODES])
        size = sb("size", [128, 4, BANK])
        sc = sb("sc", [128, BANK])
        above = sb("above", [128, BANK])
        below = sb("below", [128, BANK])
        loads = [(gate[:, :, :], w_view(d["L0_ffn_w_gate"])), (up[:, :, :], w_view(d["L0_ffn_w_up"])),
                 (down[:, :, :], w_view(d["L0_ffn_w_down"]))]
        norm_phases(core, c, c.x, c.xn, c.xnT, loads=loads)

        cuts = [(a, min(a + BANK, FFN0)) for a in range(0, FFN0, BANK)]
        pieces = [w[:, k, a:b] for w in (gate, up) for a, b in cuts for k in range(CH)]
        pieces += [down[:, f, :] for f in range(FT)]
        N = len(pieces)
        UP = len(cuts) * CH
        H = 2 * FT

        steps = [("sum", n) for n in range(CH)]
        for j in range(H):
            ahead = CH + ((N - CH) * (j + 1) + H - 1) // H
            steps += [("sum", n) for n in range(sum(1 for s in steps if s[0] == "sum"), ahead)]
            steps.append(("gate", j))

        names = ["sized", "summed", "quantised", "gate_filled", "silu_done", "up_filled", "up_taken",
                 "down_filled", "down_taken"]
        sem = {n: ctx.enter_context(nc.semaphore("f0_" + n)) for n in names}
        with nc.Block() as block:

            @block.tensor
            def _(pe):
                for kind, n in steps:
                    if kind == "sum":
                        pe.wait_ge(sem["sized"], n + 1)
                        if n >= 4:
                            pe.wait_ge(sem["quantised"], n - 3)
                        width = pieces[n].shape[-1]
                        nc.tensor.matmul(core.psum[:, n % 4, 0:width], c.ones[:, :], size[:, n % 4, 0:width],
                                         start=True, stop=True).then_inc(sem["summed"], 1)
                    else:
                        f, (a, b) = n // 2, HALVES[n % 2]
                        pe.wait_ge(sem["quantised"], CH * (f // PER_CUT + 1))
                        if n >= 4:
                            pe.wait_ge(sem["silu_done"], n - 3)
                        fill(nc, core.psum[:, 4 + n % 4, :], [product(
                            128, [(gate[:, k, chunk(f)], c.xnT[:, k, a:b]) for k in range(CH)], b - a)]).then_inc(
                            sem["gate_filled"], 1)
                for n in range(H):
                    f, (a, b) = n // 2, HALVES[n % 2]
                    pe.wait_ge(sem["quantised"], UP + CH * (f // PER_CUT + 1))
                    if n < 4:
                        pe.wait_ge(sem["silu_done"], H + n - 3)
                    else:
                        pe.wait_ge(sem["up_taken"], n - 3)
                    fill(nc, core.psum[:, 4 + (H + n) % 4, :], [product(
                        128, [(up[:, k, chunk(f)], c.xnT[:, k, a:b]) for k in range(CH)], b - a)]).then_inc(
                        sem["up_filled"], 1)
                pe.wait_ge(sem["quantised"], N)
                pe.wait_ge(sem["up_taken"], H)
                for j, products in enumerate(row_products(hT, down, chunks=FT)):
                    fill(nc, core.bank(j), products).then_inc(sem["down_filled"], 1)

            @block.scalar
            def _(act):
                def take_size(n):
                    if n >= 4:
                        act.wait_ge(sem["summed"], n - 3)
                    nc.scalar.activation(size[:, n % 4, 0:pieces[n].shape[-1]], pieces[n], ACT.Abs).then_inc(
                        sem["sized"], 1)

                for n in range(4):
                    take_size(n)
                for kind, n in steps:
                    if kind == "sum":
                        if n + 4 < N:
                            take_size(n + 4)
                    else:
                        f, (a, b) = n // 2, HALVES[n % 2]
                        act.wait_ge(sem["gate_filled"], n + 1)
                        nc.scalar.activation(hT[:, f, a:b], core.psum[:, 4 + n % 4, 0:b - a], ACT.Silu).then_inc(
                            sem["silu_done"], 1)

            @block.vector
            def _(dve):
                for n, w in enumerate(pieces):
                    width = w.shape[-1]
                    dve.wait_ge(sem["summed"], n + 1)
                    if n:
                        dve.wait_ge(sem["quantised"], n)
                    nc.vector.tensor_scalar(sc[:, 0:width], core.psum[:, n % 4, 0:width], 1.0 / 128, 1e-5,
                                            ALU.mult, ALU.add).then_inc(core.vector_done.sem, 1)
                    dve.wait_ge(core.vector_done.sem, core.vector_done.up())
                    nc.vector.scalar_tensor_tensor(out=above[:, 0:width], in0=w, scalar=2.0, in1=sc[:, 0:width],
                                                   op0=ALU.mult, op1=ALU.is_gt)
                    nc.vector.scalar_tensor_tensor(out=below[:, 0:width], in0=w, scalar=-2.0, in1=sc[:, 0:width],
                                                   op0=ALU.mult, op1=ALU.is_gt).then_inc(core.vector_done.sem, 1)
                    dve.wait_ge(core.vector_done.sem, core.vector_done.up())
                    nc.vector.tensor_tensor(above[:, 0:width], above[:, 0:width], below[:, 0:width],
                                            ALU.subtract).then_inc(core.vector_done.sem, 1)
                    dve.wait_ge(core.vector_done.sem, core.vector_done.up())
                    nc.vector.tensor_tensor(w, above[:, 0:width], sc[:, 0:width], ALU.mult).then_inc(
                        sem["quantised"], 1)
                for n in range(H):
                    f, (a, b) = n // 2, HALVES[n % 2]
                    dve.wait_ge(sem["up_filled"], n + 1)
                    dve.wait_ge(sem["silu_done"], n + 1)
                    nc.vector.tensor_tensor(hT[:, f, a:b], hT[:, f, a:b], core.psum[:, 4 + (H + n) % 4, 0:b - a],
                                            ALU.mult).then_inc(sem["up_taken"], 1)
                for j in range(TILES):
                    dve.wait_ge(sem["down_filled"], j + 1)
                    nc.vector.tensor_tensor(c.x[:, j, :], c.x[:, j, :], core.bank(j)[0:ROWS, :], ALU.add).then_inc(
                        sem["down_taken"], 1)
                dve.wait_ge(sem["down_taken"], TILES)




def layer1_gnn(core, c, d):
    nc = core.nc
    with ExitStack() as ctx:
        sb = Scope(nc, ctx, "g1_")
        W = sb("W", [128, 2 * CH, DIM])
        b = sb("b", [ROWS, DIM])
        rdeg = sb("rdeg", [128, NODES])
        meanT = sb("meanT", [128, CH, NODES])
        u = sb("u", [ROWS, DIM])
        loads = [(W[:, :, :], w_view(d["L1_gnn_W"])), (b[:, :], bcast(d["L1_gnn_b"]))]
        norm_phases(core, c, c.x, c.xn, c.xnT, loads=loads)
        banks = halves(128, lambda a, b: [(c.ones[0:ROWS, :], c.CT[:, s, a:b]) for s in range(TILES)])

        def degree(dve, j, bank):
            a, e = HALVES[j]
            nc.vector.tensor_scalar(rdeg[:, a:e], bank[:, 0:e - a], 1.0, None, ALU.max).then_inc(core.vector_done.sem, 1)
            dve.wait_ge(core.vector_done.sem, core.vector_done.up())
            last = nc.vector.reciprocal(rdeg[:, a:e], rdeg[:, a:e])
            return last

        filled, freed = core.bank_filled.span(len(banks)), core.vector_freed.span(len(banks))
        with nc.Block() as block:

            @block.tensor
            def _(pe):
                for j, products in enumerate(banks):
                    if j >= BANKS:
                        pe.wait_ge(core.vector_freed.sem, freed + j - BANKS + 1)
                    fill(nc, core.bank(j), products).then_inc(core.bank_filled.sem, 1)

            @block.vector
            def _(dve):
                for j in range(len(banks)):
                    dve.wait_ge(core.bank_filled.sem, filled + j + 1)
                    if j:
                        dve.wait_ge(core.vector_freed.sem, freed + j)
                    degree(dve, j, core.bank(j)).then_inc(core.vector_freed.sem, 1)

        banks = []
        for m in range(CH):
            banks += halves(128, lambda a, b: [(c.xn[:, s, chunk(m)], c.CT[:, s, a:b]) for s in range(TILES)])

        def mean(dve, j, bank):
            m, (a, e) = j // 2, HALVES[j % 2]
            return nc.vector.tensor_tensor(meanT[:, m, a:e], bank[:, 0:e - a], rdeg[:, a:e], ALU.mult)

        filled, freed = core.bank_filled.span(len(banks)), core.vector_freed.span(len(banks))
        with nc.Block() as block:

            @block.tensor
            def _(pe):
                for j, products in enumerate(banks):
                    if j >= BANKS:
                        pe.wait_ge(core.vector_freed.sem, freed + j - BANKS + 1)
                    fill(nc, core.bank(j), products).then_inc(core.bank_filled.sem, 1)

            @block.vector
            def _(dve):
                for j in range(len(banks)):
                    dve.wait_ge(core.bank_filled.sem, filled + j + 1)
                    if j:
                        dve.wait_ge(core.vector_freed.sem, freed + j)
                    mean(dve, j, core.bank(j)).then_inc(core.vector_freed.sem, 1)

        banks = [[product(ROWS, [(c.xnT[:, k, rows_of(t)], W[:, k, :]) for k in range(CH)]
                          + [(meanT[:, k, rows_of(t)], W[:, CH + k, :]) for k in range(CH)], DIM)]
                 for t in range(TILES)]

        def finish(dve, t, bank):
            nc.vector.tensor_tensor(u[:, :], bank[0:ROWS, :], b[:, :], ALU.add).then_inc(core.vector_done.sem, 1)
            dve.wait_ge(core.vector_done.sem, core.vector_done.up())
            return nc.vector.scalar_tensor_tensor(out=c.x[:, t, :], in0=u[:, :], scalar=0.0,
                                                  in1=c.x[:, t, :], op0=ALU.max, op1=ALU.add)

        filled, freed = core.bank_filled.span(len(banks)), core.vector_freed.span(len(banks))
        with nc.Block() as block:

            @block.tensor
            def _(pe):
                for j, products in enumerate(banks):
                    if j >= BANKS:
                        pe.wait_ge(core.vector_freed.sem, freed + j - BANKS + 1)
                    fill(nc, core.bank(j), products).then_inc(core.bank_filled.sem, 1)

            @block.vector
            def _(dve):
                for j in range(len(banks)):
                    dve.wait_ge(core.bank_filled.sem, filled + j + 1)
                    if j:
                        dve.wait_ge(core.vector_freed.sem, freed + j)
                    finish(dve, j, core.bank(j)).then_inc(core.vector_freed.sem, 1)


def linear_attention(core, c, QT, K, V1, sink, eps, accumulate):
    nc = core.nc
    with ExitStack() as ctx:
        sb = Scope(nc, ctx, "la_")
        kv = sb("kv", [128, PAIRS, 130])
        r = sb("r", [ROWS, 2, 2])
        with nc.Block() as block:

            @block.gpsimd
            def _(gp):
                nc.gpsimd.memset(kv[:, :, :], 0.0).then_inc(core.pool_done.sem, 1)
                gp.wait_ge(core.pool_done.sem, core.pool_done.up())

        banks = [[product(128, [(K[:, t, chunk(p)], V1[:, t, p, :]) for t in range(TILES)], 129)]
                 for p in range(PAIRS)]

        def blocks(dve, p, bank):
            for i in range(2):
                h = slice(HDIM * i, HDIM * (i + 1))
                nc.vector.tensor_copy(kv[h, p, h], bank[h, h])
                last = nc.vector.tensor_copy(kv[h, p, 128 + i:129 + i], bank[h, 128:129])
            return last

        filled, freed = core.bank_filled.span(len(banks)), core.vector_freed.span(len(banks))
        with nc.Block() as block:

            @block.tensor
            def _(pe):
                for j, products in enumerate(banks):
                    if j >= BANKS:
                        pe.wait_ge(core.vector_freed.sem, freed + j - BANKS + 1)
                    fill(nc, core.bank(j), products).then_inc(core.bank_filled.sem, 1)

            @block.vector
            def _(dve):
                for j in range(len(banks)):
                    dve.wait_ge(core.bank_filled.sem, filled + j + 1)
                    if j:
                        dve.wait_ge(core.vector_freed.sem, freed + j)
                    blocks(dve, j, core.bank(j)).then_inc(core.vector_freed.sem, 1)

        banks = [[product(ROWS, [(QT[:, p, rows_of(t)], kv[:, p, :])], 130)]
                 for t in range(TILES) for p in range(PAIRS)]

        def divide(dve, j, bank):
            t, p = j // PAIRS, j % PAIRS
            rj = r[:, j % 2, :]
            if eps:
                nc.vector.tensor_scalar(rj, bank[0:ROWS, 128:130], eps, None, ALU.add).then_inc(core.vector_done.sem, 1)
                dve.wait_ge(core.vector_done.sem, core.vector_done.up())
                nc.vector.reciprocal(rj, rj).then_inc(core.vector_done.sem, 1)
                dve.wait_ge(core.vector_done.sem, core.vector_done.up())
            else:
                nc.vector.reciprocal(rj, bank[0:ROWS, 128:130]).then_inc(core.vector_done.sem, 1)
                dve.wait_ge(core.vector_done.sem, core.vector_done.up())
            for i in range(2):
                dst = sink[:, t, 128 * p + HDIM * i:128 * p + HDIM * (i + 1)]
                num = bank[0:ROWS, HDIM * i:HDIM * (i + 1)]
                if accumulate:
                    last = nc.vector.scalar_tensor_tensor(out=dst, in0=num, scalar=rj[:, i:i + 1], in1=dst,
                                                          op0=ALU.mult, op1=ALU.add)
                else:
                    last = nc.vector.tensor_scalar(dst, num, rj[:, i:i + 1], None, ALU.mult)
            return last

        filled, freed = core.bank_filled.span(len(banks)), core.vector_freed.span(len(banks))
        with nc.Block() as block:

            @block.tensor
            def _(pe):
                for j, products in enumerate(banks):
                    if j >= BANKS:
                        pe.wait_ge(core.vector_freed.sem, freed + j - BANKS + 1)
                    fill(nc, core.bank(j), products).then_inc(core.bank_filled.sem, 1)

            @block.vector
            def _(dve):
                for j in range(len(banks)):
                    dve.wait_ge(core.bank_filled.sem, filled + j + 1)
                    if j:
                        dve.wait_ge(core.vector_freed.sem, freed + j)
                    divide(dve, j, core.bank(j)).then_inc(core.vector_freed.sem, 1)


def layer1_mix(core, c, d):
    nc = core.nc
    with ExitStack() as ctx:
        sb = Scope(nc, ctx, "m1_")
        Wq = sb("Wq", [128, CH, DIM])
        Wkv = sb("Wkv", [128, CH, 2 * DIM])
        QT = sb("QT", [128, CH, NODES])
        QT2 = sb("QT2", [128, CH, NODES])
        K = sb("K", [ROWS, TILES, DIM])
        K2 = sb("K2", [ROWS, TILES, DIM])
        V1 = sb("V1", [ROWS, TILES, PAIRS, 129])
        with nc.Block() as block:

            @block.gpsimd
            def _(gp):
                nc.gpsimd.memset(V1[:, :, :, 128:129], 1.0).then_inc(core.pool_done.sem, 1)
                gp.wait_ge(core.pool_done.sem, core.pool_done.up())

            @block.sync
            def _(sync):
                moves = [(Wq[:, :, :], w_view(d["L1_mix_Wq"])), (Wkv[:, :, :], w_view(d["L1_mix_Wkv"]))]
                for dst, src in moves:
                    sync.dma_start(dst, src).then_inc(core.landed.sem, 16)
                sync.wait_ge(core.landed.sem, core.landed.up(16 * len(moves)))

        banks = []
        for m in range(CH):
            banks += halves(128, lambda a, b: [(Wq[:, k, chunk(m)], c.xnT[:, k, a:b]) for k in range(CH)])
        nq = len(banks)
        for part in range(2):
            banks += row_products(c.xnT, Wkv[:, :, part * DIM:(part + 1) * DIM])

        def parts(dve, j, bank):
            if j >= nq + TILES:
                return nc.vector.tensor_copy(V1[:, j - nq - TILES, :, 0:128],
                                             bank[0:ROWS, :].rearrange("p (a n) -> p a n", a=PAIRS))
            if j < nq:
                m, (a, b) = j // 2, HALVES[j % 2]
                lo, hi, y = QT[:, m, a:b], QT2[:, m, a:b], bank[:, 0:b - a]
            else:
                lo, hi, y = K[:, j - nq, :], K2[:, j - nq, :], bank[0:ROWS, :]
            nc.vector.tensor_scalar(lo, y, 0.0, None, ALU.min)
            return nc.vector.tensor_scalar(hi, y, 0.0, None, ALU.max)

        filled, freed = core.bank_filled.span(len(banks)), core.vector_freed.span(len(banks))
        with nc.Block() as block:

            @block.tensor
            def _(pe):
                for j, products in enumerate(banks):
                    if j >= BANKS:
                        pe.wait_ge(core.vector_freed.sem, freed + j - BANKS + 1)
                    fill(nc, core.bank(j), products).then_inc(core.bank_filled.sem, 1)

            @block.vector
            def _(dve):
                for j in range(len(banks)):
                    dve.wait_ge(core.bank_filled.sem, filled + j + 1)
                    if j:
                        dve.wait_ge(core.vector_freed.sem, freed + j)
                    parts(dve, j, core.bank(j)).then_inc(core.vector_freed.sem, 1)


        def exps(act):
            nc.scalar.activation(QT[:, :, :], QT[:, :, :], ACT.Exp)
            nc.scalar.activation(K[:, :, :], K[:, :, :], ACT.Exp).then_inc(core.scalar_done.sem, 1)
            act.wait_ge(core.scalar_done.sem, core.scalar_done.up())

        with nc.Block() as block:

            @block.scalar
            def _(act):
                exps(act)


        def sums(dve):
            nc.vector.tensor_tensor(QT[:, :, :], QT[:, :, :], QT2[:, :, :], ALU.add)
            nc.vector.tensor_tensor(K[:, :, :], K[:, :, :], K2[:, :, :], ALU.add).then_inc(core.vector_done.sem, 1)
            dve.wait_ge(core.vector_done.sem, core.vector_done.up())

        with nc.Block() as block:

            @block.vector
            def _(dve):
                sums(dve)

        linear_attention(core, c, QT, K, V1, c.x, 1e-6, True)


def layer1_ffn(core, c, d):
    nc = core.nc
    FT = FF1 // 128
    with ExitStack() as ctx:
        sb = Scope(nc, ctx, "e1_")
        Wg = sb("Wg", [128, CH, EXP1])
        S = sb("S", [ROWS, TILES, EXP1])
        row = sb("row", [ROWS, TILES])
        rank = sb("rank", [ROWS, 3, TILES, EXP1])
        junk = sb("junk", [ROWS, 2, TILES, ROWS], BF16)
        tie = sb("tie", [ROWS, 2, ROWS], BF16)
        place_i = sb("place_i", [ROWS, TOP1], I32)
        place = sb("place", [ROWS, TOP1])
        W1 = sb("W1", [128, 2, CH, FF1])
        W2 = sb("W2", [128, 2, FT, DIM])
        b1 = sb("b1", [128, EXP1, FT])
        b2 = sb("b2", [TOPC, EXP1, DIM])
        P = sb("P", [ROWS, 2, TILES, TOP1])
        G = sb("G", [ROWS, 2, TILES, TOP1])
        GT = sb("GT", [TOPC, 2, 2, NODES])
        xgT = sb("xgT", [128, CH, TOP1])
        hT = sb("hT", [128, FT, TOP1])
        O = sb("O", [TOPC, 2, DIM])
        loads = [(Wg[:, :, :], w_view(d["L1_ffn_Wg"])),
                 (b1[:, :, :], d["L1_ffn_b1"]),
                 (b2[:, :, :], d["L1_ffn_b2"].rearrange("(a e) n -> a e n", a=1).to_broadcast([TOPC, EXP1, DIM]))]

        def expert_loads(e):
            return [(W1[:, e % 2, :, :], w_view(d["L1_ffn_W1"][e])), (W2[:, e % 2, :, :], w_view(d["L1_ffn_W2"][e]))]

        norm_phases(core, c, c.x, c.xn, c.xnT, loads=loads)
        banks = row_products(c.xnT, Wg, cols=EXP1)
        filled, freed = core.bank_filled.span(len(banks)), core.vector_freed.span(len(banks))
        with nc.Block() as block:

            @block.tensor
            def _(pe):
                for j, products in enumerate(banks):
                    if j >= BANKS:
                        pe.wait_ge(core.vector_freed.sem, freed + j - BANKS + 1)
                    fill(nc, core.bank(j), products).then_inc(core.bank_filled.sem, 1)

            @block.vector
            def _(dve):
                for j in range(len(banks)):
                    dve.wait_ge(core.bank_filled.sem, filled + j + 1)
                    if j:
                        dve.wait_ge(core.vector_freed.sem, freed + j)
                    nc.vector.tensor_copy(
                        S[:, j, :], core.bank(j)[0:ROWS, 0:EXP1]).then_inc(
                        core.vector_freed.sem, 1)

            @block.gpsimd
            def _(gp):
                nc.gpsimd.iota(place_i[:, :], [[1, TOP1]], base=0, channel_multiplier=0).then_inc(core.pool_done.sem, 1)
                gp.wait_ge(core.pool_done.sem, core.pool_done.up())


        def spread(v):
            return v[:, :].unsqueeze(2).to_broadcast([ROWS, TILES, EXP1])

        def less_max(dve):
            nc.vector.tensor_copy(place[:, :], place_i[:, :])
            nc.vector.memset(rank[:, :, :, :], 0.0)
            nc.vector.tensor_reduce(row[:, :], S[:, :, :], AX.X, ALU.max).then_inc(core.vector_done.sem, 1)
            dve.wait_ge(core.vector_done.sem, core.vector_done.up())
            nc.vector.tensor_tensor(S[:, :, :], S[:, :, :], spread(row), ALU.subtract).then_inc(core.vector_done.sem, 1)
            dve.wait_ge(core.vector_done.sem, core.vector_done.up())

        with nc.Block() as block:

            @block.vector
            def _(dve):
                less_max(dve)

            @block.sync
            def _(sync):
                moves = expert_loads(0)
                for dst, src in moves:
                    sync.dma_start(dst, src).then_inc(core.landed.sem, 16)
                sync.wait_ge(core.landed.sem, core.landed.up(16 * len(moves)))

        with nc.Block() as block:

            @block.scalar
            def _(act):
                nc.scalar.activation(S[:, :, :], S[:, :, :], ACT.Exp).then_inc(core.scalar_done.sem, 1)
                act.wait_ge(core.scalar_done.sem, core.scalar_done.up())


        def normed(dve):
            nc.vector.tensor_reduce(row[:, :], S[:, :, :], AX.X, ALU.add).then_inc(core.vector_done.sem, 1)
            dve.wait_ge(core.vector_done.sem, core.vector_done.up())
            nc.vector.reciprocal(row[:, :], row[:, :]).then_inc(core.vector_done.sem, 1)
            dve.wait_ge(core.vector_done.sem, core.vector_done.up())
            nc.vector.tensor_tensor(S[:, :, :], S[:, :, :], spread(row), ALU.mult).then_inc(core.vector_done.sem, 1)
            dve.wait_ge(core.vector_done.sem, core.vector_done.up())

        with nc.Block() as block:

            @block.vector
            def _(dve):
                normed(dve)


        spread, ranked = core.spread, core.ranked
        with nc.Block() as block:

            @block.tensor
            def _(pe):
                for e in range(EXP1):
                    if e >= 4:
                        pe.wait_ge(ranked.sem, e - 3)
                    for t in range(TILES):
                        k = (e % 4) * 2 + t // 4
                        at = t % 4 * 128
                        last = nc.tensor.transpose(core.psum[0:ROWS, k, at:at + ROWS],
                                                   S[:, t, e:e + 1].to_broadcast([ROWS, ROWS]),
                                                   c.ident[0:ROWS, 0:ROWS])
                    last.then_inc(spread.sem, 1)

            @block.vector
            def _(dve):
                for e in range(EXP1):
                    dve.wait_ge(spread.sem, e + 1)
                    k = (e % 4) * 2
                    others = core.psum[0:ROWS, k:k + 2, :].rearrange("p b (t n) -> p (b t) n", n=128)
                    for t in range(TILES):
                        own = S[:, t, e:e + 1]
                        if t:
                            nc.vector.tensor_scalar(
                                junk[:, t % 2, 0:t, :], others[:, 0:t, 0:ROWS], own, 0.0, ALU.is_ge, ALU.add,
                                accum_out=rank[:, 0, t, e:e + 1]).then_inc(core.vector_done.sem, 1)
                            dve.wait_ge(core.vector_done.sem, core.vector_done.up() - 2)
                        nc.vector.tensor_scalar(
                            junk[:, t % 2, t:TILES, :], others[:, t:TILES, 0:ROWS], own, 0.0, ALU.is_gt, ALU.add,
                            accum_out=rank[:, 1, t, e:e + 1]).then_inc(core.vector_done.sem, 1)
                        dve.wait_ge(core.vector_done.sem, core.vector_done.up() - 2)
                        nc.vector.scalar_tensor_tensor(
                            out=tie[:, t % 2, :], in0=others[:, t, 0:ROWS], scalar=own,
                            in1=c.below[0:ROWS, 0:ROWS], op0=ALU.is_equal, op1=ALU.mult,
                            accum_out=rank[:, 2, t, e:e + 1]).then_inc(core.vector_done.sem, 1)
                        dve.wait_ge(core.vector_done.sem, core.vector_done.up() - 2)
                    dve.wait_ge(core.vector_done.sem, core.vector_done.count)
                    nc.vector.engine_nop().then_inc(ranked.sem, 1)

            @block.sync
            def _(sync):
                moves = expert_loads(1)
                for dst, src in moves:
                    sync.dma_start(dst, src).then_inc(core.landed.sem, 16)
                sync.wait_ge(core.landed.sem, core.landed.up(16 * len(moves)))


        def total(dve):
            nc.vector.tensor_tensor(rank[:, 0, :, :], rank[:, 0, :, :], rank[:, 1, :, :], ALU.add).then_inc(core.vector_done.sem, 1)
            dve.wait_ge(core.vector_done.sem, core.vector_done.up())
            nc.vector.tensor_tensor(rank[:, 0, :, :], rank[:, 0, :, :], rank[:, 2, :, :], ALU.add).then_inc(core.vector_done.sem, 1)
            dve.wait_ge(core.vector_done.sem, core.vector_done.up())

        with nc.Block() as block:

            @block.vector
            def _(dve):
                total(dve)


        GATHERS = CH + TILES
        A = GATHERS + FT
        V = 2 + TILES
        names = ["chosen", "scalar_bank_filled", "scalar_bank_freed", "vector_bank_filled", "vector_bank_freed",
                 "w1_landed0", "w1_landed1", "w2_landed0", "w2_landed1"]
        sem = {n: ctx.enter_context(nc.semaphore("e1_" + n)) for n in names}
        with nc.Block() as block:

            @block.tensor
            def _(pe):
                def fill_for_scalar(n, products):
                    if n >= 4:
                        pe.wait_ge(sem["scalar_bank_freed"], n - 3)
                    fill(nc, core.psum[:, n % 4, :], products).then_inc(sem["scalar_bank_filled"], 1)

                def fill_for_vector(n, products):
                    if n >= 4:
                        pe.wait_ge(sem["vector_bank_freed"], n - 3)
                    fill(nc, core.psum[:, 4 + n % 4, :], products).then_inc(sem["vector_bank_filled"], 1)

                def gather(e):
                    pe.wait_ge(sem["chosen"], e + 1)
                    for k in range(CH):
                        fill_for_scalar(e * A + k, [product(
                            128, [(c.xn[:, t, chunk(k)], P[:, e % 2, t, :]) for t in range(TILES)], TOP1)])
                    for t in range(TILES):
                        fill_for_scalar(e * A + CH + t, [turned(
                            TOPC, ROWS, G[:, e % 2, t, i * TOPC:(i + 1) * TOPC], c.ident[0:ROWS, 0:ROWS],
                            at=128 * i) for i in range(2)])

                def hidden(e):
                    pe.wait_ge(sem["scalar_bank_freed"], e * A + CH)
                    if e >= 2:
                        pe.wait_ge(sem[f"w1_landed{e % 2}"], 16 * (e // 2))
                    for f in range(FT):
                        fill_for_scalar(e * A + GATHERS + f, [product(
                            128, [(W1[:, e % 2, k, chunk(f)], xgT[:, k, :]) for k in range(CH)], TOP1)])

                def output(e):
                    pe.wait_ge(sem["scalar_bank_freed"], (e + 1) * A)
                    if e >= 2:
                        pe.wait_ge(sem[f"w2_landed{e % 2}"], 16 * (e // 2))
                    for i in range(2):
                        fill_for_vector(e * V + i, [product(
                            TOPC, [(hT[:, f, i * TOPC:(i + 1) * TOPC], W2[:, e % 2, f, :]) for f in range(FT)],
                            DIM)])

                def weigh(e):
                    pe.wait_ge(sem["vector_bank_freed"], e * V + 2)
                    for t in range(TILES):
                        fill_for_vector(e * V + 2 + t, [product(
                            ROWS, [(GT[:, e % 2, i, rows_of(t)], O[:, i, :]) for i in range(2)], DIM)])

                gather(0)
                hidden(0)
                for e in range(EXP1):
                    if e + 1 < EXP1:
                        gather(e + 1)
                    output(e)
                    if e + 1 < EXP1:
                        hidden(e + 1)
                    weigh(e)

            @block.scalar
            def _(act):
                for e in range(EXP1):
                    for j in range(A):
                        n = e * A + j
                        bank = core.psum[:, n % 4, :]
                        act.wait_ge(sem["scalar_bank_filled"], n + 1)
                        if j < CH:
                            last = nc.scalar.activation(xgT[:, j, :], bank[:, 0:TOP1], ACT.Copy)
                        elif j < GATHERS:
                            last = nc.scalar.activation(
                                GT[:, e % 2, :, rows_of(j - CH)],
                                bank[0:TOPC, 0:256].rearrange("p (i n) -> p i n", i=2)[:, :, 0:ROWS], ACT.Copy)
                        else:
                            f = j - GATHERS
                            last = nc.scalar.activation(hT[:, f, :], bank[:, 0:TOP1], ACT.Gelu,
                                                        bias=b1[:, e, f:f + 1])
                        last.then_inc(sem["scalar_bank_freed"], 1)

            @block.vector
            def _(dve):
                def choose(e):
                    for t in range(TILES):
                        nc.vector.tensor_scalar(P[:, e % 2, t, :], place[:, :], rank[:, 0, t, e:e + 1], None,
                                                ALU.is_equal)
                        last = nc.vector.tensor_scalar(G[:, e % 2, t, :], place[:, :], rank[:, 0, t, e:e + 1],
                                                       S[:, t, e:e + 1], ALU.is_equal, ALU.mult)
                    last.then_inc(sem["chosen"], 1)

                choose(0)
                choose(1)
                for e in range(EXP1):
                    for i in range(2):
                        dve.wait_ge(sem["vector_bank_filled"], e * V + i + 1)
                        nc.vector.tensor_tensor(O[:, i, :], core.psum[0:TOPC, 4 + (e * V + i) % 4, :], b2[:, e, :],
                                                ALU.add).then_inc(sem["vector_bank_freed"], 1)
                    if e + 2 < EXP1:
                        choose(e + 2)
                    for t in range(TILES):
                        n = e * V + 2 + t
                        dve.wait_ge(sem["vector_bank_filled"], n + 1)
                        dve.wait_ge(sem["vector_bank_freed"], n)
                        nc.vector.tensor_tensor(c.x[:, t, :], c.x[:, t, :], core.psum[0:ROWS, 4 + n % 4, :],
                                                ALU.add).then_inc(sem["vector_bank_freed"], 1)

            @block.sync
            def _(sync):
                for e in range(2, EXP1):
                    sync.wait_ge(sem["scalar_bank_filled"], (e - 1) * A)
                    sync.dma_start(W1[:, e % 2, :, :], w_view(d["L1_ffn_W1"][e])).then_inc(
                        sem[f"w1_landed{e % 2}"], 16)
                    sync.wait_ge(sem["vector_bank_filled"], (e - 2) * V + 2)
                    sync.dma_start(W2[:, e % 2, :, :], w_view(d["L1_ffn_W2"][e])).then_inc(
                        sem[f"w2_landed{e % 2}"], 16)




def gat_layer(core, c, d, k, inT, chunks, h, masked, out, names, ctx_tag):
    nc = core.nc
    with ExitStack() as ctx:
        sb = Scope(nc, ctx, ctx_tag)
        W = sb("W", [128, chunks, GAT_DIM])
        att = sb("att", [ROWS, 2, GAT_DIM])
        b = sb("b", [ROWS, GAT_DIM])
        norm_phases(core, c, c.x, c.xn, inT, loads=[
            (W[:, :, :], w_view(d[names[0]])), (att[:, 0, :], bcast(d[names[1]])),
            (att[:, 1, :], bcast(d[names[2]])), (b[:, :], bcast(d[names[3]]))])
        banks = []
        for t in range(TILES):
            for j in range(2):
                banks.append([product(ROWS, [(inT[:, q, rows_of(t)], W[:, q, j * DIM:(j + 1) * DIM])
                                             for q in range(chunks)], DIM)])
        filled, freed = core.bank_filled.span(len(banks)), core.scalar_freed.span(len(banks))
        with nc.Block() as block:

            @block.tensor
            def _(pe):
                for j, products in enumerate(banks):
                    if j >= BANKS:
                        pe.wait_ge(core.scalar_freed.sem, freed + j - BANKS + 1)
                    fill(nc, core.bank(j), products).then_inc(core.bank_filled.sem, 1)

            @block.scalar
            def _(act):
                for j in range(len(banks)):
                    act.wait_ge(core.bank_filled.sem, filled + j + 1)
                    nc.scalar.activation(
                        h[:, j // 2, 2 * (j % 2):2 * (j % 2) + 2, 0:GAT_HID],
                        core.bank(j)[0:ROWS, :].rearrange("p (a n) -> p a n", a=2), ACT.Copy).then_inc(
                        core.scalar_freed.sem, 1)

        gat_heads(core, c, h, att, b, masked, out)


def gat_heads(core, c, h, att, b, masked, out):
    nc = core.nc
    NH = GAT_HEADS
    with ExitStack() as ctx:
        sb = Scope(nc, ctx, "gat_")
        a = sb("a", [ROWS, 2, TILES, NH])
        a_low = sb("a_low", [ROWS, TILES, NH])
        top = sb("top", [ROWS, TILES, NH])
        tmp = sb("tmp", [ROWS, TILES, NH])
        high = sb("high", [ROWS, TILES, NH])
        low = sb("low", [ROWS, TILES, NH])
        junk = sb("junk", [ROWS, 2, TILES, ROWS])
        highB = sb("highB", [ROWS, TILES, ROWS])
        u = sb("u", [ROWS, 2, TILES, NODES])
        r = sb("r", [ROWS, 2])
        names = ["scored", "source_spread", "shifts_made", "shifts_spread", "low_added", "higher_taken",
                 "exponents_done", "weighted", "aggregated", "combined"]
        sem = {n: ctx.enter_context(nc.semaphore(n + f"_{Scope.made}")) for n in names}

        def spread(bank0, col):
            for t in range(TILES):
                last = nc.tensor.transpose(core.psum[0:ROWS, bank0 + t // 4, t % 4 * 128:t % 4 * 128 + ROWS],
                                           col(t).to_broadcast([ROWS, ROWS]), c.ident[0:ROWS, 0:ROWS])
            return last

        def spread_view(bank0):
            return core.psum[0:ROWS, bank0:bank0 + 2, :].rearrange("p b (t n) -> p (b t) n", n=128)[:, 0:TILES, 0:ROWS]

        with nc.Block() as block:

            @block.tensor
            def _(pe):
                pe.wait_ge(sem["scored"], 1)
                for hd in range(NH):
                    spread(2 * hd, lambda t: a[:, 0, t, hd:hd + 1]).then_inc(sem["source_spread"], 1)

                def aggregate(hd):
                    pe.wait_ge(sem["weighted"], hd + 1)
                    for t in range(TILES):
                        n = hd * TILES + t
                        if n >= 4:
                            pe.wait_ge(sem["combined"], n - 3)
                        for s in range(TILES):
                            last = nc.tensor.matmul(core.psum[0:ROWS, 4 + n % 4, 0:GAT_HID + 1],
                                                    u[:, hd % 2, s, rows_of(t)], h[:, s, hd, :],
                                                    start=(s == 0), stop=(s == TILES - 1))
                        last.then_inc(sem["aggregated"], 1)

                for hd in range(NH):
                    if hd == 0:
                        pe.wait_ge(sem["shifts_made"], 1)
                    else:
                        pe.wait_ge(sem["low_added"], hd)
                    spread(0, lambda t: high[:, t, hd:hd + 1])
                    spread(2, lambda t: low[:, t, hd:hd + 1]).then_inc(sem["shifts_spread"], 1)
                    if hd:
                        aggregate(hd - 1)
                aggregate(NH - 1)

            @block.scalar
            def _(act):
                def exponents(hd):
                    act.wait_ge(sem["higher_taken"], hd + 1)
                    nc.scalar.activation(u[:, hd % 2, :, :], u[:, hd % 2, :, :], ACT.Relu, scale=-1.0).then_inc(
                        core.scalar_done.sem, 1)
                    act.wait_ge(core.scalar_done.sem, core.scalar_done.up())
                    nc.scalar.activation(u[:, hd % 2, :, :], u[:, hd % 2, :, :], ACT.Exp, scale=-1.0).then_inc(
                        sem["exponents_done"], 1)

                for hd in range(NH):
                    act.wait_ge(sem["shifts_spread"], hd + 1)
                    if hd >= 1:
                        act.wait_ge(sem["higher_taken"], hd)
                    if hd >= 2:
                        act.wait_ge(sem["aggregated"], TILES * (hd - 1))
                    nc.scalar.activation(highB[:, :, :], spread_view(0), ACT.Copy)
                    for s in range(TILES):
                        last = nc.scalar.activation(u[:, hd % 2, s, :].rearrange("p (t n) -> p t n", n=ROWS),
                                                    spread_view(2), ACT.Identity, bias=a_low[:, s, hd:hd + 1])
                    last.then_inc(sem["low_added"], 1)
                    if hd == 1:
                        exponents(0)
                    if hd:
                        exponents(hd)

            @block.vector
            def _(dve):
                start = core.vector_done.count
                for w in range(2):
                    for t in range(TILES):
                        for hd in range(NH):
                            nc.vector.tensor_tensor_reduce(
                                out=u[:, hd % 2, 0, 0:GAT_HID], in0=h[:, t, hd, 0:GAT_HID],
                                in1=att[:, w, hd * GAT_HID:(hd + 1) * GAT_HID], scale=1.0, scalar=0.0,
                                op0=ALU.mult, op1=ALU.add, accum_out=a[:, w, t, hd:hd + 1]).then_inc(
                                core.vector_done.sem, 1)
                            if core.vector_done.up() > start + 1:
                                dve.wait_ge(core.vector_done.sem, core.vector_done.count - 1)
                dve.wait_ge(core.vector_done.sem, core.vector_done.count)
                nc.vector.tensor_scalar(a_low[:, :, :], a[:, 0, :, :], 0.2, None, ALU.mult).then_inc(sem["scored"], 1)
                start = core.vector_done.count
                for hd in range(NH):
                    dve.wait_ge(sem["source_spread"], hd + 1)
                    for t in range(TILES):
                        nc.vector.tensor_tensor_reduce(
                            out=junk[:, (hd * TILES + t) % 2, :, :], in0=spread_view(2 * hd),
                            in1=masked[:, t, :].rearrange("p (t n) -> p t n", n=ROWS), scale=1.0, scalar=-3e38,
                            op0=ALU.add, op1=ALU.max, accum_out=top[:, t, hd:hd + 1]).then_inc(
                            core.vector_done.sem, 1)
                        if core.vector_done.up() > start + 1:
                            dve.wait_ge(core.vector_done.sem, core.vector_done.count - 1)
                dve.wait_ge(core.vector_done.sem, core.vector_done.count)
                nc.vector.tensor_tensor(top[:, :, :], top[:, :, :], a[:, 1, :, :], ALU.add).then_inc(
                    core.vector_done.sem, 1)
                dve.wait_ge(core.vector_done.sem, core.vector_done.up())
                nc.vector.scalar_tensor_tensor(out=tmp[:, :, :], in0=top[:, :, :], scalar=0.2, in1=top[:, :, :],
                                               op0=ALU.mult, op1=ALU.max).then_inc(core.vector_done.sem, 1)
                dve.wait_ge(core.vector_done.sem, core.vector_done.up())
                nc.vector.tensor_tensor(high[:, :, :], a[:, 1, :, :], tmp[:, :, :], ALU.subtract)
                nc.vector.scalar_tensor_tensor(out=low[:, :, :], in0=a[:, 1, :, :], scalar=0.2, in1=tmp[:, :, :],
                                               op0=ALU.mult, op1=ALU.subtract).then_inc(sem["shifts_made"], 1)

                def combine(hd):
                    for t in range(TILES):
                        n = hd * TILES + t
                        bank = core.psum[0:ROWS, 4 + n % 4, :]
                        dst = out[:, t, hd * GAT_HID:(hd + 1) * GAT_HID]
                        rt = r[:, t % 2:t % 2 + 1]
                        dve.wait_ge(sem["aggregated"], n + 1)
                        nc.vector.tensor_scalar(rt, bank[:, GAT_HID:GAT_HID + 1], 1e-16, None, ALU.add).then_inc(
                            core.vector_done.sem, 1)
                        dve.wait_ge(core.vector_done.sem, core.vector_done.up())
                        nc.vector.reciprocal(rt, rt).then_inc(core.vector_done.sem, 1)
                        dve.wait_ge(core.vector_done.sem, core.vector_done.up())
                        nc.vector.scalar_tensor_tensor(
                            out=dst, in0=bank[:, 0:GAT_HID], scalar=rt, in1=b[:, hd * GAT_HID:(hd + 1) * GAT_HID],
                            op0=ALU.mult, op1=ALU.add).then_inc(sem["combined"], 1)
                        dve.wait_ge(sem["combined"], n + 1)

                def take_higher(hd):
                    dve.wait_ge(sem["low_added"], hd + 1)
                    for s in range(TILES):
                        us = u[:, hd % 2, s, :].rearrange("p (t n) -> p t n", n=ROWS)
                        last = nc.vector.scalar_tensor_tensor(out=us, in0=highB[:, :, :],
                                                              scalar=a[:, 0, s, hd:hd + 1], in1=us,
                                                              op0=ALU.add, op1=ALU.max)
                    last.then_inc(sem["higher_taken"], 1)

                def weigh(hd):
                    dve.wait_ge(sem["exponents_done"], hd + 1)
                    nc.vector.tensor_tensor(u[:, hd % 2, :, :], u[:, hd % 2, :, :], c.CT[:, :, :],
                                            ALU.mult).then_inc(sem["weighted"], 1)

                take_higher(0)
                take_higher(1)
                weigh(0)
                weigh(1)
                for hd in range(NH):
                    combine(hd)
                    if 2 <= hd + 1 < NH:
                        weigh(hd + 1)
                    if hd + 2 < NH:
                        take_higher(hd + 2)
                nc.vector.tensor_scalar(out[:, :, :], out[:, :, :], 0.0, None, ALU.max)


def layer2_gnn(core, c, d):
    nc = core.nc
    with ExitStack() as ctx:
        sb = Scope(nc, ctx, "g2_")
        masked = sb("masked", [ROWS, TILES, NODES])
        out = sb("out", [ROWS, TILES, GAT_DIM])
        h = sb("h", [ROWS, TILES, GAT_HEADS, GAT_HID + 1])

        def own_loops(dve):
            for t in range(TILES):
                last = nc.vector.tensor_tensor(c.CT[:, t, rows_of(t)], c.CT[:, t, rows_of(t)],
                                               c.ident[0:ROWS, 0:ROWS], ALU.add)
            last.then_inc(core.vector_done.sem, 1)
            dve.wait_ge(core.vector_done.sem, core.vector_done.up())
            nc.vector.memset(h[:, :, :, GAT_HID:GAT_HID + 1], 1.0).then_inc(core.vector_done.sem, 1)
            dve.wait_ge(core.vector_done.sem, core.vector_done.up())

        with nc.Block() as block:

            @block.vector
            def _(dve):
                own_loops(dve)

        banks, where = [], []
        for t in range(TILES):
            for s0 in (0, 4):
                n = min(4, TILES - s0)
                banks.append([turned(ROWS, ROWS, c.CT[:, s, rows_of(t)], c.ident[0:ROWS, 0:ROWS],
                                     at=128 * (s - s0)) for s in range(s0, s0 + n)])
                where.append((t, s0, n))

        def mask(dve, j, bank):
            t, s0, n = where[j]
            src = bank[0:ROWS, :].rearrange("p (t n) -> p t n", n=128)[:, 0:n, 0:ROWS]
            dst = masked[:, t, s0 * ROWS:(s0 + n) * ROWS].rearrange("p (t n) -> p t n", n=ROWS)
            return nc.vector.tensor_scalar(dst, src, 0.0, -1e30, ALU.is_equal, ALU.mult)

        filled, freed = core.bank_filled.span(len(banks)), core.vector_freed.span(len(banks))
        with nc.Block() as block:

            @block.tensor
            def _(pe):
                for j, products in enumerate(banks):
                    if j >= BANKS:
                        pe.wait_ge(core.vector_freed.sem, freed + j - BANKS + 1)
                    fill(nc, core.bank(j), products).then_inc(core.bank_filled.sem, 1)

            @block.vector
            def _(dve):
                for j in range(len(banks)):
                    dve.wait_ge(core.bank_filled.sem, filled + j + 1)
                    if j:
                        dve.wait_ge(core.vector_freed.sem, freed + j)
                    mask(dve, j, core.bank(j)).then_inc(core.vector_freed.sem, 1)

        n1 = ["L2_gnn_W1", "L2_gnn_att_src1", "L2_gnn_att_dst1", "L2_gnn_b1"]
        n2 = ["L2_gnn_W2", "L2_gnn_att_src2", "L2_gnn_att_dst2", "L2_gnn_b2"]
        gat_layer(core, c, d, 1, c.xnT, CH, h, masked, out, n1, "ga_")
        with ExitStack() as inner:
            sb2 = Scope(nc, inner, "gh_")
            att = sb2("att", [ROWS, 2, GAT_DIM])
            b = sb2("b", [ROWS, GAT_DIM])
            gat_layer_weights(core, c, d, out, h, n2, [
                (att[:, 0, :], bcast(d[n2[1]])), (att[:, 1, :], bcast(d[n2[2]])), (b[:, :], bcast(d[n2[3]]))])
            gat_heads(core, c, h, att, b, masked, out)
        with ExitStack() as inner:
            sb2 = Scope(nc, inner, "gf_")
            outT = sb2("outT", [128, 2 * CH, NODES])
            W = sb2("W", [128, 2 * CH, DIM])
            bf = sb2("bf", [ROWS, DIM])
            u = sb2("u", [ROWS, DIM])
            turn_phase(core, c, out, outT, 2 * CH, loads=[(W[:, :, :], w_view(d["L2_gnn_fcW"])),
                                                         (bf[:, :], bcast(d["L2_gnn_fcb"]))])
            add_to_x = add_biased(core, c, u, bf, None)
            banks = row_products(outT, W, chunks=2 * CH)
            filled, freed = core.bank_filled.span(len(banks)), core.vector_freed.span(len(banks))
            with nc.Block() as block:

                @block.tensor
                def _(pe):
                    for j, products in enumerate(banks):
                        if j >= BANKS:
                            pe.wait_ge(core.vector_freed.sem, freed + j - BANKS + 1)
                        fill(nc, core.bank(j), products).then_inc(core.bank_filled.sem, 1)

                @block.vector
                def _(dve):
                    for j in range(len(banks)):
                        dve.wait_ge(core.bank_filled.sem, filled + j + 1)
                        if j:
                            dve.wait_ge(core.vector_freed.sem, freed + j)
                        add_to_x(dve, j, core.bank(j)).then_inc(core.vector_freed.sem, 1)


def gat_layer_weights(core, c, d, rows, h, names, loads):
    nc = core.nc
    chunks = 2 * CH
    with ExitStack() as ctx:
        sb = Scope(nc, ctx, "gw_")
        inT = sb("inT", [128, chunks, NODES])
        W2 = sb("W", [128, 2, chunks, DIM])

        def half_load(half):
            return (W2[:, half, :, :], w_view(d[names[0]])[:, :, half * DIM:(half + 1) * DIM])

        turn_phase(core, c, rows, inT, 2 * CH, loads=[half_load(0)])
        for half in range(2):
            banks = row_products(inT, W2[:, half, :, :], chunks=chunks)
            filled, freed = core.bank_filled.span(len(banks)), core.scalar_freed.span(len(banks))
            with nc.Block() as block:

                @block.sync
                def _(sync):
                    moves = [half_load(1)] + loads if half == 0 else []
                    for dst, src in moves:
                        sync.dma_start(dst, src).then_inc(core.landed.sem, 16)
                    if moves:
                        sync.wait_ge(core.landed.sem, core.landed.up(16 * len(moves)))

                @block.tensor
                def _(pe):
                    for j, products in enumerate(banks):
                        if j >= BANKS:
                            pe.wait_ge(core.scalar_freed.sem, freed + j - BANKS + 1)
                        fill(nc, core.bank(j), products).then_inc(core.bank_filled.sem, 1)

                @block.scalar
                def _(act):
                    for j in range(len(banks)):
                        act.wait_ge(core.bank_filled.sem, filled + j + 1)
                        nc.scalar.activation(
                            h[:, j, 2 * half:2 * half + 2, 0:GAT_HID], core.bank(j)[0:ROWS, :].rearrange("p (a n) -> p a n", a=2), ACT.Copy).then_inc(
                            core.scalar_freed.sem, 1)


def layer2_mix(core, c, d):
    nc = core.nc
    EPS, CLAMP = 1e-8, 50.0
    with ExitStack() as ctx:
        sb = Scope(nc, ctx, "m2_")
        W = {k: sb("W" + k, [128, CH, DIM]) for k in "qkvo"}
        om = {k: sb("om" + k, [128, 128]) for k in "qk"}
        both = sb("both", [128, 128])
        T = {k: sb("T" + k, [128, CH, NODES]) for k in "qk"}
        sq = sb("sq", [128, CH, NODES])
        K = sb("K", [ROWS, TILES, DIM])
        V1 = sb("V1", [ROWS, TILES, PAIRS, 129])
        o_rows = sb("o", [ROWS, TILES, DIM])

        def clear(gp):
            for k in "qk":
                nc.gpsimd.memset(om[k][:, :], 0.0)
            nc.gpsimd.memset(both[:, :], 0.0)
            last = nc.gpsimd.memset(V1[:, :, :, 128:129], 1.0)
            last.then_inc(core.pool_done.sem, 1)
            gp.wait_ge(core.pool_done.sem, core.pool_done.up())
            for i in range(2):
                h = slice(HDIM * i, HDIM * (i + 1))
                last = nc.gpsimd.memset(both[h, h], 1.0)
            last.then_inc(core.pool_done.sem, 1)
            gp.wait_ge(core.pool_done.sem, core.pool_done.up())

        with nc.Block() as block:

            @block.gpsimd
            def _(gp):
                clear(gp)

        loads = [(W[k][:, :, :], w_view(d["L2_mix_W" + k])) for k in "qkvo"]
        for k in "qk":
            for i in range(2):
                h = slice(HDIM * i, HDIM * (i + 1))
                loads.append((om[k][h, h], d["L2_mix_omega_" + k]))
        with nc.Block() as block:

            @block.sync
            def _(sync):
                for dst, src in loads:
                    sync.dma_start(dst, src).then_inc(core.landed.sem, 16)
                sync.wait_ge(core.landed.sem, core.landed.up(16 * len(loads)))

        banks = []
        for k in "qk":
            for m in range(CH):
                banks += halves(128, lambda a, b: [(W[k][:, q, chunk(m)], c.xnT[:, q, a:b]) for q in range(CH)])
        nq = len(banks)
        banks += row_products(c.xnT, W["v"])

        def keep(act, j, bank):
            if j >= nq:
                return nc.scalar.activation(V1[:, j - nq, :, 0:128],
                                            bank[0:ROWS, :].rearrange("p (a n) -> p a n", a=PAIRS), ACT.Copy)
            k, m, (a, b) = "qk"[j // (2 * CH)], j // 2 % CH, HALVES[j % 2]
            return nc.scalar.activation(T[k][:, m, a:b], bank[:, 0:b - a], ACT.Copy, scale=HDIM ** -0.5)

        filled, freed = core.bank_filled.span(len(banks)), core.scalar_freed.span(len(banks))
        with nc.Block() as block:

            @block.tensor
            def _(pe):
                for j, products in enumerate(banks):
                    if j >= BANKS:
                        pe.wait_ge(core.scalar_freed.sem, freed + j - BANKS + 1)
                    fill(nc, core.bank(j), products).then_inc(core.bank_filled.sem, 1)

            @block.scalar
            def _(act):
                for j in range(len(banks)):
                    act.wait_ge(core.bank_filled.sem, filled + j + 1)
                    keep(act, j, core.bank(j)).then_inc(core.scalar_freed.sem, 1)

        for k in "qk":
            with nc.Block() as block:

                @block.vector
                def _(dve):
                    nc.vector.tensor_tensor(
                        sq[:, :, :], T[k][:, :, :], T[k][:, :, :], ALU.mult).then_inc(core.vector_done.sem, 1)
                    dve.wait_ge(core.vector_done.sem, core.vector_done.up())

            banks = []
            for m in range(CH):
                banks += halves(128, lambda a, b: [(om[k][:, :], T[k][:, m, a:b])])
                banks += halves(128, lambda a, b: [(both[:, :], sq[:, m, a:b])])

            def features(dve, j, bank):
                m, part, (a, b) = j // 4, j // 2 % 2, HALVES[j % 2]
                if part == 0:
                    return nc.vector.tensor_scalar(T[k][:, m, a:b], bank[:, 0:b - a], CLAMP, None, ALU.min)
                return nc.vector.tensor_scalar(sq[:, m, a:b], bank[:, 0:b - a], EPS * EPS, None, ALU.max)

            filled, freed = core.bank_filled.span(len(banks)), core.vector_freed.span(len(banks))
            with nc.Block() as block:

                @block.tensor
                def _(pe):
                    for j, products in enumerate(banks):
                        if j >= BANKS:
                            pe.wait_ge(core.vector_freed.sem, freed + j - BANKS + 1)
                        fill(nc, core.bank(j), products).then_inc(core.bank_filled.sem, 1)

                @block.vector
                def _(dve):
                    for j in range(len(banks)):
                        dve.wait_ge(core.bank_filled.sem, filled + j + 1)
                        if j:
                            dve.wait_ge(core.vector_freed.sem, freed + j)
                        features(dve, j, core.bank(j)).then_inc(core.vector_freed.sem, 1)


            def exps(act):
                nc.scalar.activation(sq[:, :, :], sq[:, :, :], ACT.Exp, scale=-0.5)
                nc.scalar.activation(T[k][:, :, :], T[k][:, :, :], ACT.Exp).then_inc(core.scalar_done.sem, 1)
                act.wait_ge(core.scalar_done.sem, core.scalar_done.up())

            with nc.Block() as block:

                @block.scalar
                def _(act):
                    exps(act)

            with nc.Block() as block:

                @block.vector
                def _(dve):
                    nc.vector.scalar_tensor_tensor(
                        out=T[k][:, :, :], in0=sq[:, :, :], scalar=EPS, in1=T[k][:, :, :], op0=ALU.max, op1=ALU.mult).then_inc(core.vector_done.sem, 1)
                    dve.wait_ge(core.vector_done.sem, core.vector_done.up())

        banks = [[turned(ROWS, 128, T["k"][:, m, rows_of(t)], c.ident[:, :], at=128 * m) for m in range(CH)]
                 for t in range(TILES)]
        filled, freed = core.bank_filled.span(len(banks)), core.scalar_freed.span(len(banks))
        with nc.Block() as block:

            @block.tensor
            def _(pe):
                for j, products in enumerate(banks):
                    if j >= BANKS:
                        pe.wait_ge(core.scalar_freed.sem, freed + j - BANKS + 1)
                    fill(nc, core.bank(j), products).then_inc(core.bank_filled.sem, 1)

            @block.scalar
            def _(act):
                for j in range(len(banks)):
                    act.wait_ge(core.bank_filled.sem, filled + j + 1)
                    nc.scalar.activation(
                        K[:, j, :], core.bank(j)[0:ROWS, :], ACT.Copy).then_inc(
                        core.scalar_freed.sem, 1)

        linear_attention(core, c, T["q"], K, V1, o_rows, 0.0, False)
        turn_phase(core, c, o_rows, sq, CH)
        banks = row_products(sq, W["o"])
        filled, freed = core.bank_filled.span(len(banks)), core.vector_freed.span(len(banks))
        with nc.Block() as block:

            @block.tensor
            def _(pe):
                for j, products in enumerate(banks):
                    if j >= BANKS:
                        pe.wait_ge(core.vector_freed.sem, freed + j - BANKS + 1)
                    fill(nc, core.bank(j), products).then_inc(core.bank_filled.sem, 1)

            @block.vector
            def _(dve):
                for j in range(len(banks)):
                    dve.wait_ge(core.bank_filled.sem, filled + j + 1)
                    if j:
                        dve.wait_ge(core.vector_freed.sem, freed + j)
                    nc.vector.tensor_tensor(
                        c.x[:, j, :], c.x[:, j, :], core.bank(j)[0:ROWS, :], ALU.add).then_inc(
                        core.vector_freed.sem, 1)


def layer2_ffn(core, c, d, ctx):
    nc = core.nc
    FT = FF2 // 128
    sorted_x, sorted_y = c.sorted_x, c.sorted_y
    with ExitStack() as local:
        sb = Scope(nc, local, "e2_")
        pos = sb("pos", [ROWS, TILES], I32)
        slot_i = sb("slot_i", [1, SLOTS + 1], I32)
        scattered = local.enter_context(nc.semaphore("tokens_scattered"))
        gathered = local.enter_context(nc.semaphore("results_gathered"))
        with ExitStack() as inner:
            sb2 = Scope(nc, inner, "r2_")
            Wr = sb2("Wr", [128, CH, EXP2 - 1])
            br = sb2("br", [ROWS, EXP2 - 1])
            right = sb2("right", [ROWS, TILES, EXP2 - 1])
            leaf = sb2("leaf", [ROWS, 2, TILES, EXP2])
            rank = sb2("rank", [ROWS, TILES, EXP2])
            count = sb2("count", [ROWS, EXP2])
            used = sb2("used", [ROWS, EXP2])
            ends = sb2("ends", [ROWS, 2, EXP2])
            posf = sb2("posf", [ROWS, TILES])
            slot_n = sb2("slot_n", [1, SLOTS], I32)
            slot_f = sb2("slot_f", [1, SLOTS])
            slot_c = sb2("slot_c", [1, SLOTS, EXP2])
            norm_phases(core, c, c.x, c.xn, c.xnT, loads=[(Wr[:, :, :], w_view(d["L2_ffn_Wr"])),
                                                         (br[:, :], bcast(d["L2_ffn_br"]))])
            banks = row_products(c.xnT, Wr, cols=EXP2 - 1)
            filled, freed = core.bank_filled.span(len(banks)), core.vector_freed.span(len(banks))
            with nc.Block() as block:

                @block.gpsimd
                def _(gp):
                    nc.gpsimd.iota(slot_n[:, :], [[1, SLOTS]], base=0, channel_multiplier=0)

                @block.tensor
                def _(pe):
                    for j, products in enumerate(banks):
                        if j >= BANKS:
                            pe.wait_ge(core.vector_freed.sem, freed + j - BANKS + 1)
                        fill(nc, core.bank(j), products).then_inc(core.bank_filled.sem, 1)

                @block.vector
                def _(dve):
                    for j in range(len(banks)):
                        dve.wait_ge(core.bank_filled.sem, filled + j + 1)
                        if j:
                            dve.wait_ge(core.vector_freed.sem, freed + j)
                        nc.vector.tensor_tensor(right[:, j, :], core.bank(j)[0:ROWS, 0:EXP2 - 1], br[:, :], ALU.add).then_inc(
                            core.vector_freed.sem, 1)


            def descend(dve):
                nc.vector.tensor_scalar(right[:, :, :], right[:, :, :], 0.0, None, ALU.is_gt).then_inc(core.vector_done.sem, 1)
                dve.wait_ge(core.vector_done.sem, core.vector_done.up())
                nc.vector.memset(leaf[:, 0, :, 0:1], 1.0).then_inc(core.vector_done.sem, 1)
                dve.wait_ge(core.vector_done.sem, core.vector_done.up())
                depth = EXP2.bit_length() - 1
                for lv in range(depth):
                    n = 2 ** lv
                    old, new = leaf[:, lv % 2, :, 0:n], leaf[:, (lv + 1) % 2, :, 0:2 * n].rearrange(
                        "p t (n b) -> p t n b", b=2)
                    nc.vector.tensor_tensor(new[:, :, :, 1], old, right[:, :, n - 1:2 * n - 1], ALU.mult).then_inc(core.vector_done.sem, 1)
                    dve.wait_ge(core.vector_done.sem, core.vector_done.up())
                    nc.vector.tensor_tensor(new[:, :, :, 0], old, new[:, :, :, 1], ALU.subtract).then_inc(core.vector_done.sem, 1)
                    dve.wait_ge(core.vector_done.sem, core.vector_done.up())
            with nc.Block() as block:

                @block.vector
                def _(dve):
                    descend(dve)

            oh = leaf[:, (EXP2.bit_length() - 1) % 2, :, :]
            banks = [[product(ROWS, [(c.above[0:ROWS, 0:ROWS], oh[:, t, :])]
                              + [(c.ones[0:ROWS, 0:ROWS], oh[:, s, :]) for s in range(t)], EXP2)]
                     for t in range(TILES)]
            banks.append([product(ROWS, [(c.ones[0:ROWS, 0:ROWS], oh[:, s, :]) for s in range(TILES)], EXP2)])
            filled, freed = core.bank_filled.span(len(banks)), core.vector_freed.span(len(banks))
            with nc.Block() as block:

                @block.tensor
                def _(pe):
                    for j, products in enumerate(banks):
                        if j >= BANKS:
                            pe.wait_ge(core.vector_freed.sem, freed + j - BANKS + 1)
                        fill(nc, core.bank(j), products).then_inc(core.bank_filled.sem, 1)

                @block.vector
                def _(dve):
                    for j in range(len(banks)):
                        dve.wait_ge(core.bank_filled.sem, filled + j + 1)
                        if j:
                            dve.wait_ge(core.vector_freed.sem, freed + j)
                        nc.vector.tensor_copy(
                            rank[:, j, :] if j < TILES else count[:, :], core.bank(j)[0:ROWS, 0:EXP2]).then_inc(
                            core.vector_freed.sem, 1)


            def assign(dve):
                nc.vector.tensor_scalar(used[:, :], count[:, :], 0.0, None, ALU.is_gt).then_inc(core.vector_done.sem, 1)
                dve.wait_ge(core.vector_done.sem, core.vector_done.up())
                for k in range(1, (NODES + SLOT - 1) // SLOT):
                    nc.vector.scalar_tensor_tensor(out=used[:, :], in0=count[:, :], scalar=float(k * SLOT),
                                                          in1=used[:, :], op0=ALU.is_gt, op1=ALU.add).then_inc(core.vector_done.sem, 1)
                    dve.wait_ge(core.vector_done.sem, core.vector_done.up())
                nc.vector.tensor_copy(ends[:, 0, :], used[:, :]).then_inc(core.vector_done.sem, 1)
                dve.wait_ge(core.vector_done.sem, core.vector_done.up())
                now, step = 0, 1
                while step < EXP2:
                    nc.vector.tensor_copy(ends[:, 1 - now, 0:step], ends[:, now, 0:step])
                    nc.vector.tensor_tensor(ends[:, 1 - now, step:EXP2], ends[:, now, step:EXP2],
                                                   ends[:, now, 0:EXP2 - step], ALU.add).then_inc(core.vector_done.sem, 1)
                    dve.wait_ge(core.vector_done.sem, core.vector_done.up())
                    now, step = 1 - now, step * 2
                end = ends[:, now, :]
                start = ends[:, 1 - now, :]
                nc.vector.tensor_tensor(start, end, used[:, :], ALU.subtract).then_inc(core.vector_done.sem, 1)
                dve.wait_ge(core.vector_done.sem, core.vector_done.up())
                nc.vector.tensor_scalar(start, start, float(SLOT), None, ALU.mult).then_inc(core.vector_done.sem, 1)
                dve.wait_ge(core.vector_done.sem, core.vector_done.up())
                nc.vector.tensor_tensor(rank[:, :, :], rank[:, :, :],
                                               start.unsqueeze(1).to_broadcast([ROWS, TILES, EXP2]), ALU.add).then_inc(core.vector_done.sem, 1)
                dve.wait_ge(core.vector_done.sem, core.vector_done.up())
                nc.vector.tensor_tensor(rank[:, :, :], rank[:, :, :], oh, ALU.mult).then_inc(core.vector_done.sem, 1)
                dve.wait_ge(core.vector_done.sem, core.vector_done.up())
                nc.vector.tensor_reduce(posf[:, :], rank[:, :, :], AX.X, ALU.add).then_inc(core.vector_done.sem, 1)
                dve.wait_ge(core.vector_done.sem, core.vector_done.up())
                nc.vector.tensor_copy(pos[:, :], posf[:, :])
                nc.vector.tensor_copy(slot_f[:, :], slot_n[:, :]).then_inc(core.vector_done.sem, 1)
                dve.wait_ge(core.vector_done.sem, core.vector_done.up())
                nc.vector.tensor_tensor(
                    slot_c[:, :, :], end[0:1, :].unsqueeze(1).to_broadcast([1, SLOTS, EXP2]),
                    slot_f[:, :].unsqueeze(2).to_broadcast([1, SLOTS, EXP2]), ALU.is_le).then_inc(core.vector_done.sem, 1)
                dve.wait_ge(core.vector_done.sem, core.vector_done.up())
                nc.vector.tensor_reduce(slot_f[:, :], slot_c[:, :, :], AX.X, ALU.add).then_inc(core.vector_done.sem, 1)
                dve.wait_ge(core.vector_done.sem, core.vector_done.up())
                even = slot_c[:, 0, 0:SLOTS // 2]
                nc.vector.tensor_scalar(even, slot_f[:, :].rearrange("p (a b) -> p a b", b=2)[:, :, 0],
                                        float(EXP2), None, ALU.is_lt).then_inc(core.vector_done.sem, 1)
                dve.wait_ge(core.vector_done.sem, core.vector_done.up())
                nc.vector.tensor_reduce(slot_c[:, 1, 0:1], even, AX.X, ALU.add).then_inc(core.vector_done.sem, 1)
                dve.wait_ge(core.vector_done.sem, core.vector_done.up())
                nc.vector.tensor_copy(slot_i[:, SLOTS:SLOTS + 1], slot_c[:, 1, 0:1])
                nc.vector.tensor_scalar(slot_f[:, :], slot_f[:, :], float(EXP2 - 1), None, ALU.min).then_inc(core.vector_done.sem, 1)
                dve.wait_ge(core.vector_done.sem, core.vector_done.up())
                nc.vector.tensor_copy(slot_i[:, 0:SLOTS], slot_f[:, :]).then_inc(core.vector_done.sem, 1)
                dve.wait_ge(core.vector_done.sem, core.vector_done.up())

            with nc.Block() as block:

                @block.vector
                def _(dve):
                    assign(dve)


        def scatter(gp):
            for t in range(TILES):
                nc.gpsimd.indirect_dma_start(
                    out=sorted_x[:, :], out_offset=bass.IndirectOffsetOnAxis(ap=pos[:, t:t + 1], axis=0),
                    in_=c.xn[:, t, :], in_offset=None).then_inc(scattered, 16)
            gp.wait_ge(scattered, 16 * TILES)

        with nc.Block() as block:

            @block.gpsimd
            def _(gp):
                scatter(gp)


        with ExitStack() as inner:
            sb2 = Scope(nc, inner, "s2_")
            W1 = sb2("W1", [128, 2, CH, FF2])
            W2 = sb2("W2", [128, FT, DIM])
            b1 = sb2("b1", [128, 2, FT])
            b2 = sb2("b2", [SLOT, 2, DIM])
            xg = sb2("xg", [SLOT, 2, DIM])
            xgT = sb2("xgT", [128, CH, SLOT])
            hT = sb2("hT", [128, FT, SLOT])
            y = sb2("y", [SLOT, 2, DIM])
            sems = {n: inner.enter_context(nc.semaphore("slot_" + n)) for n in
                    ["tokens_landed0", "tokens_landed1", "w1_landed0", "w1_landed1", "w2_landed", "turned", "turns_kept", "hidden", "gelu_done",
                     "summed", "y_ready", "y_stored", "y_free"]}
            HB = 4
            with nc.Block() as block:

                @block.sync
                def _(sync):
                    pairs = sync.value_load(slot_i[0:1, SLOTS:SLOTS + 1], min_val=1, max_val=SLOTS // 2)
                    with sync.Fori(0, pairs) as i:
                        for b in range(2):
                            s = i * 2 + b
                            e = sync.value_load(slot_i[0:1, bass.ds(s, 1)], min_val=0, max_val=EXP2 - 1)
                            sync.wait_ge(sems["y_ready"], i * 2 + b + 1)
                            sync.dma_start(xg[:, b, :], sorted_x[bass.ds(s * SLOT, SLOT), :]).then_inc(
                                sems[f"tokens_landed{b}"], 16)
                            sync.dma_start(b1[:, b, :], d["L2_ffn_b1"][bass.ds(e, 1)].rearrange(
                                "a p f -> (a p) f")).then_inc(sems[f"tokens_landed{b}"], 16)
                            sync.dma_start(b2[:, b, :], d["L2_ffn_b2"][bass.ds(e, 1), :].to_broadcast(
                                [SLOT, DIM])).then_inc(sems[f"tokens_landed{b}"], 16)
                            sync.dma_start(W1[:, b, :, :], d["L2_ffn_W1"][bass.ds(e, 1)].rearrange(
                                "a (c p) n -> p (a c) n", p=128)).then_inc(sems[f"w1_landed{b}"], 16)
                            sync.wait_ge(sems["y_ready"], i * 2 + b + 2)
                            sync.dma_start(W2[:, :, :], d["L2_ffn_W2"][bass.ds(e, 1)].rearrange(
                                "a (f p) n -> p (a f) n", p=128)).then_inc(sems["w2_landed"], 16)

                @block.tensor
                def _(pe):
                    pairs = pe.value_load(slot_i[0:1, SLOTS:SLOTS + 1], min_val=1, max_val=SLOTS // 2)
                    with pe.Fori(0, pairs) as i:
                        for b in range(2):
                            pe.wait_ge(sems[f"tokens_landed{b}"], (i + 1) * 48)
                            for k in range(CH):
                                last = nc.tensor.transpose(core.psum[:, 0, chunk(k)], xg[:, b, chunk(k)],
                                                           c.ident[:, :])
                            last.then_inc(sems["turned"], 1)
                            pe.wait_ge(sems["turns_kept"], i * 2 + b + 1)
                            pe.wait_ge(sems[f"w1_landed{b}"], (i + 1) * 16)
                            for f in range(FT):
                                if f >= HB:
                                    pe.wait_ge(sems["gelu_done"], (i * 2 + b) * FT + f - HB + 1)
                                for k in range(CH):
                                    last = nc.tensor.matmul(core.psum[:, 1 + f % HB, 0:SLOT],
                                                            W1[:, b, k, chunk(f)], xgT[:, k, :],
                                                            start=(k == 0), stop=(k == CH - 1))
                                last.then_inc(sems["hidden"], 1)
                            pe.wait_ge(sems["w2_landed"], (i * 2 + b + 1) * 16)
                            pe.wait_ge(sems["y_ready"], i * 2 + b + 1)
                            for f in range(FT):
                                pe.wait_ge(sems["gelu_done"], (i * 2 + b) * FT + f + 1)
                                last = nc.tensor.matmul(core.psum[:, 5 + b, :], hT[:, f, :], W2[:, f, :],
                                                        start=(f == 0), stop=(f == FT - 1))
                            last.then_inc(sems["summed"], 1)

                @block.scalar
                def _(act):
                    pairs = act.value_load(slot_i[0:1, SLOTS:SLOTS + 1], min_val=1, max_val=SLOTS // 2)
                    with act.Fori(0, pairs) as i:
                        for b in range(2):
                            act.wait_ge(sems["turned"], i * 2 + b + 1)
                            nc.scalar.activation(xgT[:, :, :], core.psum[:, 0, :].rearrange(
                                "p (c n) -> p c n", c=CH), ACT.Copy).then_inc(sems["turns_kept"], 1)
                            for f in range(FT):
                                act.wait_ge(sems["hidden"], (i * 2 + b) * FT + f + 1)
                                nc.scalar.activation(hT[:, f, :], core.psum[:, 1 + f % HB, 0:SLOT], ACT.Gelu,
                                                     bias=b1[:, b, f:f + 1]).then_inc(sems["gelu_done"], 1)

                @block.vector
                def _(dve):
                    dve.sem_inc(sems["y_ready"], 2)
                    pairs = dve.value_load(slot_i[0:1, SLOTS:SLOTS + 1], min_val=1, max_val=SLOTS // 2)
                    with dve.Fori(0, pairs) as i:
                        for b in range(2):
                            dve.wait_ge(sems["summed"], i * 2 + b + 1)
                            dve.wait_ge(sems["y_free"], i * 2 + b + 1)
                            nc.vector.tensor_tensor(y[:, b, :], core.psum[:, 5 + b, :], b2[:, b, :],
                                                    ALU.add).then_inc(sems["y_ready"], 1)

                @block.gpsimd
                def _(gp):
                    gp.sem_inc(sems["y_free"], 2)
                    pairs = gp.value_load(slot_i[0:1, SLOTS:SLOTS + 1], min_val=1, max_val=SLOTS // 2)
                    with gp.Fori(0, pairs) as i:
                        for b in range(2):
                            s = i * 2 + b
                            gp.wait_ge(sems["y_ready"], i * 2 + b + 3)
                            gp.dma_start(sorted_y[bass.ds(s * SLOT, SLOT), :], y[:, b, :]).then_inc(
                                sems["y_stored"], 16)
                            gp.wait_ge(sems["y_stored"], (i * 2 + b + 1) * 16)
                            gp.sem_inc(sems["y_free"], 1)

        with ExitStack() as inner:
            yg = Scope(nc, inner, "y2_")("yg", [ROWS, TILES, DIM])

            def gather(gp):
                for t in range(TILES):
                    nc.gpsimd.indirect_dma_start(
                        out=yg[:, t, :], out_offset=None, in_=sorted_y[:, :],
                        in_offset=bass.IndirectOffsetOnAxis(ap=pos[:, t:t + 1], axis=0)).then_inc(gathered, 16)
                gp.wait_ge(gathered, 16 * TILES)

            with nc.Block() as block:

                @block.gpsimd
                def _(gp):
                    gather(gp)

            with nc.Block() as block:

                @block.vector
                def _(dve):
                    nc.vector.tensor_tensor(
                        c.x[:, :, :], c.x[:, :, :], yg[:, :, :], ALU.add).then_inc(core.vector_done.sem, 1)
                    dve.wait_ge(core.vector_done.sem, core.vector_done.up())




def layer3_gnn(core, c, d):
    nc = core.nc
    with ExitStack() as ctx:
        sb = Scope(nc, ctx, "g3_")
        W = sb("W", [128, CH, DIM])
        aggT = sb("aggT", [128, CH, NODES])
        norm_phases(core, c, c.x, c.xn, c.xnT, loads=[(W[:, :, :], w_view(d["L3_gnn_weight"]))])
        banks, where = [], []
        for t in range(TILES):
            for s0 in (0, 4):
                n = min(4, TILES - s0)
                banks.append([turned(ROWS, ROWS, c.AT[:, s, rows_of(t)], c.ident[0:ROWS, 0:ROWS],
                                     at=128 * (s - s0)) for s in range(s0, s0 + n)])
                where.append((t, s0, n))

        def keep_turned(act, j, bank):
            t, s0, n = where[j]
            return nc.scalar.activation(
                c.CT[:, t, s0 * ROWS:(s0 + n) * ROWS].rearrange("p (t n) -> p t n", n=ROWS),
                bank[0:ROWS, :].rearrange("p (t n) -> p t n", n=128)[:, 0:n, 0:ROWS], ACT.Copy)

        filled, freed = core.bank_filled.span(len(banks)), core.scalar_freed.span(len(banks))
        with nc.Block() as block:

            @block.tensor
            def _(pe):
                for j, products in enumerate(banks):
                    if j >= BANKS:
                        pe.wait_ge(core.scalar_freed.sem, freed + j - BANKS + 1)
                    fill(nc, core.bank(j), products).then_inc(core.bank_filled.sem, 1)

            @block.scalar
            def _(act):
                for j in range(len(banks)):
                    act.wait_ge(core.bank_filled.sem, filled + j + 1)
                    keep_turned(act, j, core.bank(j)).then_inc(core.scalar_freed.sem, 1)

        banks = []
        for m in range(CH):
            banks += halves(128, lambda a, b: [(c.xn[:, s, chunk(m)], c.CT[:, s, a:b]) for s in range(TILES)])
        filled, freed = core.bank_filled.span(len(banks)), core.scalar_freed.span(len(banks))
        with nc.Block() as block:

            @block.tensor
            def _(pe):
                for j, products in enumerate(banks):
                    if j >= BANKS:
                        pe.wait_ge(core.scalar_freed.sem, freed + j - BANKS + 1)
                    fill(nc, core.bank(j), products).then_inc(core.bank_filled.sem, 1)

            @block.scalar
            def _(act):
                for j in range(len(banks)):
                    act.wait_ge(core.bank_filled.sem, filled + j + 1)
                    nc.scalar.activation(
                        aggT[:, j // 2, HALVES[j % 2][0]:HALVES[j % 2][1]],
                        core.bank(j)[:, 0:HALVES[j % 2][1] - HALVES[j % 2][0]], ACT.Copy).then_inc(
                        core.scalar_freed.sem, 1)

        banks = row_products(aggT, W)
        filled, freed = core.bank_filled.span(len(banks)), core.vector_freed.span(len(banks))
        with nc.Block() as block:

            @block.tensor
            def _(pe):
                for j, products in enumerate(banks):
                    if j >= BANKS:
                        pe.wait_ge(core.vector_freed.sem, freed + j - BANKS + 1)
                    fill(nc, core.bank(j), products).then_inc(core.bank_filled.sem, 1)

            @block.vector
            def _(dve):
                for j in range(len(banks)):
                    dve.wait_ge(core.bank_filled.sem, filled + j + 1)
                    if j:
                        dve.wait_ge(core.vector_freed.sem, freed + j)
                    nc.vector.tensor_tensor(
                        c.x[:, j, :], c.x[:, j, :], core.bank(j)[0:ROWS, :], ALU.add).then_inc(
                        core.vector_freed.sem, 1)


def layer3_mix(core, c, d):
    nc = core.nc
    EPS = 1e-6
    N = "L3_mix_"
    with ExitStack() as ctx:
        sb = Scope(nc, ctx, "m3_")
        r2 = sb("r2", [ROWS, TILES, DIM])
        xa = sb("xa", [ROWS, TILES, DIM])
        xaT = sb("xaT", [128, CH, NODES])
        with ExitStack() as inner:
            sb2 = Scope(nc, inner, "a3_")
            gain = sb2("gain", [ROWS, DIM])
            shift = sb2("shift", [ROWS, DIM])
            W = {k: sb2("W" + k, [128, CH, DIM]) for k in "qkvo"}
            bT = {k: sb2("bT" + k, [128, CH]) for k in "qk"}
            B = {k: sb2("B" + k, [ROWS, DIM]) for k in "vo"}
            T = {k: sb2("T" + k, [128, CH, NODES]) for k in "qk"}
            R = {k: sb2("R" + k, [ROWS, TILES, DIM]) for k in "qk"}
            V = sb2("V", [ROWS, TILES, DIM])
            part = sb2("part", [128, 2, CH, 2])
            tot = sb2("tot", [128, 2, CH])
            wide = sb2("wide", [128, 2, CH, 2])
            kv = sb2("kv", [128, CH, 128])
            eps_tile = sb2("eps_tile", [128, ROWS])
            flow = sb2("flow", [ROWS, 2, TILES, HEADS])
            keep = sb2("keep", [ROWS, 2, TILES, HEADS])
            norm = sb2("norm", [ROWS, HEADS])

            def clear(gp):
                nc.gpsimd.memset(kv[:, :, :], 0.0)
                nc.gpsimd.memset(wide[:, :, :, :], 0.0)
                nc.gpsimd.memset(eps_tile[:, :], EPS).then_inc(core.pool_done.sem, 1)
                gp.wait_ge(core.pool_done.sem, core.pool_done.up())

            with nc.Block() as block:

                @block.gpsimd
                def _(gp):
                    clear(gp)

                @block.sync
                def _(sync):
                    moves = [(gain[:, :], bcast(d[N + "g1"])), (shift[:, :], bcast(d[N + "be1"]))]
                    for dst, src in moves:
                        sync.dma_start(dst, src).then_inc(core.landed.sem, 16)
                    sync.wait_ge(core.landed.sem, core.landed.up(16 * len(moves)))

            loads = [(W[k][:, :, :], w_view(d[N + "W" + k])) for k in "qkvo"]
            loads += [(bT[k][:, :], d[N + "b" + k]) for k in "qk"]
            loads += [(B[k][:, :], bcast(d[N + "b" + k])) for k in "vo"]
            norm_phases(core, c, c.xn, xa, xaT, loads=loads, gain=gain, shift=shift)
            banks = []
            for k in "qk":
                for m in range(CH):
                    banks += halves(128, lambda a, b: [(W[k][:, q, chunk(m)], xaT[:, q, a:b]) for q in range(CH)])

            def squash(act, j, bank):
                i, m, (a, b) = j // (2 * CH), j // 2 % CH, HALVES[j % 2]
                return nc.scalar.activation(T["qk"[i]][:, m, a:b], bank[:, 0:b - a], ACT.Sigmoid,
                                            bias=bT["qk"[i]][:, m:m + 1], accum_out=part[:, i, m, j % 2:j % 2 + 1])

            filled, freed = core.bank_filled.span(len(banks)), core.scalar_freed.span(len(banks))
            with nc.Block() as block:

                @block.tensor
                def _(pe):
                    for j, products in enumerate(banks):
                        if j >= BANKS:
                            pe.wait_ge(core.scalar_freed.sem, freed + j - BANKS + 1)
                        fill(nc, core.bank(j), products).then_inc(core.bank_filled.sem, 1)

                @block.scalar
                def _(act):
                    for j in range(len(banks)):
                        act.wait_ge(core.bank_filled.sem, filled + j + 1)
                        squash(act, j, core.bank(j)).then_inc(core.scalar_freed.sem, 1)

            banks = row_products(xaT, W["v"])
            filled, freed = core.bank_filled.span(len(banks)), core.vector_freed.span(len(banks))
            with nc.Block() as block:

                @block.tensor
                def _(pe):
                    for j, products in enumerate(banks):
                        if j >= BANKS:
                            pe.wait_ge(core.vector_freed.sem, freed + j - BANKS + 1)
                        fill(nc, core.bank(j), products).then_inc(core.bank_filled.sem, 1)

                @block.vector
                def _(dve):
                    for j in range(len(banks)):
                        dve.wait_ge(core.bank_filled.sem, filled + j + 1)
                        if j:
                            dve.wait_ge(core.vector_freed.sem, freed + j)
                        nc.vector.tensor_tensor(
                            V[:, j, :], core.bank(j)[0:ROWS, :], B["v"][:, :], ALU.add).then_inc(
                            core.vector_freed.sem, 1)

            banks = [[turned(ROWS, 128, T[k][:, m, rows_of(t)], c.ident[:, :], at=128 * m) for m in range(CH)]
                     for k in "qk" for t in range(TILES)]
            filled, freed = core.bank_filled.span(len(banks)), core.scalar_freed.span(len(banks))
            with nc.Block() as block:

                @block.tensor
                def _(pe):
                    for j, products in enumerate(banks):
                        if j >= BANKS:
                            pe.wait_ge(core.scalar_freed.sem, freed + j - BANKS + 1)
                        fill(nc, core.bank(j), products).then_inc(core.bank_filled.sem, 1)

                @block.scalar
                def _(act):
                    for j in range(len(banks)):
                        act.wait_ge(core.bank_filled.sem, filled + j + 1)
                        nc.scalar.activation(
                            R["qk"[j // TILES]][:, j % TILES, :], core.bank(j)[0:ROWS, :], ACT.Copy).then_inc(
                            core.scalar_freed.sem, 1)


            def widen(dve, of):
                for i in range(2):
                    for half in range(2):
                        h = slice(HDIM * half, HDIM * (half + 1))
                        last = nc.vector.tensor_scalar(wide[h, i, :, half], of[h, 1 - i, :], EPS, None, ALU.add)
                last.then_inc(core.vector_done.sem, 1)
                dve.wait_ge(core.vector_done.sem, core.vector_done.up())

            def first(dve):
                nc.vector.tensor_tensor(tot[:, :, :], part[:, :, :, 0], part[:, :, :, 1], ALU.add).then_inc(core.vector_done.sem, 1)
                dve.wait_ge(core.vector_done.sem, core.vector_done.up())
                widen(dve, tot)

            with nc.Block() as block:

                @block.vector
                def _(dve):
                    first(dve)


            def dot_banks():
                return [[product(ROWS, [(eps_tile[:, :], wide[:, i, p, :]),
                                        (T["qk"[i]][:, p, rows_of(t)], wide[:, i, p, :])], 2, at=8 * i + 2 * p)
                         for i in range(2) for p in range(PAIRS)] for t in range(TILES)]

            def inverse(dve, t, bank):
                return nc.vector.reciprocal(flow[:, :, t, :], bank[0:ROWS, 0:16].rearrange("p (i h) -> p i h", i=2))

            banks = dot_banks()
            filled, freed = core.bank_filled.span(len(banks)), core.vector_freed.span(len(banks))
            with nc.Block() as block:

                @block.tensor
                def _(pe):
                    for j, products in enumerate(banks):
                        if j >= BANKS:
                            pe.wait_ge(core.vector_freed.sem, freed + j - BANKS + 1)
                        fill(nc, core.bank(j), products).then_inc(core.bank_filled.sem, 1)

                @block.vector
                def _(dve):
                    for j in range(len(banks)):
                        dve.wait_ge(core.bank_filled.sem, filled + j + 1)
                        if j:
                            dve.wait_ge(core.vector_freed.sem, freed + j)
                        inverse(dve, j, core.bank(j)).then_inc(core.vector_freed.sem, 1)

            banks = [[product(128, [(R["qk"[i]][:, t, chunk(p)], flow[:, i, t, :]) for t in range(TILES)], HEADS,
                              at=8 * p) for p in range(PAIRS)] for i in range(2)]

            def pick(dve, i, bank):
                v = bank[:, 0:32].rearrange("p (a h) -> p a h", a=PAIRS)
                for p in range(PAIRS):
                    for half in range(2):
                        h = slice(HDIM * half, HDIM * (half + 1))
                        last = nc.vector.tensor_copy(tot[h, i, p:p + 1], v[h, p, 2 * p + half:2 * p + half + 1])
                return last

            filled, freed = core.bank_filled.span(len(banks)), core.vector_freed.span(len(banks))
            with nc.Block() as block:

                @block.tensor
                def _(pe):
                    for j, products in enumerate(banks):
                        if j >= BANKS:
                            pe.wait_ge(core.vector_freed.sem, freed + j - BANKS + 1)
                        fill(nc, core.bank(j), products).then_inc(core.bank_filled.sem, 1)

                @block.vector
                def _(dve):
                    for j in range(len(banks)):
                        dve.wait_ge(core.bank_filled.sem, filled + j + 1)
                        if j:
                            dve.wait_ge(core.vector_freed.sem, freed + j)
                        pick(dve, j, core.bank(j)).then_inc(core.vector_freed.sem, 1)

            with nc.Block() as block:

                @block.vector
                def _(dve):
                    widen(dve, tot)

            banks = dot_banks()
            filled, freed = core.bank_filled.span(len(banks)), core.vector_freed.span(len(banks))
            with nc.Block() as block:

                @block.tensor
                def _(pe):
                    for j, products in enumerate(banks):
                        if j >= BANKS:
                            pe.wait_ge(core.vector_freed.sem, freed + j - BANKS + 1)
                        fill(nc, core.bank(j), products).then_inc(core.bank_filled.sem, 1)

                @block.vector
                def _(dve):
                    for j in range(len(banks)):
                        dve.wait_ge(core.bank_filled.sem, filled + j + 1)
                        if j:
                            dve.wait_ge(core.vector_freed.sem, freed + j)
                        nc.vector.tensor_copy(
                            keep[:, :, j, :], core.bank(j)[0:ROWS, 0:16].rearrange("p (i h) -> p i h", i=2)).then_inc(
                            core.vector_freed.sem, 1)

            with nc.Block() as block:

                @block.vector
                def _(dve):
                    nc.vector.tensor_scalar(
                        keep[:, 1, :, :], keep[:, 1, :, :], 1.0, -1.0, ALU.min, ALU.max).then_inc(core.vector_done.sem, 1)
                    dve.wait_ge(core.vector_done.sem, core.vector_done.up())


            def acts(act):
                nc.scalar.activation(keep[:, 0, :, :], keep[:, 0, :, :], ACT.Sigmoid)
                nc.scalar.activation(keep[:, 1, :, :], keep[:, 1, :, :], ACT.Exp).then_inc(core.scalar_done.sem, 1)
                act.wait_ge(core.scalar_done.sem, core.scalar_done.up())

            with nc.Block() as block:

                @block.scalar
                def _(act):
                    acts(act)

            banks = [[product(ROWS, [(c.ones[0:ROWS, 0:ROWS], keep[:, 1, t, :]) for t in range(TILES)], HEADS)]]
            filled, freed = core.bank_filled.span(len(banks)), core.vector_freed.span(len(banks))
            with nc.Block() as block:

                @block.tensor
                def _(pe):
                    for j, products in enumerate(banks):
                        if j >= BANKS:
                            pe.wait_ge(core.vector_freed.sem, freed + j - BANKS + 1)
                        fill(nc, core.bank(j), products).then_inc(core.bank_filled.sem, 1)

                @block.vector
                def _(dve):
                    for j in range(len(banks)):
                        dve.wait_ge(core.bank_filled.sem, filled + j + 1)
                        if j:
                            dve.wait_ge(core.vector_freed.sem, freed + j)
                        nc.vector.reciprocal(norm[:, :], core.bank(j)[0:ROWS, 0:HEADS]).then_inc(
                            core.vector_freed.sem, 1)


            def weigh(dve):
                nc.vector.tensor_scalar(norm[:, :], norm[:, :], float(NODES), None, ALU.mult).then_inc(core.vector_done.sem, 1)
                dve.wait_ge(core.vector_done.sem, core.vector_done.up())
                for t in range(TILES):
                    last = nc.vector.tensor_tensor(keep[:, 1, t, :], keep[:, 1, t, :], norm[:, :], ALU.mult)
                last.then_inc(core.vector_done.sem, 1)
                dve.wait_ge(core.vector_done.sem, core.vector_done.up())
                nc.vector.tensor_tensor(flow[:, 0, :, :], flow[:, 0, :, :], keep[:, 0, :, :], ALU.mult).then_inc(core.vector_done.sem, 1)
                dve.wait_ge(core.vector_done.sem, core.vector_done.up())
                for t in range(TILES):
                    last = nc.vector.tensor_tensor(
                        V[:, t, :].rearrange("p (h e) -> p h e", h=HEADS), V[:, t, :].rearrange("p (h e) -> p h e", h=HEADS),
                        keep[:, 1, t, :].unsqueeze(2).to_broadcast([ROWS, HEADS, HDIM]), ALU.mult)
                last.then_inc(core.vector_done.sem, 1)
                dve.wait_ge(core.vector_done.sem, core.vector_done.up())

            with nc.Block() as block:

                @block.vector
                def _(dve):
                    weigh(dve)

            banks = [[product(128, [(R["k"][:, t, chunk(p)], V[:, t, chunk(p)]) for t in range(TILES)], 128)]
                     for p in range(PAIRS)]

            def blocks(dve, p, bank):
                for half in range(2):
                    h = slice(HDIM * half, HDIM * (half + 1))
                    last = nc.vector.tensor_copy(kv[h, p, h], bank[h, h])
                return last

            filled, freed = core.bank_filled.span(len(banks)), core.vector_freed.span(len(banks))
            with nc.Block() as block:

                @block.tensor
                def _(pe):
                    for j, products in enumerate(banks):
                        if j >= BANKS:
                            pe.wait_ge(core.vector_freed.sem, freed + j - BANKS + 1)
                        fill(nc, core.bank(j), products).then_inc(core.bank_filled.sem, 1)

                @block.vector
                def _(dve):
                    for j in range(len(banks)):
                        dve.wait_ge(core.bank_filled.sem, filled + j + 1)
                        if j:
                            dve.wait_ge(core.vector_freed.sem, freed + j)
                        blocks(dve, j, core.bank(j)).then_inc(core.vector_freed.sem, 1)

            banks = [[product(ROWS, [(T["q"][:, p, rows_of(t)], kv[:, p, :])], 128, at=128 * p)
                      for p in range(PAIRS)] for t in range(TILES)]
            filled, freed = core.bank_filled.span(len(banks)), core.vector_freed.span(len(banks))
            with nc.Block() as block:

                @block.tensor
                def _(pe):
                    for j, products in enumerate(banks):
                        if j >= BANKS:
                            pe.wait_ge(core.vector_freed.sem, freed + j - BANKS + 1)
                        fill(nc, core.bank(j), products).then_inc(core.bank_filled.sem, 1)

                @block.vector
                def _(dve):
                    for j in range(len(banks)):
                        dve.wait_ge(core.bank_filled.sem, filled + j + 1)
                        if j:
                            dve.wait_ge(core.vector_freed.sem, freed + j)
                        nc.vector.tensor_tensor(
                            R["q"][:, j, :].rearrange("p (h e) -> p h e", h=HEADS), core.bank(j)[0:ROWS, :].rearrange("p (h e) -> p h e", h=HEADS),
                            flow[:, 0, j, :].unsqueeze(2).to_broadcast([ROWS, HEADS, HDIM]), ALU.mult).then_inc(
                            core.vector_freed.sem, 1)

            turn_phase(core, c, R["q"], xaT, CH)

            def residual(dve, t, bank):
                nc.vector.tensor_tensor(r2[:, t, :], bank[0:ROWS, :], B["o"][:, :], ALU.add).then_inc(core.vector_done.sem, 1)
                dve.wait_ge(core.vector_done.sem, core.vector_done.up())
                return nc.vector.tensor_tensor(r2[:, t, :], r2[:, t, :], c.xn[:, t, :], ALU.add)

            banks = row_products(xaT, W["o"])
            filled, freed = core.bank_filled.span(len(banks)), core.vector_freed.span(len(banks))
            with nc.Block() as block:

                @block.tensor
                def _(pe):
                    for j, products in enumerate(banks):
                        if j >= BANKS:
                            pe.wait_ge(core.vector_freed.sem, freed + j - BANKS + 1)
                        fill(nc, core.bank(j), products).then_inc(core.bank_filled.sem, 1)

                @block.vector
                def _(dve):
                    for j in range(len(banks)):
                        dve.wait_ge(core.bank_filled.sem, filled + j + 1)
                        if j:
                            dve.wait_ge(core.vector_freed.sem, freed + j)
                        residual(dve, j, core.bank(j)).then_inc(core.vector_freed.sem, 1)

        with ExitStack() as inner:
            sb2 = Scope(nc, inner, "b3_")
            gain = sb2("gain", [ROWS, DIM])
            shift = sb2("shift", [ROWS, DIM])
            W1 = sb2("W1", [128, CH, FF3])
            W2 = sb2("W2", [FF3, DIM])
            b1 = sb2("b1", [FF3, 1])
            b2 = sb2("b2", [ROWS, DIM])
            hT = sb2("hT", [FF3, NODES])
            u = sb2("u", [ROWS, DIM])
            loads = [(gain[:, :], bcast(d[N + "g2"])), (shift[:, :], bcast(d[N + "be2"])),
                     (W1[:, :, :], w_view(d[N + "W1"])), (W2[:, :], d[N + "W2"]),
                     (b1[:, :], d[N + "b1"]), (b2[:, :], bcast(d[N + "b2"]))]
            with nc.Block() as block:

                @block.sync
                def _(sync):
                    for dst, src in loads:
                        sync.dma_start(dst, src).then_inc(core.landed.sem, 16)
                    sync.wait_ge(core.landed.sem, core.landed.up(16 * len(loads)))

            norm_phases(core, c, r2, xa, xaT, gain=gain, shift=shift)
            banks = halves(128, lambda a, b: [(W1[:, k, :], xaT[:, k, a:b]) for k in range(CH)])
            filled, freed = core.bank_filled.span(len(banks)), core.scalar_freed.span(len(banks))
            with nc.Block() as block:

                @block.tensor
                def _(pe):
                    for j, products in enumerate(banks):
                        if j >= BANKS:
                            pe.wait_ge(core.scalar_freed.sem, freed + j - BANKS + 1)
                        fill(nc, core.bank(j), products).then_inc(core.bank_filled.sem, 1)

                @block.scalar
                def _(act):
                    for j in range(len(banks)):
                        act.wait_ge(core.bank_filled.sem, filled + j + 1)
                        nc.scalar.activation(
                            hT[:, HALVES[j][0]:HALVES[j][1]], core.bank(j)[:, 0:HALVES[j][1] - HALVES[j][0]], ACT.Gelu, bias=b1[:, 0:1]).then_inc(
                            core.scalar_freed.sem, 1)

            banks = [[product(ROWS, [(hT[:, rows_of(t)], W2[:, :])], DIM)] for t in range(TILES)]
            add_to_x = add_biased(core, c, u, b2, r2)
            filled, freed = core.bank_filled.span(len(banks)), core.vector_freed.span(len(banks))
            with nc.Block() as block:

                @block.tensor
                def _(pe):
                    for j, products in enumerate(banks):
                        if j >= BANKS:
                            pe.wait_ge(core.vector_freed.sem, freed + j - BANKS + 1)
                        fill(nc, core.bank(j), products).then_inc(core.bank_filled.sem, 1)

                @block.vector
                def _(dve):
                    for j in range(len(banks)):
                        dve.wait_ge(core.bank_filled.sem, filled + j + 1)
                        if j:
                            dve.wait_ge(core.vector_freed.sem, freed + j)
                        add_to_x(dve, j, core.bank(j)).then_inc(core.vector_freed.sem, 1)


def layer3_ffn(core, c, d):
    nc = core.nc
    EPS = 1e-5
    with ExitStack() as ctx:
        sb = Scope(nc, ctx, "f3_")
        up = sb("up", [128, CH, FF3])
        down = sb("down", [FF3, DIM])
        size = sb("size", [128, 2])
        scale = sb("scale", [128, 2])
        t1 = sb("t1", [128, DIM])
        t2 = sb("t2", [128, DIM])
        upq = sb("upq", [128, CH, FF3])
        downq = sb("downq", [FF3, DIM])
        xq = sb("xq", [ROWS, TILES, DIM])
        xqT = sb("xqT", [128, CH, NODES])
        h = sb("h", [ROWS, TILES, FF3])
        hT = sb("hT", [FF3, NODES])
        big = sb("big", [ROWS, TILES])
        inv = sb("inv", [ROWS, TILES])
        out_scale = sb("out_scale", [ROWS, TILES])
        norm_phases(core, c, c.x, c.xn, c.xnT, loads=[(up[:, :, :], w_view(d["L3_ffn_w_up"])),
                                                     (down[:, :], d["L3_ffn_w_down"])])

        def sizes(dve):
            nc.vector.tensor_reduce(size[:, 0:1], up[:, :, :].rearrange("p c n -> p (c n)"), AX.X, ALU.add,
                                    apply_absolute_value=True)
            nc.vector.tensor_reduce(size[:, 1:2], down[:, :], AX.X, ALU.add, apply_absolute_value=True).then_inc(core.vector_done.sem, 1)
            dve.wait_ge(core.vector_done.sem, core.vector_done.up())

        with nc.Block() as block:

            @block.vector
            def _(dve):
                sizes(dve)

        banks = [[product(128, [(c.ones[:, :], size[:, :])], 2)]]
        filled, freed = core.bank_filled.span(len(banks)), core.vector_freed.span(len(banks))
        with nc.Block() as block:

            @block.tensor
            def _(pe):
                for j, products in enumerate(banks):
                    if j >= BANKS:
                        pe.wait_ge(core.vector_freed.sem, freed + j - BANKS + 1)
                    fill(nc, core.bank(j), products).then_inc(core.bank_filled.sem, 1)

            @block.vector
            def _(dve):
                for j in range(len(banks)):
                    dve.wait_ge(core.bank_filled.sem, filled + j + 1)
                    if j:
                        dve.wait_ge(core.vector_freed.sem, freed + j)
                    nc.vector.tensor_scalar(scale[:, :], core.bank(j)[:, 0:2], 1.0 / (DIM * FF3), EPS, ALU.mult, ALU.max).then_inc(
                        core.vector_freed.sem, 1)


        def round_weights(dve):
            for i, (w, q) in enumerate(((up[:, :, :].rearrange("p c n -> p (c n)"),
                                         upq[:, :, :].rearrange("p c n -> p (c n)")), (down[:, :], downq[:, :]))):
                nc.vector.tensor_scalar(t1[:, :], w, 2.0, scale[:, i:i + 1], ALU.mult, ALU.is_gt).then_inc(core.vector_done.sem, 1)
                dve.wait_ge(core.vector_done.sem, core.vector_done.up())
                nc.vector.tensor_scalar(t2[:, :], w, -2.0, scale[:, i:i + 1], ALU.mult, ALU.is_gt).then_inc(core.vector_done.sem, 1)
                dve.wait_ge(core.vector_done.sem, core.vector_done.up())
                nc.vector.tensor_tensor(q, t1[:, :], t2[:, :], ALU.subtract).then_inc(core.vector_done.sem, 1)
                dve.wait_ge(core.vector_done.sem, core.vector_done.up())

        with nc.Block() as block:

            @block.vector
            def _(dve):
                round_weights(dve)


        def quantise(dve, src, dst, width, i):
            nc.vector.tensor_reduce(big[:, :], src, AX.X, ALU.max, apply_absolute_value=True).then_inc(core.vector_done.sem, 1)
            dve.wait_ge(core.vector_done.sem, core.vector_done.up())
            nc.vector.tensor_scalar(big[:, :], big[:, :], EPS, None, ALU.max).then_inc(core.vector_done.sem, 1)
            dve.wait_ge(core.vector_done.sem, core.vector_done.up())
            nc.vector.reciprocal(inv[:, :], big[:, :]).then_inc(core.vector_done.sem, 1)
            dve.wait_ge(core.vector_done.sem, core.vector_done.up())
            nc.vector.tensor_scalar(inv[:, :], inv[:, :], 127.0, None, ALU.mult).then_inc(core.vector_done.sem, 1)
            dve.wait_ge(core.vector_done.sem, core.vector_done.up())
            nc.vector.reciprocal(out_scale[:, :], inv[:, :]).then_inc(core.vector_done.sem, 1)
            dve.wait_ge(core.vector_done.sem, core.vector_done.up())
            nc.vector.tensor_scalar(out_scale[:, :], out_scale[:, :], scale[0:ROWS, i:i + 1], None, ALU.mult).then_inc(core.vector_done.sem, 1)
            dve.wait_ge(core.vector_done.sem, core.vector_done.up())
            for t in range(TILES):
                last = nc.vector.tensor_scalar(dst[:, t, :], src[:, t, :], inv[:, t:t + 1], ROUND, ALU.mult, ALU.add)
            last.then_inc(core.vector_done.sem, 1)
            dve.wait_ge(core.vector_done.sem, core.vector_done.up())
            for t in range(TILES):
                last = nc.vector.tensor_scalar(dst[:, t, :], dst[:, t, :], ROUND, 127.0, ALU.subtract, ALU.min)
            last.then_inc(core.vector_done.sem, 1)
            dve.wait_ge(core.vector_done.sem, core.vector_done.up())
            nc.vector.tensor_scalar(dst, dst, -128.0, None, ALU.max).then_inc(core.vector_done.sem, 1)
            dve.wait_ge(core.vector_done.sem, core.vector_done.up())

        with nc.Block() as block:

            @block.vector
            def _(dve):
                quantise(dve, c.xn[:, :, :], xq[:, :, :], DIM, 0)

        turn_phase(core, c, xq, xqT, CH)
        banks = row_products(xqT, upq, cols=FF3)

        def hidden(dve, t, bank):
            nc.vector.tensor_scalar(h[:, t, :], bank[0:ROWS, 0:FF3], out_scale[:, t:t + 1], 0.0, ALU.mult, ALU.max).then_inc(core.vector_done.sem, 1)
            dve.wait_ge(core.vector_done.sem, core.vector_done.up())
            nc.vector.tensor_scalar(h[:, t, :], h[:, t, :], 127.0, ROUND, ALU.min, ALU.add).then_inc(core.vector_done.sem, 1)
            dve.wait_ge(core.vector_done.sem, core.vector_done.up())
            return nc.vector.tensor_scalar(h[:, t, :], h[:, t, :], ROUND, None, ALU.subtract)

        filled, freed = core.bank_filled.span(len(banks)), core.vector_freed.span(len(banks))
        with nc.Block() as block:

            @block.tensor
            def _(pe):
                for j, products in enumerate(banks):
                    if j >= BANKS:
                        pe.wait_ge(core.vector_freed.sem, freed + j - BANKS + 1)
                    fill(nc, core.bank(j), products).then_inc(core.bank_filled.sem, 1)

            @block.vector
            def _(dve):
                for j in range(len(banks)):
                    dve.wait_ge(core.bank_filled.sem, filled + j + 1)
                    if j:
                        dve.wait_ge(core.vector_freed.sem, freed + j)
                    hidden(dve, j, core.bank(j)).then_inc(core.vector_freed.sem, 1)

        with nc.Block() as block:

            @block.vector
            def _(dve):
                quantise(dve, h[:, :, :], h[:, :, :], FF3, 1)

        banks = [[turned(FF3, ROWS, h[:, t, :], c.ident[0:ROWS, 0:ROWS])] for t in range(TILES)]
        filled, freed = core.bank_filled.span(len(banks)), core.scalar_freed.span(len(banks))
        with nc.Block() as block:

            @block.tensor
            def _(pe):
                for j, products in enumerate(banks):
                    if j >= BANKS:
                        pe.wait_ge(core.scalar_freed.sem, freed + j - BANKS + 1)
                    fill(nc, core.bank(j), products).then_inc(core.bank_filled.sem, 1)

            @block.scalar
            def _(act):
                for j in range(len(banks)):
                    act.wait_ge(core.bank_filled.sem, filled + j + 1)
                    nc.scalar.activation(hT[:, rows_of(j)], core.bank(j)[:, 0:ROWS], ACT.Copy).then_inc(
                        core.scalar_freed.sem, 1)

        banks = [[product(ROWS, [(hT[:, rows_of(t)], downq[:, :])], DIM)] for t in range(TILES)]
        filled, freed = core.bank_filled.span(len(banks)), core.vector_freed.span(len(banks))
        with nc.Block() as block:

            @block.tensor
            def _(pe):
                for j, products in enumerate(banks):
                    if j >= BANKS:
                        pe.wait_ge(core.vector_freed.sem, freed + j - BANKS + 1)
                    fill(nc, core.bank(j), products).then_inc(core.bank_filled.sem, 1)

            @block.vector
            def _(dve):
                for j in range(len(banks)):
                    dve.wait_ge(core.bank_filled.sem, filled + j + 1)
                    if j:
                        dve.wait_ge(core.vector_freed.sem, freed + j)
                    nc.vector.scalar_tensor_tensor(
                        out=c.x[:, j, :], in0=core.bank(j)[0:ROWS, :], scalar=out_scale[:, j:j + 1], in1=c.x[:, j, :],
                        op0=ALU.mult, op1=ALU.add).then_inc(
                        core.vector_freed.sem, 1)


class Shared:
    pass


STAGES = 8


def build(nc, d, out, stages=STAGES, first=1):
    with ExitStack() as ctx:
        core = Core(nc, ctx)
        c = Shared()
        sb = Scope(nc, ctx, "")
        c.x = sb("x_rows", [ROWS, TILES, DIM])
        c.xn = sb("xn_rows", [ROWS, TILES, DIM])
        c.xnT = sb("xn_turned", [128, CH, NODES])
        c.AT = sb("weights_from_to", [ROWS, TILES, NODES])
        c.CT = sb("edges_from_to", [ROWS, TILES, NODES])
        c.ident = sb("ident", [128, 128])
        c.ones = sb("ones", [128, 128])
        c.below = sb("below", [128, 128])
        c.above = sb("above", [128, 128])
        c.sorted_x = nc.dram_tensor("sorted_x", [SLOTS * SLOT, DIM], F32, kind="Internal").ap()
        c.sorted_y = nc.dram_tensor("sorted_y", [SLOTS * SLOT, DIM], F32, kind="Internal").ap()

        def constants(gp):
            nc.gpsimd.memset(c.ones[:, :], 1.0)
            nc.gpsimd.memset(c.ident[:, :], 0.0)
            nc.gpsimd.memset(c.below[:, :], 0.0)
            nc.gpsimd.memset(c.above[:, :], 0.0).then_inc(core.pool_done.sem, 1)
            gp.wait_ge(core.pool_done.sem, core.pool_done.up())
            nc.gpsimd.affine_select(out=c.ident[:, :], in_=c.ident[:, :], compare_op=ALU.not_equal, fill=1.0,
                                    base=0, pattern=[[-1, 128]], channel_multiplier=1)
            nc.gpsimd.affine_select(out=c.below[:, :], in_=c.below[:, :], compare_op=ALU.is_ge, fill=1.0,
                                    base=0, pattern=[[1, 128]], channel_multiplier=-1)
            nc.gpsimd.affine_select(out=c.above[:, :], in_=c.above[:, :], compare_op=ALU.is_ge, fill=1.0,
                                           base=0, pattern=[[-1, 128]], channel_multiplier=1).then_inc(core.pool_done.sem, 1)
            gp.wait_ge(core.pool_done.sem, core.pool_done.up())

        with nc.Block() as block:

            @block.gpsimd
            def _(gp):
                constants(gp)

            @block.sync
            def _(sync):
                moves = [(c.x[:, :, :], d["x"].rearrange("(t p) n -> p t n", p=ROWS))]
                for dst, src in moves:
                    sync.dma_start(dst, src).then_inc(core.landed.sem, 16)
                sync.wait_ge(core.landed.sem, core.landed.up(16 * len(moves)))

        adjacency_phases(core, c, d, ctx)
        if stages >= 1 >= first:
            layer0_gnn(core, c, d)
            layer0_mix(core, c, d)
        if stages >= 2 >= first:
            layer0_ffn(core, c, d)
        if stages >= 3 >= first:
            layer1_gnn(core, c, d)
            layer1_mix(core, c, d)
        if stages >= 4 >= first:
            layer1_ffn(core, c, d)
        if stages >= 5 >= first:
            layer2_gnn(core, c, d)
            layer2_mix(core, c, d)
        if stages >= 6 >= first:
            layer2_ffn(core, c, d, ctx)
        if stages >= 7 >= first:
            layer3_gnn(core, c, d)
            layer3_mix(core, c, d)
        if stages >= 8 >= first:
            layer3_ffn(core, c, d)
        with nc.Block() as block:

            @block.sync
            def _(sync):
                moves = [(out.rearrange("(t p) n -> p t n", p=ROWS), c.x[:, :, :])]
                for dst, src in moves:
                    sync.dma_start(dst, src).then_inc(core.landed.sem, 16)
                sync.wait_ge(core.landed.sem, core.landed.up(16 * len(moves)))


TURNED = ["L0_ffn_w_gate", "L0_ffn_w_up", "L0_ffn_w_down", "L1_mix_Wq", "L1_mix_Wkv", "L2_ffn_Wr",
          "L3_gnn_weight", "L3_ffn_w_up", "L3_ffn_w_down"]
PER_PARTITION = ["L0_gnn_b1", "L3_mix_bq", "L3_mix_bk", "L3_mix_b1"]
NAMES = """x src dst edge_weight node_vec L0_gnn_W0_1 L0_gnn_W1_1 L0_gnn_b1 L0_gnn_W0_2 L0_gnn_W1_2 L0_gnn_b2
L0_mix_Wq L0_mix_bq L0_mix_Wk L0_mix_bk L0_mix_Wv L0_mix_bv L0_mix_Wo L0_mix_bo L0_mix_temperature
L0_ffn_w_gate L0_ffn_w_up L0_ffn_w_down L1_gnn_W L1_gnn_b L1_mix_Wq L1_mix_Wkv L1_ffn_Wg L1_ffn_W1 L1_ffn_b1
L1_ffn_W2 L1_ffn_b2 L2_gnn_W1 L2_gnn_att_src1 L2_gnn_att_dst1 L2_gnn_b1 L2_gnn_W2 L2_gnn_att_src2
L2_gnn_att_dst2 L2_gnn_b2 L2_gnn_fcW L2_gnn_fcb L2_mix_Wq L2_mix_Wk L2_mix_Wv L2_mix_Wo L2_mix_omega_q
L2_mix_omega_k L2_ffn_Wr L2_ffn_br L2_ffn_W1 L2_ffn_b1 L2_ffn_W2 L2_ffn_b2 L3_gnn_weight L3_mix_Wq L3_mix_bq
L3_mix_Wk L3_mix_bk L3_mix_Wv L3_mix_bv L3_mix_Wo L3_mix_bo L3_mix_W1 L3_mix_b1 L3_mix_W2 L3_mix_b2 L3_mix_g1
L3_mix_be1 L3_mix_g2 L3_mix_be2 L3_ffn_w_up L3_ffn_w_down""".split()


def lay_out(inputs):
    arrays = {}
    for name in NAMES:
        a = np.asarray(inputs[name])
        if name in TURNED:
            a = a.T
        if "_att_" in name:
            a = a.reshape(-1)
        if name in PER_PARTITION:
            a = a.reshape(-1, 128).T
        if name == "L1_ffn_b1":
            a = a.reshape(EXP1, FF1 // 128, 128).transpose(2, 0, 1)
        if name == "L2_ffn_b1":
            a = a.reshape(EXP2, FF2 // 128, 128).transpose(0, 2, 1)
        arrays["in_" + name] = np.ascontiguousarray(a)
    return arrays


def kernel(**inputs):
    import concourse.bacc as _bacc
    from concourse.bass_utils import run_bass_kernel_spmd as _run

    nc = _bacc.Bacc("TRN2", target_bir_lowering=False, num_devices=1)
    arrays = lay_out(inputs)
    d = {}
    for name in NAMES:
        a = arrays["in_" + name]
        d[name] = nc.dram_tensor("in_" + name, a.shape, mybir.dt.from_np(a.dtype), kind="ExternalInput").ap()
    out = nc.dram_tensor("out_x", (NODES, DIM), F32, kind="ExternalOutput").ap()
    build(nc, d, out)
    r = _run(nc, [arrays], core_ids=[0])
    return r.results[0]["out_x"]
```
